# Optimizing a Trainium2 kernel written in Bass

```python
import numpy as np
import jax
import jax.numpy as jnp

def _softmax(x, axis=-1):
    return jax.nn.softmax(x, axis=axis)

def _gelu(x):
    return jax.nn.gelu(x, approximate=True)

def _silu(x):
    return jax.nn.silu(x)

def _sigmoid(x):
    return jax.nn.sigmoid(x)

def _layernorm(x, axis=-1, eps=1e-05):
    m = jnp.mean(x, axis=axis, keepdims=True)
    v = jnp.var(x, axis=axis, keepdims=True)
    return (x - m) / jnp.sqrt(v + eps)

def _scatter_add(tgt, idx, src, axis=0):
    return tgt.at[idx].add(src)

def _segment_sum(src, seg, n):
    return jax.ops.segment_sum(src, seg, n)
kernel_name = 'mk_gnn_ffn_d2_gnn_r32_17fb08'

def setup_inputs(seed: int=0):
    np.random.seed(seed)
    _w = jnp.asarray

    def _rec_inputs():
        import jax
        import jax.numpy as jnp
        _gk = jax.random.key(seed)
        x = -0.0003713 + 1 * jax.random.normal(jax.random.fold_in(_gk, 1), (3125, 256), jnp.float32)
        src = jax.random.randint(jax.random.fold_in(_gk, 2), (50000,), 0, 3125, jnp.int32)
        dst = jnp.minimum((3125 * jax.random.uniform(jax.random.fold_in(_gk, 3), (50000,)) ** 2.0).astype(jnp.int32), 99999)
        _o = jnp.argsort(dst, stable=True)
        src = src[_o]
        dst = dst[_o]
        edge_type_64 = jax.random.randint(jax.random.fold_in(_gk, 12), (50000,), 0, 64, jnp.int32)
        return (x, src, dst, edge_type_64)
    x, src, dst, edge_type_64 = _rec_inputs()

    def _L0_gnn_setup():
        import jax, jax.numpy as jnp
        import numpy as np
        N_NODES = 50000
        N_EDGES = 25000
        IN_FEAT = 256
        HEADS = 8
        OUT_FEAT = 32
        key = jax.random.key(seed)
        k = jax.random.split(key, 6)
        x = jax.random.normal(k[0], (N_NODES, IN_FEAT), dtype=jnp.float32)
        edge_index = jax.random.randint(k[1], (2, N_EDGES), 0, N_NODES, dtype=jnp.int64)
        gain = np.sqrt(2.0)
        std_w = gain * np.sqrt(2.0 / (IN_FEAT + HEADS * OUT_FEAT))
        W = jax.random.normal(k[2], (HEADS * OUT_FEAT, IN_FEAT), dtype=jnp.float32) * std_w
        std_a = gain * np.sqrt(2.0 / (HEADS + OUT_FEAT))
        a_src = jax.random.normal(k[3], (HEADS, OUT_FEAT), dtype=jnp.float32) * std_a
        a_dst = jax.random.normal(k[4], (HEADS, OUT_FEAT), dtype=jnp.float32) * std_a
        bias = jax.random.normal(k[5], (HEADS * OUT_FEAT,), dtype=jnp.float32) * 0.02
        return {'x': x, 'edge_index': edge_index, 'W': W, 'a_src': a_src, 'a_dst': a_dst, 'bias': bias}
    _L0_gnn_all = _L0_gnn_setup()
    _L0_gnn_in = {k: v for k, v in _L0_gnn_all.items() if k in ('W', 'a_src', 'a_dst', 'bias')}
    del _L0_gnn_all

    def _L0_ffn_setup():
        import math
        import jax, jax.numpy as jnp
        import numpy as np
        CAPACITY_FACTOR = 1.25
        TOP_K = 2
        LN_EPS = 1e-05

        def _layer_norm(x, gamma, beta):
            mu = jnp.mean(x, axis=-1, keepdims=True)
            var = jnp.var(x, axis=-1, keepdims=True)
            return (x - mu) * jax.lax.rsqrt(var + LN_EPS) * gamma + beta
        key = jax.random.key(seed)
        ks = jax.random.split(key, 4)
        B, S, D, F, E = (8, 128, 256, 512, 8)
        x = jax.random.normal(ks[0], (B, S, D), dtype=jnp.float32)
        Wr = jax.random.normal(ks[1], (D, E), dtype=jnp.float32) / np.sqrt(D)
        br = jnp.zeros((E,), jnp.float32)
        W1 = jax.random.normal(ks[2], (E, D, F), dtype=jnp.float32) / np.sqrt(D)
        b1 = jnp.zeros((E, F), jnp.float32)
        W2 = jax.random.normal(ks[3], (E, F, D), dtype=jnp.float32) / np.sqrt(F)
        b2 = jnp.zeros((E, D), jnp.float32)
        gamma = jnp.ones((D,), jnp.float32)
        beta = jnp.zeros((D,), jnp.float32)
        return {'x': x, 'Wr': Wr, 'br': br, 'W1': W1, 'b1': b1, 'W2': W2, 'b2': b2, 'gamma': gamma, 'beta': beta}
    _L0_ffn_all = _L0_ffn_setup()
    _L0_ffn_in = {k: v for k, v in _L0_ffn_all.items() if k in ('Wr', 'br', 'W1', 'b1', 'W2', 'b2', 'gamma', 'beta')}
    del _L0_ffn_all

    def _L1_gnn_setup():
        import jax, jax.numpy as jnp
        import numpy as np
        N_NODES = 50000
        N_EDGES = 15625
        IN_DIM = 256
        HID = 64
        HEADS = 4
        N_REL = 64
        key = jax.random.key(seed)
        ks = jax.random.split(key, 16)
        s = 0.02
        return {'node_features': jax.random.normal(ks[0], (N_NODES, IN_DIM), jnp.float32), 'edge_index': jax.random.randint(ks[1], (2, N_EDGES), 0, N_NODES, jnp.int32), 'edge_relations': jax.random.randint(ks[2], (N_EDGES,), 0, N_REL, jnp.int32), 'query_emb': jax.random.normal(ks[3], (IN_DIM,), jnp.float32), 'Wq': jax.random.normal(ks[4], (IN_DIM, HID * HEADS), jnp.float32) * s, 'bq': jnp.zeros((HID * HEADS,), jnp.float32), 'Wk': jax.random.normal(ks[5], (IN_DIM, HID * HEADS), jnp.float32) * s, 'bk': jnp.zeros((HID * HEADS,), jnp.float32), 'Wv': jax.random.normal(ks[6], (IN_DIM, HID * HEADS), jnp.float32) * s, 'bv': jnp.zeros((HID * HEADS,), jnp.float32), 'rel_w': jax.random.normal(ks[7], (N_REL, HID), jnp.float32) * s, 'Wo': jax.random.normal(ks[8], (HID * HEADS, IN_DIM), jnp.float32) * s, 'bo': jnp.zeros((IN_DIM,), jnp.float32), 'gamma': jnp.ones((IN_DIM,), jnp.float32), 'beta': jnp.zeros((IN_DIM,), jnp.float32)}
    _L1_gnn_all = _L1_gnn_setup()
    _L1_gnn_in = {k: v for k, v in _L1_gnn_all.items() if k in ('query_emb', 'Wq', 'bq', 'Wk', 'bk', 'Wv', 'bv', 'rel_w', 'Wo', 'bo', 'gamma', 'beta')}
    del _L1_gnn_all

    def _L1_ffn_setup():
        import jax, jax.numpy as jnp
        import numpy as np
        B, K, D = (512, 16, 256)
        E = 32
        H = int(D * 0.25)
        key = jax.random.key(seed)
        ks = jax.random.split(key, 7)
        d_rs = D ** (-0.5)
        h_rs = H ** (-0.5)
        x = jax.random.normal(ks[0], (B, K, D), dtype=jnp.float32)
        router_w = jax.random.uniform(ks[1], (E, D), jnp.float32, -d_rs, d_rs)
        router_b = jax.random.uniform(ks[2], (E,), jnp.float32, -d_rs, d_rs)
        W1 = jax.random.uniform(ks[3], (E, D, H), jnp.float32, -h_rs, h_rs)
        b1 = jax.random.uniform(ks[4], (E, H), jnp.float32, -h_rs, h_rs)
        W2 = jax.random.uniform(ks[5], (E, H, D), jnp.float32, -d_rs, d_rs)
        b2 = jax.random.uniform(ks[6], (E, D), jnp.float32, -d_rs, d_rs)
        return {'x': x, 'router_w': router_w, 'router_b': router_b, 'W1': W1, 'b1': b1, 'W2': W2, 'b2': b2}
    _L1_ffn_all = _L1_ffn_setup()
    _L1_ffn_in = {k: v for k, v in _L1_ffn_all.items() if k in ('router_w', 'router_b', 'W1', 'b1', 'W2', 'b2')}
    del _L1_ffn_all
    return {'x': x, 'src': src, 'dst': dst, 'edge_type_64': edge_type_64, 'L0_gnn_W': _L0_gnn_in['W'], 'L0_gnn_a_src': _L0_gnn_in['a_src'], 'L0_gnn_a_dst': _L0_gnn_in['a_dst'], 'L0_gnn_bias': _L0_gnn_in['bias'], 'L0_ffn_Wr': _L0_ffn_in['Wr'], 'L0_ffn_br': _L0_ffn_in['br'], 'L0_ffn_W1': _L0_ffn_in['W1'], 'L0_ffn_b1': _L0_ffn_in['b1'], 'L0_ffn_W2': _L0_ffn_in['W2'], 'L0_ffn_b2': _L0_ffn_in['b2'], 'L0_ffn_gamma': _L0_ffn_in['gamma'], 'L0_ffn_beta': _L0_ffn_in['beta'], 'L1_gnn_query_emb': _L1_gnn_in['query_emb'], 'L1_gnn_Wq': _L1_gnn_in['Wq'], 'L1_gnn_bq': _L1_gnn_in['bq'], 'L1_gnn_Wk': _L1_gnn_in['Wk'], 'L1_gnn_bk': _L1_gnn_in['bk'], 'L1_gnn_Wv': _L1_gnn_in['Wv'], 'L1_gnn_bv': _L1_gnn_in['bv'], 'L1_gnn_rel_w': _L1_gnn_in['rel_w'], 'L1_gnn_Wo': _L1_gnn_in['Wo'], 'L1_gnn_bo': _L1_gnn_in['bo'], 'L1_gnn_gamma': _L1_gnn_in['gamma'], 'L1_gnn_beta': _L1_gnn_in['beta'], 'L1_ffn_router_w': _L1_ffn_in['router_w'], 'L1_ffn_router_b': _L1_ffn_in['router_b'], 'L1_ffn_W1': _L1_ffn_in['W1'], 'L1_ffn_b1': _L1_ffn_in['b1'], 'L1_ffn_W2': _L1_ffn_in['W2'], 'L1_ffn_b2': _L1_ffn_in['b2']}

def reference(x, src, dst, edge_type_64, L0_gnn_W, L0_gnn_a_src, L0_gnn_a_dst, L0_gnn_bias, L0_ffn_Wr, L0_ffn_br, L0_ffn_W1, L0_ffn_b1, L0_ffn_W2, L0_ffn_b2, L0_ffn_gamma, L0_ffn_beta, L1_gnn_query_emb, L1_gnn_Wq, L1_gnn_bq, L1_gnn_Wk, L1_gnn_bk, L1_gnn_Wv, L1_gnn_bv, L1_gnn_rel_w, L1_gnn_Wo, L1_gnn_bo, L1_gnn_gamma, L1_gnn_beta, L1_ffn_router_w, L1_ffn_router_b, L1_ffn_W1, L1_ffn_b1, L1_ffn_W2, L1_ffn_b2):
    import jax
    import jax.numpy as jnp

    def _L0_gnn_ref(x, edge_index, W, a_src, a_dst, bias):
        import jax, jax.numpy as jnp
        import numpy as np
        N_NODES = 50000
        N_EDGES = 25000
        IN_FEAT = 256
        HEADS = 8
        OUT_FEAT = 32
        N = x.shape[0]
        H, F = a_src.shape
        h = (x @ W.T).reshape(N, H, F)
        src, dst = (edge_index[0], edge_index[1])
        h_src = h[src]
        h_dst = h[dst]
        alpha = jnp.einsum('ehf,hf->eh', h_src, a_src) + jnp.einsum('ehf,hf->eh', h_dst, a_dst)
        alpha = jnp.where(alpha >= 0, alpha, 0.2 * alpha)
        seg_max = jax.ops.segment_max(alpha, dst, num_segments=N)
        exp_a = jnp.exp(alpha - seg_max[dst])
        seg_sum = jax.ops.segment_sum(exp_a, dst, num_segments=N)
        alpha = exp_a / jnp.maximum(seg_sum[dst], 1e-10)
        msgs = h_src * alpha[:, :, None]
        agg = jax.ops.segment_sum(msgs, dst, num_segments=N)
        return agg.reshape(N, H * F) + bias

    def _L0_ffn_ref(x, Wr, br, W1, b1, W2, b2, gamma, beta):
        import math
        import jax, jax.numpy as jnp
        import numpy as np
        CAPACITY_FACTOR = 1.25
        TOP_K = 2
        LN_EPS = 1e-05

        def _layer_norm(x, gamma, beta):
            mu = jnp.mean(x, axis=-1, keepdims=True)
            var = jnp.var(x, axis=-1, keepdims=True)
            return (x - mu) * jax.lax.rsqrt(var + LN_EPS) * gamma + beta
        B, S, D = x.shape
        E = Wr.shape[1]
        N = B * S
        K = TOP_K
        logits = jnp.mean(x, axis=1) @ Wr + br
        routing_weights = jax.nn.softmax(logits, axis=-1)
        capacity = float(math.ceil(N * CAPACITY_FACTOR / E))
        expected_loads = routing_weights.sum(axis=0) * (N / B)
        scale = jnp.where(expected_loads > capacity, capacity / expected_loads, 1.0)
        routing_weights = jax.nn.softmax(routing_weights * scale, axis=-1)
        rw_tok = jnp.broadcast_to(routing_weights[:, None, :], (B, S, E)).reshape(N, E)
        top_w, top_i = jax.lax.top_k(rw_tok, K)
        top_w = jax.nn.softmax(top_w, axis=-1)
        xf = x.reshape(N, D)
        h = jax.nn.gelu(jnp.einsum('nd,edf->enf', xf, W1) + b1[:, None, :], approximate=False)
        y = jnp.einsum('enf,efd->end', h, W2) + b2[:, None, :]
        w_dense = jnp.zeros((N, E), x.dtype).at[jnp.arange(N)[:, None], top_i].add(top_w)
        out = jnp.einsum('ne,end->nd', w_dense, y).reshape(B, S, D)
        out = _layer_norm(out + x, gamma, beta)
        return out

    def _L1_gnn_ref(node_features, edge_index, edge_relations, query_emb, Wq, bq, Wk, bk, Wv, bv, rel_w, Wo, bo, gamma, beta):
        import jax, jax.numpy as jnp
        import numpy as np
        N_NODES = 50000
        N_EDGES = 15625
        IN_DIM = 256
        HID = 64
        HEADS = 4
        N_REL = 64
        N = node_features.shape[0]
        D = rel_w.shape[1]
        H = Wq.shape[1] // D
        enh = node_features + 0.1 * query_emb[None, :]
        Q = (enh @ Wq + bq).reshape(N, H, D)
        K = (enh @ Wk + bk).reshape(N, H, D)
        V = (enh @ Wv + bv).reshape(N, H, D)
        src, dst = (edge_index[0], edge_index[1])
        rel = rel_w[edge_relations]
        mod_k = K[src] + 0.2 * rel[:, None, :]
        scores = jnp.einsum('ehd,ehd->eh', Q[dst], mod_k) / D ** 0.5
        seg_max = jax.ops.segment_max(scores, dst, num_segments=N)
        ex = jnp.exp(scores - seg_max[dst])
        denom = jax.ops.segment_sum(ex, dst, num_segments=N)
        w = ex / denom[dst]
        agg = jax.ops.segment_sum(w[:, :, None] * V[src], dst, num_segments=N)
        deg = jax.ops.segment_sum(jnp.ones((src.shape[0],), jnp.float32), dst, num_segments=N)
        msgs = jnp.where(deg[:, None, None] > 0, agg, V)
        out = msgs.reshape(N, H * D) @ Wo + bo
        x = out + node_features
        mu = jnp.mean(x, axis=-1, keepdims=True)
        var = jnp.var(x, axis=-1, keepdims=True)
        return (x - mu) / jnp.sqrt(var + 1e-05) * gamma + beta

    def _L1_ffn_ref(x, router_w, router_b, W1, b1, W2, b2):
        import jax, jax.numpy as jnp
        import numpy as np
        B, K, D = (512, 16, 256)
        E = 32
        H = int(D * 0.25)
        xf = x.reshape(-1, D)
        logits = xf @ router_w.T + router_b
        idx = jnp.argmax(logits, axis=-1)
        w1t = jnp.take(W1, idx, axis=0)
        h = jnp.einsum('nd,ndh->nh', xf, w1t) + jnp.take(b1, idx, axis=0)
        h = jax.nn.relu(h)
        w2t = jnp.take(W2, idx, axis=0)
        out = jnp.einsum('nh,nhd->nd', h, w2t) + jnp.take(b2, idx, axis=0)
        out = jax.nn.relu(out)
        return out.reshape(x.shape)
    edge_index = jnp.stack([src, dst])
    x = x + _L0_gnn_ref(_layernorm(x, axis=-1), edge_index, L0_gnn_W, L0_gnn_a_src, L0_gnn_a_dst, L0_gnn_bias)
    x = x + _L0_ffn_ref(_layernorm(x, axis=-1)[None], L0_ffn_Wr, L0_ffn_br, L0_ffn_W1, L0_ffn_b1, L0_ffn_W2, L0_ffn_b2, L0_ffn_gamma, L0_ffn_beta)[0]
    x = x + _L1_gnn_ref(_layernorm(x, axis=-1), edge_index, edge_type_64, L1_gnn_query_emb, L1_gnn_Wq, L1_gnn_bq, L1_gnn_Wk, L1_gnn_bk, L1_gnn_Wv, L1_gnn_bv, L1_gnn_rel_w, L1_gnn_Wo, L1_gnn_bo, L1_gnn_gamma, L1_gnn_beta)
    x = x + _L1_ffn_ref(_layernorm(x, axis=-1)[None], L1_ffn_router_w, L1_ffn_router_b, L1_ffn_W1, L1_ffn_b1, L1_ffn_W2, L1_ffn_b2)[0]
    return x

_drawn_inputs = setup_inputs


def setup_inputs(seed=0):
    import zlib

    import numpy as np

    out = dict(_drawn_inputs(seed))
    spreads = {'L0_ffn_br': (0.0, 2.0),
     'L0_ffn_b1': (0.0, 0.397),
     'L0_ffn_b2': (0.0, 0.1),
     'L0_ffn_gamma': (1.0, 0.2),
     'L0_ffn_beta': (0.0, 0.1),
     'L1_gnn_bq': (0.0, 0.8),
     'L1_gnn_bk': (0.0, 2.0),
     'L1_gnn_bv': (0.0, 0.707),
     'L1_gnn_bo': (0.0, 0.364),
     'L1_gnn_gamma': (1.0, 0.2),
     'L1_gnn_beta': (0.0, 0.1)}
    factors = {'L0_gnn_bias': 3.222,
     'L1_gnn_query_emb': 8.0,
     'L1_gnn_Wq': 8.0,
     'L1_gnn_Wk': 8.0,
     'L1_gnn_Wv': 3.589,
     'L1_gnn_rel_w': 53.491,
     'L1_gnn_Wo': 3.122,
     'L1_ffn_router_b': 4.162,
     'L1_ffn_b1': 8.0,
     'L1_ffn_b2': 7.584,
     'L0_ffn_Wr': 8.0}
    for name, (base, spread) in spreads.items():
        noise = np.random.default_rng([zlib.crc32(name.encode()), seed]).standard_normal(out[name].shape)
        drawn = base * np.exp(spread * noise) if base else spread * noise
        out[name] = jnp.asarray(drawn.astype(out[name].dtype))
    for name, factor in factors.items():
        out[name] = (out[name] * factor).astype(out[name].dtype)
    return out
```

```python
from contextlib import ExitStack

import numpy as np

import concourse.bass as bass
from concourse import mybir

F32 = mybir.dt.float32
BF16 = mybir.dt.bfloat16
I32 = mybir.dt.int32
U32 = mybir.dt.uint32
ALU = mybir.AluOpType
ACT = mybir.ActivationFunctionType
AX_X = mybir.AxisListType.X

P = 128
N = 3125
E = 50000
D = 256
DC = D // P
WIN = -(-N // P)
NPAD = WIN * P
LAST = N - (WIN - 1) * P
TILES = -(-E // P)
TROWS = TILES + 1
TC = 4
TP = TROWS // TC
BATCH = 16
STEPS = -(-(TILES + WIN - 1) // (2 * BATCH)) * 2 * BATCH
SC = 4
SP = STEPS // SC
NEG = -1e30
BANK = 512
UNR = 5
WROUNDS = WIN // UNR
EPS = 1e-5
assert TP * TC == TROWS and SP * SC == STEPS and TP <= P and SP <= P and UNR * WROUNDS == WIN

H0, F0 = 8, 32
R0 = D + H0
H1, F1 = 4, 64
R1 = 2 * D


class Chain:

    def __init__(self, eng, sem, count=0):
        self.eng, self.sem, self.count, self.at = eng, sem, count, None

    def enter(self, i, per, trips):
        self.at, self.entered, self.per, self.trips = self.count + i * per, self.count, per, trips

    def leave(self):
        assert self.count - self.entered == self.per, (self.sem, self.count - self.entered, self.per)
        self.count, self.at = self.entered + self.per * self.trips, None

    def value(self):
        return self.count if self.at is None else self.at + (self.count - self.entered)

    def inc(self, ins):
        ins.then_inc(self.sem, 1)
        self.count += 1

    def wait(self):
        self.eng.wait_ge(self.sem, self.value())

    def link(self, ins):
        self.inc(ins)
        self.wait()


def chunks(n, k):
    return [(a, min(a + k, n)) for a in range(0, n, k)]


class Kernel:

    chain = None
    loads = 0

    def expect_loads(self, n):
        self.loads += n
        return 16 * self.loads

    def chain_on(self, v):
        self.chain = Chain(v, self.dve_steps, self.chain.count if self.chain else 0)
        return self.chain


def allocate(ctx, nc, k):
    def dram(name, shape, dt):
        return nc.dram_tensor(name, shape, dt).ap()

    def sb(name, shape, dt=F32):
        return ctx.enter_context(nc.sbuf_tensor(name, shape, dt))

    k.dve_steps = ctx.enter_context(nc.semaphore("dve_steps"))
    k.ln_var = ctx.enter_context(nc.semaphore("ln_var"))
    k.ln_std = ctx.enter_context(nc.semaphore("ln_std"))
    k.ln_rounds = 0
    k.loads_in = ctx.enter_context(nc.semaphore("loads_in"))
    k.edge_rows = dram("edge_rows", [TROWS, 3 * P], I32)
    k.step_rel = dram("step_rel", [STEPS + BATCH, P], BF16)
    k.step_typ = dram("step_typ", [STEPS + BATCH, P], BF16)
    k.step_cut8 = dram("step_cut8", [STEPS, H0, P + 4], F32)
    k.step_cut4 = dram("step_cut4", [STEPS, H1, P + 4], F32)
    k.step_ends = dram("step_ends", [2, STEPS], F32)
    k.step_win = dram("step_win", [1, STEPS], I32)
    k.h_rows = dram("h_rows", [NPAD, R0], F32)
    k.kv_rows = dram("kv_rows", [NPAD, R1], F32)
    k.xin1_rows = dram("xin1_rows", [NPAD, D], F32)

    slots = WIN + 31
    k.sorted_rows = dram("sorted_rows", [slots * P, D], F32)
    k.y_rows = dram("y_rows", [slots * P, D], F32)

    k.ident = sb("ident", [P, P])
    k.iota_row = sb("iota_row", [P, P])
    k.iota_col = sb("iota_col", [P, 1])
    k.ones = sb("ones", [P, P])
    k.eps = sb("eps", [P, 1])
    k.x = sb("x", [P, WIN, D])
    k.rel_col = sb("rel_col", [P, STEPS])
    k.src_col = sb("src_col", [P, STEPS], I32)
    k.win_row = sb("win_row", [1, STEPS + BATCH], I32)
    k.joined = sb("joined", [8, 3, STEPS + BATCH])
    k.hsel8 = sb("hsel8", [P, H0])
    k.hselT8 = sb("hselT8", [H0, P])
    k.mask8 = sb("mask8", [P, BATCH])
    k.hsel4 = sb("hsel4", [P, H1])
    k.hselT4 = sb("hselT4", [H1, P // 2])
    k.mask4 = sb("mask4", [P // 2, BATCH])


def steps_of_edges(nc, k, a):
    with ExitStack() as ctx:
        def sb(name, shape, dt=F32):
            return ctx.enter_context(nc.sbuf_tensor(name, shape, dt))

        def sem(name):
            return ctx.enter_context(nc.semaphore(name))

        tiles = sb("tiles", [TP, TC, 3, P], I32)
        ends_i = sb("ends_i", [TP, 2, TC], I32)
        ends_w = sb("ends_w", [TP, 2, TC])
        count = sb("count", [TP, TC])
        last_of = sb("last_of", [TP, TC])
        tril = sb("tril", [TP, TP])
        base = sb("base", [TP, TC])
        tot = sb("tot", [TP, TC])
        tile_g = sb("tile_g", [TP, TC, 2])
        iota_s = sb("iota_s", [TP, STEPS])
        hit = sb("hit", [TP, TC, STEPS])
        hit2 = sb("hit2", [TP, STEPS])
        step_no = sb("step_no", [SP, SC])
        tile_i = sb("tile_i", [SP, SC], I32)
        win_f = sb("win_f", [SP, SC])
        win_i = sb("win_i", [SP, SC], I32)
        win_x = sb("win_x", [SP, SC])
        rows = sb("rows", [SP, SC, 3, P], I32)
        rows_f = sb("rows_f", [SP, SC, 3, P])
        rel = sb("rel", [SP, SC, P])
        rel_b = sb("rel_b", [SP, SC, P], BF16)
        typ_b = sb("typ_b", [SP, SC, P], BF16)
        cut = sb("cut", [SP, SC, P + 4])
        ends_f = sb("ends_f", [SP, 2, SC])
        ends_r = sb("ends_r", [8, 2, STEPS])
        single = sb("single", [8, STEPS])
        ps_a = ctx.enter_context(nc.psum_tensor("ps_a", [P, 512], F32))
        ps_b = ctx.enter_context(nc.psum_tensor("ps_b", [P, 512], F32))
        ps_c = ctx.enter_context(nc.psum_tensor("ps_c", [P, 512], F32))

        ready = sem("pool_consts")
        pads = sem("tile_pads")
        loaded, all_loaded = k.loads_in, k.expect_loads(9)
        kept = sem("edges_kept")
        pe_done = sem("prep_pe")
        tile_ready = sem("tile_ready")
        gathered = sem("rows_gathered")
        stored = sem("prep_stored")
        reread = sem("ends_reread")
        block = ctx.enter_context(nc.Block())
        marks = {}

        FULL = E // P
        CL = TC - 1
        assert (FULL == CL * TP + TP - 2) and TP - 2 == 96

        @block.gpsimd
        def _(pool):
            pool.memset(tiles[96:TP, CL, 0, :], 4000).then_inc(pads, 1)
            pool.memset(tiles[96:TP, CL, 1:3, :], 0).then_inc(pads, 1)
            pool.wait_ge(pads, 2)
            pool.memset(tiles[96:97, CL, 0, :], NPAD - 1).then_inc(pads, 1)
            pool.wait_ge(pads, 3)
            c = Chain(pool, ready)
            pool.memset(k.win_row[:, STEPS:STEPS + BATCH], 0)
            pool.memset(k.ident[:, :], 0.0).then_inc(ready, 1)
            pool.memset(tril[:, :], 0.0).then_inc(ready, 1)
            pool.memset(k.ones[:, :], 1.0).then_inc(ready, 1)
            pool.memset(k.hsel8[:, :], 0.0).then_inc(ready, 1)
            pool.memset(k.hselT8[:, :], 0.0).then_inc(ready, 1)
            pool.memset(k.mask8[:, :], 1.0).then_inc(ready, 1)
            pool.memset(k.hsel4[:, :], 0.0).then_inc(ready, 1)
            pool.memset(k.hselT4[:, :], 0.0).then_inc(ready, 1)
            pool.memset(k.mask4[:, :], 1.0).then_inc(ready, 1)
            pool.memset(k.eps[:, :], EPS).then_inc(ready, 1)
            c.count = 10
            c.wait()
            pool.affine_select(out=k.ident[:, :], in_=k.ident[:, :], compare_op=ALU.not_equal, fill=1.0,
                               base=0, pattern=[[-1, P]], channel_multiplier=1).then_inc(ready, 1)
            pool.affine_select(out=tril[:, :], in_=tril[:, :], compare_op=ALU.is_ge, fill=1.0,
                               base=0, pattern=[[-1, TP]], channel_multiplier=1).then_inc(ready, 1)
            pool.iota(k.iota_row[:, :], pattern=[[1, P]], base=0, channel_multiplier=0,
                      allow_small_or_imprecise_dtypes=True).then_inc(ready, 1)
            pool.iota(k.iota_col[:, :], pattern=[[1, 1]], base=0, channel_multiplier=1,
                      allow_small_or_imprecise_dtypes=True).then_inc(ready, 1)
            pool.iota(iota_s[:, :], pattern=[[1, STEPS]], base=0, channel_multiplier=0,
                      allow_small_or_imprecise_dtypes=True).then_inc(ready, 1)
            pool.iota(step_no[:, :], pattern=[[SP, SC]], base=0, channel_multiplier=1,
                      allow_small_or_imprecise_dtypes=True).then_inc(ready, 1)
            pool.iota(tile_g[:, :, 0], pattern=[[TP, TC]], base=0, channel_multiplier=1,
                      allow_small_or_imprecise_dtypes=True).then_inc(ready, 1)
            c.count = 17
            for hsel, hselT, mask, H in ((k.hsel8, k.hselT8, k.mask8, H0), (k.hsel4, k.hselT4, k.mask4, H1)):
                c.wait()
                v = hselT[:, :].rearrange("h (s g) -> h s g", g=H)
                c.link(pool.affine_select(out=v, in_=v, compare_op=ALU.not_equal, fill=1.0, base=0,
                                          pattern=[[0, BATCH], [-1, H]], channel_multiplier=1))
                c.link(pool.affine_select(out=mask[:, :], in_=mask[:, :], compare_op=ALU.is_ge, fill=0.0,
                                          base=0, pattern=[[-H, BATCH]], channel_multiplier=1))
                c.link(pool.affine_select(out=mask[:, :], in_=mask[:, :], compare_op=ALU.is_ge, fill=0.0,
                                          base=H - 1, pattern=[[H, BATCH]], channel_multiplier=-1))
            marks["consts"] = c.count
            pool.wait_ge(kept, 16)
            pool.wait_ge(tile_ready, 1)
            for c4 in range(SC):
                pool.indirect_dma_start(out=rows[:, c4, :, :].rearrange("p a e -> p (a e)"), out_offset=None,
                                        in_=k.edge_rows[:, :],
                                        in_offset=bass.IndirectOffsetOnAxis(ap=tile_i[:, c4:c4 + 1], axis=0)
                                        ).then_inc(gathered, 16)

        @block.vector
        def _(v):
            c = k.chain_on(v)
            v.wait_ge(loaded, all_loaded)
            v.wait_ge(ready, marks["consts"])
            c.inc(v.tensor_single_scalar(ends_i[:, 0, :], tiles[:, :, 0, 0], 7, ALU.arith_shift_right))
            c.link(v.tensor_single_scalar(ends_i[:, 1, :], tiles[:, :, 0, P - 1], 7, ALU.arith_shift_right))
            c.link(v.tensor_copy(ends_w[:, :, :], ends_i[:, :, :]))
            c.link(v.scalar_tensor_tensor(out=count[:, :], in0=ends_w[:, 1, :], scalar=1.0,
                                          in1=ends_w[:, 0, :], op0=ALU.add, op1=ALU.subtract))
            marks["count"] = c.count
            v.wait_ge(pe_done, 1)
            c.link(v.tensor_copy(tot[:, :], ps_a[0:TP, 8:8 + TC]))
            c.link(v.tensor_copy(base[:, :], ps_a[0:TP, 0:TC]))
            for j in range(1, TC):
                c.link(v.tensor_tensor(base[:, j:TC], base[:, j:TC],
                                       tot[:, j - 1:j].to_broadcast([TP, TC - j]), ALU.add))
            c.link(v.tensor_tensor(last_of[:, :], base[:, :], count[:, :], ALU.add))
            c.link(v.tensor_tensor(tile_g[:, :, 1], ends_w[:, 0, :], base[:, :], ALU.subtract))
            for j in range(TC):
                if j == TC - 1:
                    c.link(v.tensor_scalar(tot[:, j:j + 1], ends_w[:, 0, j:j + 1], float(WIN), None, ALU.is_gt))
                    c.link(v.scalar_tensor_tensor(out=last_of[:, j:j + 1], in0=tot[:, j:j + 1],
                                                  scalar=float(STEPS), in1=last_of[:, j:j + 1],
                                                  op0=ALU.mult, op1=ALU.add))
                c.link(v.tensor_scalar(hit2[:, :], iota_s[:, :], last_of[:, j:j + 1], None, ALU.is_ge))
                c.link(v.scalar_tensor_tensor(out=hit[:, j, :], in0=iota_s[:, :], scalar=base[:, j:j + 1],
                                              in1=hit2[:, :], op0=ALU.is_ge, op1=ALU.subtract))
            marks["hit"] = c.count
            v.wait_ge(pe_done, 2)
            pv = ps_b[0:SP, 0:2 * SC].rearrange("p (c j) -> p c j", j=2)
            v.tensor_copy(tile_i[:, :], pv[:, :, 0]).then_inc(tile_ready, 1)
            c.link(v.tensor_tensor(win_f[:, :], step_no[:, :], pv[:, :, 1], ALU.add))
            c.link(v.tensor_scalar(win_f[:, :], win_f[:, :], float(WIN - 1), None, ALU.min))
            c.link(v.tensor_copy(win_i[:, :], win_f[:, :]))
            c.link(v.tensor_scalar(win_x[:, :], win_f[:, :], float(P), None, ALU.mult))
            v.wait_ge(pe_done, 3)
            c.inc(v.tensor_copy(k.hsel8[:, :], ps_c[:, 0:H0]))
            c.inc(v.tensor_copy(k.hsel4[0:P // 2, :], ps_c[0:P // 2, 16:16 + H1]))
            v.wait_ge(gathered, 16 * SC)
            c.link(v.tensor_copy(rows_f[:, :, :, :], rows[:, :, :, :]))
            c.inc(v.tensor_copy(ends_f[:, 0, :], rows_f[:, :, 0, 0]))
            c.inc(v.tensor_copy(ends_f[:, 1, :], rows_f[:, :, 0, P - 1]))
            marks["ends"] = c.count
            for j in range(SC):
                c.inc(v.tensor_scalar(rel[:, j, :], rows_f[:, j, 0, :], win_x[:, j:j + 1], None, ALU.subtract))
            c.wait()
            marks["rows"] = c.count
            c.inc(v.tensor_copy(rel_b[:, :, :], rel[:, :, :]))
            c.inc(v.tensor_copy(typ_b[:, :, :], rows_f[:, :, 2, :]))
            c.link(v.memset(cut[:, :, :], 0.0))
            c.link(v.tensor_tensor(cut[:, :, 1:P], rows_f[:, :, 0, 1:P], rows_f[:, :, 0, 0:P - 1], ALU.not_equal))
            c.link(v.tensor_scalar(cut[:, :, 1:P], cut[:, :, 1:P], NEG, None, ALU.mult))
            marks["stores"] = c.count
            v.wait_ge(pe_done, 4)
            c.inc(v.tensor_copy(k.rel_col[:, :], ps_a[:, 0:STEPS]))
            c.inc(v.tensor_copy(k.src_col[:, :], ps_b[:, 0:STEPS]))
            v.wait_ge(reread, 32)
            c.link(v.memset(k.joined[:, :, :], 1.0))
            c.link(v.tensor_tensor(k.joined[:, 0, 1:STEPS], ends_r[:, 0, 1:STEPS], ends_r[:, 1, 0:STEPS - 1],
                                   ALU.not_equal))
            c.link(v.tensor_tensor(single[:, :], ends_r[:, 0, :], ends_r[:, 1, :], ALU.not_equal))
            c.inc(v.tensor_tensor(k.joined[:, 1, 0:STEPS], k.joined[:, 0, 0:STEPS], single[:, :], ALU.max))
            c.link(v.tensor_tensor(k.joined[:, 2, 0:STEPS - 1], k.joined[:, 0, 1:STEPS], single[:, 0:STEPS - 1],
                                   ALU.max))
            c.link(v.tensor_scalar(k.joined[:, :, :], k.joined[:, :, :], NEG, None, ALU.mult))

        @block.tensor
        def _(pe):
            pe.wait_ge(ready, marks["consts"])
            pe.wait_ge(k.dve_steps, marks["count"])
            pe.matmul(ps_a[0:TP, 0:TC], tril[:, :], count[:, :], start=True, stop=True)
            pe.matmul(ps_a[0:TP, 8:8 + TC], k.ones[0:TP, 0:TP], count[:, :], start=True, stop=True
                      ).then_inc(pe_done, 1)
            pe.wait_ge(k.dve_steps, marks["hit"])
            for sc in range(SC):
                for c in range(TC):
                    mm = pe.matmul(ps_b[0:SP, 2 * sc:2 * sc + 2], hit[:, c, sc * SP:(sc + 1) * SP],
                                   tile_g[:, c, :], start=(c == 0), stop=(c == TC - 1))
            mm.then_inc(pe_done, 1)
            pe.transpose(ps_c[:, 0:H0], k.hselT8[:, :], k.ident[0:H0, 0:H0])
            pe.transpose(ps_c[0:P // 2, 16:16 + H1], k.hselT4[:, :], k.ident[0:H1, 0:H1]).then_inc(pe_done, 1)
            pe.wait_ge(k.dve_steps, marks["rows"])
            for sc in range(SC):
                pe.transpose(ps_a[:, sc * SP:(sc + 1) * SP], rel[:, sc, :], k.ident[0:SP, 0:SP])
            for sc in range(SC):
                mm = pe.transpose(ps_b[:, sc * SP:(sc + 1) * SP], rows_f[:, sc, 1, :], k.ident[0:SP, 0:SP])
            mm.then_inc(pe_done, 1)

        @block.sync
        def _(sp):
            for j, name in enumerate(("dst", "src", "edge_type_64")):
                v = a[name]
                sp.dma_start(tiles[:, 0:CL, j, :],
                             v[0:CL * TP * P].rearrange("(c p e) -> p c e", c=CL, e=P)).then_inc(loaded, 16)
                sp.dma_start(tiles[0:96, CL, j, :],
                             v[CL * TP * P:FULL * P].rearrange("(p e) -> p e", e=P)).then_inc(loaded, 16)
            sp.wait_ge(pads, 3)
            for j, name in enumerate(("dst", "src", "edge_type_64")):
                sp.dma_start(tiles[96:97, CL, j, 0:E - FULL * P],
                             a[name][FULL * P:E].rearrange("(p e) -> p e", p=1)).then_inc(loaded, 16)
            sp.wait_ge(loaded, all_loaded)
            sp.dma_start(k.edge_rows[:, :].rearrange("(c p) (j e) -> p c j e", p=TP, e=P),
                         tiles[:, :, :, :]).then_inc(kept, 16)
            sp.wait_ge(k.dve_steps, marks["ends"])
            for j in range(2):
                for c4 in range(SC):
                    sp.dma_start(k.step_ends[j:j + 1, c4 * SP:(c4 + 1) * SP].rearrange("o p -> p o"),
                                 ends_f[:, j, c4:c4 + 1]).then_inc(stored, 16)
            for c4 in range(SC):
                sp.dma_start(k.step_win[0:1, c4 * SP:(c4 + 1) * SP].rearrange("o p -> p o"),
                             win_i[:, c4:c4 + 1]).then_inc(stored, 16)
            sp.wait_ge(stored, 12 * 16)
            sp.dma_start(ends_r[:, :, :].rearrange("p j s -> p (j s)"),
                         k.step_ends[:, :].rearrange("j s -> (j s)").partition_broadcast(8)
                         ).then_inc(reread, 16)
            sp.dma_start(k.win_row[:, 0:STEPS], k.step_win[:, :]).then_inc(reread, 16)
            sp.wait_ge(k.dve_steps, marks["stores"])
            for dst, of in ((k.step_rel, rel_b), (k.step_typ, typ_b)):
                sp.dma_start(dst[0:STEPS, :].rearrange("(c p) e -> p c e", p=SP), of[:, :, :]).then_inc(stored, 16)
                sp.dma_start(dst[STEPS:STEPS + BATCH, :], of[0:BATCH, 0, :]).then_inc(stored, 16)
            for H, dst in ((H0, k.step_cut8), (H1, k.step_cut4)):
                for c4 in range(SC):
                    sp.dma_start(dst[c4 * SP:(c4 + 1) * SP, :, :],
                                 cut[:, c4, :].unsqueeze(1).to_broadcast([SP, H, P + 4])).then_inc(stored, 16)
            sp.wait_ge(stored, 24 * 16)
            sp.wait_ge(reread, 32)


LOTS = ((0, 3), (3, UNR))


def lot_of(j):
    return [n for n, (lo, hi) in enumerate(LOTS) if lo <= j < hi][0]


class Norm:

    def __init__(self, ctx, nc, k, name, turn=0, turns=1):
        self.stats = ctx.enter_context(nc.sbuf_tensor(name + "_stats", [P, UNR, 6], F32))
        self.mv = ctx.enter_context(nc.sbuf_tensor(name + "_mv", [P, UNR, 2], F32))
        self.std = ctx.enter_context(nc.sbuf_tensor(name + "_std", [P, UNR], F32))
        self.rstd = ctx.enter_context(nc.sbuf_tensor(name + "_rstd", [P, UNR], F32))
        self.var_ready, self.std_ready = k.ln_var, k.ln_std
        self.before, self.turns = k.ln_rounds + turn + 1, turns
        if turn == turns - 1:
            k.ln_rounds += turns * WROUNDS
        self.pad = ctx.enter_context(nc.sbuf_tensor(name + "_pad", [P, 1], F32))

    LINKS = 2 * UNR + 2

    def on_vector(self, v, c, i, x_of):
        c.inc(v.memset(self.pad[:, :], 0.0))
        for j in range(UNR):
            c.inc(v.bn_stats(self.stats[:, j, :], x_of(j)))
        c.wait()
        c.inc(v.memset(self.pad[:, :], 0.0))
        for j in range(UNR):
            ins = v.bn_aggr(self.mv[:, j, :], self.stats[:, j, :])
            if j < UNR - 1:
                c.inc(ins)
        ins.then_inc(self.var_ready, 1)
        v.wait_ge(self.std_ready, i * self.turns + self.before)
        c.link(v.reciprocal(self.rstd[:, :], self.std[:, :]))

    def on_scalar(self, act, i, eps):
        act.wait_ge(self.var_ready, i * self.turns + self.before)
        act.activation(self.std[:, :], self.mv[:, :, 1], ACT.Sqrt, bias=eps[:, 0:1]).then_inc(self.std_ready, 1)

    def apply(self, v, out, x, j):
        return v.tensor_scalar(out, x, self.mv[:, j, 0:1], self.rstd[:, j:j + 1], ALU.subtract, ALU.mult)


def project_first(nc, k, a):
    with ExitStack() as ctx:
        def sb(name, shape, dt=F32):
            return ctx.enter_context(nc.sbuf_tensor(name, shape, dt))

        def ps(name, shape):
            return ctx.enter_context(nc.psum_tensor(name, shape, F32))

        def sem(name):
            return ctx.enter_context(nc.semaphore(name))

        RW = D + 2 * H0
        w = sb("w0", [P, DC, D])
        a_col = sb("a0_col", [P, 2, DC])
        amask = sb("amask", [P, DC, H0])
        ablk = sb("ablk", [P, DC, 2, H0])
        wx = sb("wx0", [P, DC, RW])
        ad = sb("ad0f", [P, WIN, H0])
        ad_r = sb("ad0r", [P, WIN, H0])
        xn = sb("xn0", [P, UNR, D])
        xt = sb("xt0", [P, UNR, DC, P])
        h = sb("h0", [P, UNR, RW])
        norm = Norm(ctx, nc, k, "ln0")
        ps_t = [ps(f"ps0_t{i}", [P, DC, P]) for i in range(2)]
        ps_h = [ps(f"ps0_h{i}", [P, RW]) for i in range(2)]
        ps_w = ps("ps0_w", [P, 2, D])
        ps_a = ps("ps0_a", [P, DC, 2 * H0])

        loaded, all_loaded = k.loads_in, k.expect_loads(5)
        xl = sem("x_loaded")
        xz = sem("x_zeroed")
        masks = sem("amask_ready")
        abl = sem("ablk_ready")
        wt = sem("w0_transposed")
        wxr = sem("wx0_ready")
        normed = sem("normed0")
        turned = sem("turned0")
        xt_ready = sem("xt0_ready")
        mm_done = sem("mm0_done")
        h_ready = sem("h0_ready")
        h_kept = [sem(f"h0_kept{j}") for j in range(len(LOTS))]
        block = ctx.enter_context(nc.Block())

        @block.gpsimd
        def _(pool):
            pool.memset(k.x[:, WIN - 1, :], 0.0).then_inc(xz, 1)
            pool.memset(amask[:, :, :], 1.0).then_inc(masks, 1)
            pool.wait_ge(masks, 1)
            pool.affine_select(out=amask[:, :, :], in_=amask[:, :, :], compare_op=ALU.is_ge, fill=0.0, base=0,
                               pattern=[[P, DC], [-F0, H0]], channel_multiplier=1).then_inc(masks, 1)
            pool.wait_ge(masks, 2)
            pool.affine_select(out=amask[:, :, :], in_=amask[:, :, :], compare_op=ALU.is_ge, fill=0.0, base=F0 - 1,
                               pattern=[[-P, DC], [F0, H0]], channel_multiplier=-1).then_inc(masks, 1)

        @block.sync
        def _(sp):
            sp.dma_start(k.x[:, 0:WIN - 1, :], a["x"][0:(WIN - 1) * P, :].rearrange("(w p) d -> p w d", p=P)
                         ).then_inc(xl, 16)
            sp.wait_ge(xz, 1)
            sp.dma_start(k.x[0:LAST, WIN - 1, :], a["x"][(WIN - 1) * P:N, :]).then_inc(xl, 16)
            sp.dma_start(w[:, :, :], a["L0_gnn_W"].rearrange("(c p) d -> p c d", p=P)).then_inc(loaded, 16)
            for j, name in enumerate(("L0_gnn_a_src", "L0_gnn_a_dst")):
                flat = a[name].rearrange("h f -> (h f)")
                for c in range(DC):
                    sp.dma_start(a_col[:, j, c:c + 1], flat[c * P:(c + 1) * P].rearrange("(p o) -> p o", o=1)
                                 ).then_inc(loaded, 16)
            with sp.Fori(0, WROUNDS) as i:
                for n, (lo, hi) in enumerate(LOTS):
                    sp.wait_ge(h_ready, i * UNR + hi)
                    sp.dma_start(k.h_rows[bass.ds((i * UNR + lo) * P, (hi - lo) * P), :]
                                 .rearrange("(w p) r -> p w r", p=P), h[:, lo:hi, 0:R0]).then_inc(h_kept[n], 16)
            for n in range(len(LOTS)):
                sp.wait_ge(h_kept[n], 16 * WROUNDS)

        @block.vector
        def _(v):
            c = k.chain_on(v)
            v.wait_ge(loaded, all_loaded)
            v.wait_ge(masks, 3)
            for j in range(2):
                for c2 in range(DC):
                    v.tensor_scalar(ablk[:, c2, j, :], amask[:, c2, :], a_col[:, j, c2:c2 + 1], None, ALU.mult
                                    ).then_inc(abl, 1)
            v.wait_ge(xl, 32)
            with v.Fori(0, WROUNDS) as i:
                c.enter(i, Norm.LINKS, WROUNDS)
                norm.on_vector(v, c, i, lambda j: k.x[:, i * UNR + j, :])
                for j in range(UNR):
                    v.wait_ge(turned, i * UNR)
                    norm.apply(v, xn[:, j, :], k.x[:, i * UNR + j, :], j).then_inc(normed, 1)
                c.leave()
            v.wait_ge(h_ready, WIN)
            hi, mid, lo = (k.by_dst[:, :, j, :] for j in range(3))
            c.link(v.tensor_copy(hi, ad[:, :, :]))
            c.link(v.tensor_tensor(ad_r[:, :, :], ad[:, :, :], hi, ALU.subtract))
            c.link(v.tensor_copy(mid, ad_r[:, :, :]))
            c.link(v.tensor_tensor(ad_r[:, :, :], ad_r[:, :, :], mid, ALU.subtract))
            c.link(v.tensor_copy(lo, ad_r[:, :, :]))

        @block.scalar
        def _(act):
            act.wait_ge(wt, 1)
            act.copy(wx[:, :, 0:D], ps_w[:, :, :]).then_inc(wxr, 1)
            act.wait_ge(wt, 2)
            act.copy(wx[:, :, D:RW], ps_a[:, :, :]).then_inc(wxr, 1)

            def turn(i, j):
                act.wait_ge(turned, i * UNR + (j + 1))
                act.wait_ge(mm_done, i * UNR)
                act.copy(xt[:, j, :, :], ps_t[j % 2][:, :, :]).then_inc(xt_ready, 1)

            def take(i, j):
                act.wait_ge(mm_done, i * UNR + (j + 1))
                act.wait_ge(h_kept[lot_of(j)], 16 * i)
                act.copy(h[:, j, :], ps_h[j % 2][:, :]).then_inc(h_copied, 1)
                act.wait_ge(h_copied, i * UNR + (j + 1))
                act.copy(ad[:, i * UNR + j, :], h[:, j, R0:RW]).then_inc(h_ready, 1)

            h_copied = sem("h0_copied")
            with act.Fori(0, WROUNDS) as i:
                norm.on_scalar(act, i, k.eps)
                turn(i, 0)
                for j in range(1, UNR):
                    turn(i, j)
                    take(i, j - 1)
                take(i, UNR - 1)

        @block.tensor
        def _(pe):
            pe.wait_ge(loaded, all_loaded)
            for c in range(DC):
                for dc in range(DC):
                    mm = pe.transpose(ps_w[:, dc, c * P:(c + 1) * P], w[:, c, dc * P:(dc + 1) * P], k.ident[:, :])
            mm.then_inc(wt, 1)
            pe.wait_ge(abl, 4)
            for dc in range(DC):
                for c in range(DC):
                    mm = pe.matmul(ps_a[:, dc, :], w[:, c, dc * P:(dc + 1) * P],
                                   ablk[:, c, :, :].rearrange("p j h -> p (j h)"),
                                   start=(c == 0), stop=(c == DC - 1))
            mm.then_inc(wt, 1)
            pe.wait_ge(wxr, 2)

            def turn(i, j):
                pe.wait_ge(normed, i * UNR + (j + 1))
                if j >= 2:
                    pe.wait_ge(xt_ready, i * UNR + (j - 1))
                else:
                    pe.wait_ge(xt_ready, i * UNR)
                for c in range(DC):
                    mm = pe.transpose(ps_t[j % 2][:, c, :], xn[:, j, c * P:(c + 1) * P], k.ident[:, :])
                mm.then_inc(turned, 1)

            def multiply(i, j):
                pe.wait_ge(xt_ready, i * UNR + (j + 1))
                pe.wait_ge(h_ready, i * UNR + max(j - 1, 0))
                for c in range(DC):
                    mm = pe.matmul(ps_h[j % 2][:, :], xt[:, j, c, :], wx[:, c, :], start=(c == 0), stop=(c == DC - 1))
                mm.then_inc(mm_done, 1)

            with pe.Fori(0, WROUNDS) as i:
                turn(i, 0)
                for j in range(1, UNR):
                    turn(i, j)
                    multiply(i, j - 1)
                multiply(i, UNR - 1)


class Layer:

    def __init__(self, H, F, R, ring, messages, sums, values):
        self.H, self.F, self.R = H, F, R
        self.ring = ring
        self.messages, self.sums, self.values = messages, sums, values
        self.value_column = self.R // (2 * D) * D
        self.PH = BATCH * H


FIRST = Layer(H0, F0, R0, 3, (0, R0), (D, R0), (0, D))
SECOND = Layer(H1, F1, R1, 2, (D - H1, R1), (0, H1), (H1, H1 + D))
GROUP = 4
GROUPS = BATCH // GROUP
BATCHES = STEPS // BATCH
QP = 2
PAIRS = BATCH // QP


def edges(nc, k, L, ctx, acc):
    H, F, PH = L.H, L.F, L.PH
    first = L is FIRST
    mlo, mhi = L.messages
    MW = mhi - mlo
    hsel, hselT, mask, cuts = ((k.hsel8, k.hselT8, k.mask8, k.step_cut8) if first
                               else (k.hsel4, k.hselT4, k.mask4, k.step_cut4))
    rows_of = k.h_rows if first else k.kv_rows
    n = "e0_" if first else "e1_"

    def sb(name, shape, dt=F32):
        return ctx.enter_context(nc.sbuf_tensor(n + name, shape, dt))

    def ps(name, shape):
        return ctx.enter_context(nc.psum_tensor(n + name, shape, F32))

    def sem(name):
        return ctx.enter_context(nc.semaphore(n + name))

    R = L.ring
    two = range(2)
    ring = range(R)
    PARTS = 1 if first else 2
    g = [sb(f"rows{b}", [P, BATCH, L.R]) for b in ring]
    src_i = [sb(f"src{b}", [P, BATCH], I32) for b in ring]
    rel = [sb(f"rel{b}", [P, BATCH * P], BF16) for b in ring]
    cut = [sb(f"cut{b}", [PH, P + 4]) for b in ring]
    to_dst = [sb(f"to_dst{b}", [P, BATCH * P], BF16) for b in ring]
    HOTS = 4 if first else 2
    of_dst = [sb(f"of_dst{b}", [P, GROUP, P]) for b in range(HOTS)]
    sc = sb("scores", [P, BATCH, H])
    sc2 = sb("scores2", [P, P // H, H])
    fwd = sb("fwd", [PH, P])
    bwd = sb("bwd", [PH, P])
    diff = sb("diff", [PH, P])
    prob = sb("prob", [P, P])
    tip = sb("tip", [P, 2, BATCH])
    run = [sb(f"run{b}", [H, BATCH + 1]) for b in ring]
    join_back = sb("join_back", [H, BATCH])
    back = sb("back", [H, BATCH + 1])
    ctxt = sb("ctxt", [H, 2, BATCH])
    new_max = sb("new_max", [H, 1])
    fall = sb("fall", [H, 1])
    factor = sb("factor", [H, 1])
    diag = sb("diag", [H, H])
    node0 = sb("node0", [H, P])
    ini2 = sb("ini2", [PH, 2, BATCH])
    ini = sb("ini", [PH, 2])
    fac = sb("fac", [P, H])
    tock = sb("tock", [P, 1])
    tick = sb("tick", [P, 1])
    NB = 6 if first else 3
    ZEROED = 4 if first else 7
    psm = [ps(f"sum{b}", [P, BANK])[:, 0:MW] for b in range(NB)]
    ps_t = ps("turned", [P, BANK])
    A = 2 * P
    ps_tip = ps_t[0:H, A:A + 2 * BATCH]
    ps_ctx = ps_t[0:PH, A + 2 * BATCH:A + 4 * BATCH]
    ps_fac = ps_t[:, A + 4 * BATCH:A + 4 * BATCH + H]
    if first:
        look = ps("look", [P, BANK])[:, 0:3 * PH].rearrange("p (s j h) -> p s j h", j=3, h=H)
    else:
        typ = [sb(f"typ{b}", [F1, BATCH * P], BF16) for b in ring]
        to_typ = sb("to_typ", [F1, BATCH * P], BF16)
        prod = [sb(f"prod{b}", [P, QP, H * F]) for b in two]
        ps_q = [ps(f"query{b}", [P, QP, D]) for b in two]
        ps_r = [ps(f"relation{b}", [P, BANK])[:, 0:QP * F].rearrange("p (s f) -> p s f", f=F) for b in two]

    zeroed = sem("zeroed")
    rel_in = [sem(f"rel_in{b}") for b in ring]
    cut_in = [sem(f"cut_in{b}") for b in ring]
    src_ready = sem("src_ready")
    rows_in = [[sem(f"rows_in{b}_{part}") for part in range(PARTS)] for b in ring]
    masks_ready = sem("masks_ready")
    looked = sem("looked")
    look_used = sem("look_used")
    scored = sem("scored")
    sc_turned = sem("sc_turned")
    tips = sem("tips")
    tips_by_head = sem("tips_by_head")
    fall_ready = sem("fall_ready")
    factor_ready = sem("factor_ready")
    ctx_ready = sem("ctx_ready")
    ctx_back = sem("ctx_back")
    diff_ready = sem("diff_ready")
    prob_ready = sem("prob_ready")
    prob_turned = sem("prob_turned")
    prob_in_rows = sem("prob_in_rows")
    msg_ready = sem("msg_ready")
    hot_ready = sem("hot_ready")
    BY_ACT = range(2, GROUPS) if first else range(GROUPS)
    summed = sem("summed")
    added = sem("added")
    AHEAD = R * BATCH
    KR = 16 if first else 32
    block = ctx.enter_context(nc.Block())

    plo = D if first else D - H

    def windows(eng, name):
        sets = []

        def load(m):
            regs = [eng.alloc_register(f"{n}{name}{len(sets)}_{s}") for s in range(BATCH)]
            sets.append(regs)
            eng.load(regs, k.win_row[0:1, bass.ds(m * BATCH, BATCH)])
            return [eng.snap(r, donate=True, min_val=0, max_val=WIN - 1) for r in regs]
        return load

    def after(i, b, d):
        return i + (b + d) // R, (b + d) % R

    def periods(eng, body, first_of, last, chain=None, per=0):
        assert first_of % R == 0
        trips = (last + 1 - first_of) // R
        with eng.Fori(0, trips) as i:
            if chain:
                chain.enter(i, per * R, trips)
            for b in ring:
                body(i + first_of // R if first_of else i, b)
            if chain:
                chain.leave()
        for m in range(first_of + trips * R, last + 1):
            body(m // R, m % R)

    @block.sync
    def _(sp):
        def load_rel(m, b):
            sp.dma_start(rel[b][:, :], k.step_rel[bass.ds(m * BATCH, BATCH), :].rearrange("s e -> (s e)")
                         .partition_broadcast(P)).then_inc(rel_in[b], 16)
            if not first:
                sp.dma_start(typ[b][:, :], k.step_typ[bass.ds(m * BATCH, BATCH), :].rearrange("s e -> (s e)")
                             .partition_broadcast(F1)).then_inc(rel_in[b], 16)

        def load_cut(m, b):
            sp.dma_start(cut[b][:, :], cuts[bass.ds(m * BATCH, BATCH), :, :].rearrange("s h e -> (s h) e")
                         ).then_inc(cut_in[b], 16)

        def refill(i, b):
            m = i * R + b
            sp.wait_ge(diff_ready, m - R + 1)
            load_rel(m, b)
            load_cut(m, b)

        for b in ring:
            load_rel(b, b)
            load_cut(b, b)
        periods(sp, refill, R, BATCHES - 1)
        sp.wait_ge(diff_ready, BATCHES - R + 1)
        load_rel(BATCHES, BATCHES % R)

    @block.gpsimd
    def _(pool):
        pool.memset(acc[:, :, :], 0.0).then_inc(zeroed, 1)
        pool.memset(run[R - 1][:, :], NEG).then_inc(zeroed, 1)
        pool.memset(back[:, :], NEG).then_inc(zeroed, 1)
        pool.memset(tock[:, :], 0.0).then_inc(zeroed, 1)
        for t in () if first else (sc2, prob, tip):
            pool.memset(t[:], 0.0).then_inc(zeroed, 1)
        pool.wait_ge(zeroed, ZEROED)
        pool.memset(ctxt[:, :, :], NEG).then_inc(summed, AHEAD)
        pool.memset(ini[:, :], NEG).then_inc(look_used, 2)
        pool.memset(fac[:, :], 0.0).then_inc(added, NB)

        def gather(i, b, q):
            m = i * R + b
            steps = slice(q * GROUP, (q + 1) * GROUP)
            pool.tensor_copy(src_i[b][:, steps], k.src_col[:, bass.ds(m * BATCH + steps.start, GROUP)]
                             ).then_inc(src_ready, 1)
            pool.wait_ge(src_ready, (m * GROUPS + q) * 2 + 1)
            pool.tensor_tensor(tick[:, :], tock[:, :], tock[:, :], ALU.add).then_inc(src_ready, 1)
            for s in range(steps.start, steps.stop):
                pool.indirect_dma_start(out=g[b][:, s, :], out_offset=None, in_=rows_of[:, :],
                                        in_offset=bass.IndirectOffsetOnAxis(ap=src_i[b][:, s:s + 1], axis=0)
                                        ).then_inc(rows_in[b][q * PARTS // GROUPS], 16)

        def refill(i, b):
            for q in range(GROUPS):
                pool.wait_ge(summed, (i * R + b) * BATCH + ((q + 1) * GROUP + AHEAD))
                gather(i + 1, b, q)

        for b in ring:
            for q in range(GROUPS):
                gather(0, b, q)
        periods(pool, refill, 0, BATCHES - R - 1)

    ROWS_IN = 16 * BATCH // PARTS

    @block.vector
    def _(v):
        c = k.chain_on(v)

        def masks(i, b):
            v.wait_ge(rel_in[b], (i + 1) * KR)
            if not first:
                v.tensor_scalar(to_typ[:, :], typ[b][:, :], k.iota_col[0:F1, 0:1], None, ALU.is_equal)
            v.tensor_scalar(to_dst[b][:, :], rel[b][:, :], k.iota_col[:, 0:1], None, ALU.is_equal
                            ).then_inc(masks_ready, 1)

        def scores_first(i, b):
            v.wait_ge(looked, i * R + (b + 1))
            v.wait_ge(rows_in[b][0], (i + 1) * ROWS_IN)
            c.link(v.tensor_reduce(sc[:, :, :], look.rearrange("p s j h -> p s h j"), AX_X, ALU.add))
            c.link(v.tensor_tensor(sc[:, :, :], sc[:, :, :], g[b][:, :, D:D + H], ALU.add))
            v.scalar_tensor_tensor(out=sc2[:, 0:BATCH, :], in0=sc[:, :, :], scalar=0.2, in1=sc[:, :, :],
                                   op0=ALU.mult, op1=ALU.max).then_inc(scored, 1)

        def scores_second(i, b, q, m=0, w=None, adds=()):
            at = slice(q * QP, (q + 1) * QP)
            keys = g[b][:, at, 0:D].rearrange("p s (h f) -> p s h f", h=H)
            v.wait_ge(looked, (i * R + b) * PAIRS + (q + 1))
            v.wait_ge(rows_in[b][q * PARTS // PAIRS], (i + 1) * ROWS_IN)
            c.inc(v.tensor_tensor(keys, keys, ps_r[q % 2].unsqueeze(2).to_broadcast([P, QP, H, F]), ALU.add))
            add(m, adds[:1], w)
            c.wait()
            v.tensor_tensor(prod[q % 2][:, :, :], g[b][:, at, 0:D], ps_q[q % 2][:, :, :], ALU.mult
                            ).then_inc(look_used, 1)
            add(m, adds[1:], w)
            v.wait_ge(look_used, (i * R + b) * PAIRS + (q + 3))
            v.tensor_reduce(sc2[:, at, :], prod[q % 2][:, :, :].rearrange("p s (h f) -> p s h f", h=H), AX_X, ALU.add
                            ).then_inc(scored, 1)

        def scans(b, ini_f, ini_b):
            c.inc(v.tensor_tensor_scan(fwd[:, :], cut[b][:, 0:P], ps_t[0:PH, 0:P], ini_f, ALU.add, ALU.max))
            c.link(v.tensor_tensor_scan(bwd[:, ::-1], cut[b][:, P:0:-1], ps_t[0:PH, P - 1::-1], ini_b,
                                        ALU.add, ALU.max))

        def step_maxima(i, b):
            m = i * R + b
            v.wait_ge(sc_turned, m + 1)
            v.wait_ge(cut_in[b], (i + 1) * 16)
            c.inc(v.tensor_copy(join_back[:, :], k.joined[0:H, 2, bass.ds(m * BATCH, BATCH)]))
            scans(b, NEG, NEG)
            v.tensor_scalar(tip[0:PH, 0, :], mask[:, :], fwd[:, P - 1:P], None, ALU.mult)
            v.tensor_scalar(tip[0:PH, 1, :], mask[:, :], bwd[:, 0:1], None, ALU.mult).then_inc(tips, 1)

        def across_steps(i, b):
            m = i * R + b
            before = run[(b - 1) % R]
            v.wait_ge(tips_by_head, m + 1)
            c.inc(v.tensor_copy(run[b][:, 0:1], before[:, BATCH:BATCH + 1]))
            c.inc(v.tensor_tensor_scan(run[b][:, 1:BATCH + 1], k.joined[0:H, 1, bass.ds(m * BATCH, BATCH)],
                                       ps_tip[:, 0:BATCH], before[:, BATCH:BATCH + 1], ALU.add, ALU.max))
            c.link(v.tensor_tensor_scan(back[:, BATCH - 1::-1], join_back[:, BATCH - 1::-1],
                                        ps_tip[:, 2 * BATCH - 1:BATCH - 1:-1], NEG, ALU.add, ALU.max))
            c.inc(v.tensor_tensor(ctxt[:, 0, :], run[b][:, 0:BATCH], k.joined[0:H, 0, bass.ds(m * BATCH, BATCH)],
                                  ALU.add))
            c.link(v.tensor_tensor(ctxt[:, 1, :], back[:, 1:BATCH + 1],
                                   k.joined[0:H, 0, bass.ds(m * BATCH + 1, BATCH)], ALU.add))
            c.link(v.tensor_tensor(new_max[:, :], back[:, 0:1], ctxt[:, 0, 0:1], ALU.max))
            v.tensor_scalar(fall[:, :], ctxt[:, 0, 0:1], new_max[:, 0:1], -80.0, ALU.subtract, ALU.max
                            ).then_inc(fall_ready, 1)
            v.tensor_scalar(node0[:, :], k.iota_row[0:H, :], rel[b][0:H, 0:1], None, ALU.is_equal)

        def factors(i, b):
            v.wait_ge(factor_ready, i * R + (b + 1))
            v.scalar_tensor_tensor(out=diag[:, :], in0=k.ident[0:H, 0:H], scalar=factor[:, 0:1],
                                   in1=k.ident[0:H, 0:H], op0=ALU.mult, op1=ALU.subtract).then_inc(ctx_ready, 1)

        def differences(i, b, m=0, w=None, adds=()):
            v.wait_ge(ctx_back, i * R + (b + 1))
            c.inc(v.tensor_tensor(ini2[:, :, :], ps_ctx.rearrange("p (j s) -> p j s", j=2),
                                  mask[:, :].unsqueeze(1).to_broadcast([PH, 2, BATCH]), ALU.mult))
            add(m, adds[0:1], w)
            c.wait()
            c.inc(v.tensor_copy(fac[:, :], ps_fac))
            c.inc(v.tensor_reduce(ini[:, :], ini2[:, :, :], AX_X, ALU.add))
            add(m, adds[1:2], w)
            c.wait()
            scans(b, ini[:, 0:1], ini[:, 1:2])
            add(m, adds[2:3], w)
            c.link(v.tensor_tensor(fwd[:, :], fwd[:, :], bwd[:, :], ALU.max))
            v.tensor_tensor(diff[:, :], ps_t[0:PH, 0:P], fwd[:, :], ALU.subtract).then_inc(diff_ready, 1)

        def rescale(m, w):
            v.wait_ge(added, m * BATCH + NB)
            sums = acc[:, w[0], L.sums[0]:L.sums[1]]
            vals = acc[:, w[0], L.values[0]:L.values[1]].rearrange("p (h f) -> p h f", h=H)
            c.inc(v.scalar_tensor_tensor(out=sums, in0=fac[:, :], scalar=1.0, in1=sums, op0=ALU.add, op1=ALU.mult))
            c.link(v.scalar_tensor_tensor(out=vals, in0=fac[:, :].unsqueeze(2).to_broadcast([P, H, F]), scalar=1.0,
                                          in1=vals, op0=ALU.add, op1=ALU.mult))

        def hot(i, b, q):
            ins = v.tensor_tensor(of_dst[q % HOTS][:, :, :], k.iota_row[:, :].unsqueeze(1).to_broadcast([P, GROUP, P]),
                                  k.rel_col[:, bass.ds((i * R + b) * BATCH + q * GROUP, GROUP)].unsqueeze(2)
                                  .to_broadcast([P, GROUP, P]), ALU.is_equal)
            if q in BY_ACT:
                ins.then_inc(hot_ready, 1)

        def values(i, b, q, half):
            if q == half == 0:
                v.wait_ge(prob_in_rows, i * R + (b + 1))
            lo = q * GROUP + half * GROUP // 2
            steps = slice(lo, lo + GROUP // 2)
            vals = g[b][:, steps, 0:D].rearrange("p s (h f) -> p s h f", h=H)
            pr = g[b][:, steps, plo:plo + H]
            ins = v.tensor_tensor(vals, vals, pr.unsqueeze(3).to_broadcast([P, GROUP // 2, H, F]), ALU.mult)
            if half:
                ins.then_inc(hot_ready, 1)

        def make(i, b, q):
            hot(i, b, q)
            if q not in BY_ACT:
                values(i, b, q, 0)
                values(i, b, q, 1)

        def add(m, steps, w):
            for s in steps:
                v.wait_ge(summed, m * BATCH + (s + 1 + AHEAD))
                v.wait_ge(added, m * BATCH + (s + NB))
                v.tensor_tensor(acc[:, w[s], :], acc[:, w[s], :], psm[s % NB], ALU.add).then_inc(added, 1)

        load_windows = windows(v, "dve_w")

        def period(i, b):
            m = i * R + b
            i1, b1 = after(i, b, 1)
            w = load_windows(m)
            if first:
                scores_first(i1, b1)
                rescale(m, w)
                make(i, b, 0)
                step_maxima(i1, b1)
                make(i, b, 1)
                across_steps(i1, b1)
                add(m, [0], w)
                hot(i, b, 2)
                add(m, [1], w)
                factors(i1, b1)
                add(m, [2], w)
                hot(i, b, 3)
                add(m, [3], w)
                masks(*after(i, b, 2))
                add(m, range(4, 8), w)
                differences(i1, b1, m, w, [8, 9, 10])
                add(m, range(11, BATCH), w)
            else:
                rescale(m, w)
                for q in range(PAIRS):
                    if q < 2:
                        hot(i, b, q)
                    if q == 5:
                        hot(i, b, 2)
                    scores_second(i1, b1, q, m, w, range(2 * q - 6, 2 * q - 4) if q >= 3 else ())
                hot(i, b, 3)
                step_maxima(i1, b1)
                add(m, [10], w)
                across_steps(i1, b1)
                add(m, [11, 12], w)
                factors(i1, b1)
                masks(*after(i, b, 2))
                differences(i1, b1, m, w, [13, 14, 15])

        v.wait_ge(zeroed, ZEROED)
        v.wait_ge(summed, AHEAD)
        v.wait_ge(look_used, 2)
        masks(0, 0)
        if first:
            scores_first(0, 0)
        else:
            for q in range(PAIRS):
                scores_second(0, 0, q)
        step_maxima(0, 0)
        across_steps(0, 0)
        factors(0, 0)
        differences(0, 0)
        masks(*after(0, 0, 1))
        periods(v, period, 0, BATCHES - 2, c, 17 + (2 if first else PAIRS))
        m, i, b = BATCHES - 1, (BATCHES - 1) // R, (BATCHES - 1) % R
        w = load_windows(m)
        rescale(m, w)
        for q in range(GROUPS):
            make(i, b, q)
            if q or not first:
                lo = (q - first) * GROUP
                add(m, range(lo, lo + GROUP), w)
        if first:
            add(m, range(BATCH - GROUP, BATCH), w)

    @block.scalar
    def _(act):
        def values(i, b, q):
            for s in range(q * GROUP, (q + 1) * GROUP):
                for h in range(H):
                    lo = L.value_column + h * F
                    x = g[b][:, s, lo:lo + F]
                    ins = act.activation(x, x, ACT.Copy, scale=g[b][:, s, plo + h:plo + h + 1])
            ins.then_inc(msg_ready, 1)

        def fall_factor(m):
            act.wait_ge(fall_ready, m + 1)
            act.activation(factor[:, :], fall[:, :], ACT.Exp).then_inc(factor_ready, 1)

        def probabilities(m, b):
            act.wait_ge(diff_ready, m + 1)
            act.activation(prob[0:PH, :], diff[:, :], ACT.Exp).then_inc(prob_ready, 1)
            act.wait_ge(prob_turned, m + 1)
            act.copy(g[b][:, :, plo:plo + H],
                     ps_t[:, P:P + PH].rearrange("p (s h) -> p s h", h=H)).then_inc(prob_in_rows, 1)

        def period(i, b):
            m1, b1 = i * R + (b + 1), (b + 1) % R
            act.wait_ge(prob_in_rows, m1)
            for q in BY_ACT[:-1]:
                values(i, b, q)
            if first:
                fall_factor(m1)
            values(i, b, BY_ACT[-1])
            if not first:
                fall_factor(m1)
            probabilities(m1, b1)

        fall_factor(0)
        probabilities(0, 0)
        periods(act, period, 0, BATCHES - 2)
        act.wait_ge(prob_in_rows, BATCHES)
        for q in BY_ACT:
            values(0, (BATCHES - 1) % R, q)

    @block.tensor
    def _(pe):
        load_windows = windows(pe, "pe_w")

        def look_first(m, b, scores):
            w = load_windows(m)
            pe.wait_ge(masks_ready, m + 1)
            if scores:
                pe.wait_ge(scored, m)
            for s in range(BATCH):
                mm = pe.matmul(look[:, s, :, :].rearrange("p j h -> p (j h)"), to_dst[b][:, s * P:(s + 1) * P],
                               k.by_dst[:, w[s], :, :].rearrange("p j h -> p (j h)"), start=True, stop=True)
            mm.then_inc(looked, 1)

        def look_second(m, b, q, w):
            pe.wait_ge(look_used, m * PAIRS + (q + 1))
            for t in range(QP):
                s = q * QP + t
                for j in range(3):
                    pe.matmul(ps_q[q % 2][:, t, :], to_dst[b][:, s * P:(s + 1) * P],
                              k.by_dst[:, w[s], j, :], start=(j == 0), stop=(j == 2))
                for j in range(3):
                    mm = pe.matmul(ps_r[q % 2][:, t, :], to_typ[:, s * P:(s + 1) * P],
                                   k.by_typ[:, j, :], start=(j == 0), stop=(j == 2))
            mm.then_inc(looked, 1)

        def look_pairs(m, b):
            w = load_windows(m)
            pe.wait_ge(masks_ready, m + 1)
            for q in range(2):
                look_second(m, b, q, w)

        def turn_scores(m):
            pe.wait_ge(scored, m + 1 if first else (m + 1) * PAIRS)
            if not (isinstance(m, int) and m == 0):
                pe.wait_ge(prob_in_rows, m)
            pe.transpose(ps_t[:, 0:P], sc2[:, :, :].rearrange("p s h -> p (s h)"), k.ident[:, :]
                         ).then_inc(sc_turned, 1)

        def turn_tips(m):
            pe.wait_ge(tips, m + 1)
            pe.matmul(ps_tip, hsel[:, :], tip[:, :, :].rearrange("p j s -> p (j s)"), start=True, stop=True
                      ).then_inc(tips_by_head, 1)

        def turn_context(m):
            pe.wait_ge(ctx_ready, m + 1)
            pe.matmul(ps_ctx, hselT[:, :], ctxt[:, :, :].rearrange("h j s -> h (j s)"), start=True, stop=True)
            pe.matmul(ps_fac, node0[:, :], diag[:, :], start=True, stop=True).then_inc(ctx_back, 1)

        def turn_probabilities(m):
            pe.wait_ge(prob_ready, m + 1)
            pe.transpose(ps_t[:, P:2 * P], prob[:, :], k.ident[:, :]).then_inc(prob_turned, 1)

        def sums(m, b, steps):
            for s in steps:
                q = s // GROUP
                if s % GROUP == 0:
                    pe.wait_ge(hot_ready, m * GROUPS + (q + 1))
                    if q in BY_ACT:
                        pe.wait_ge(msg_ready, m * len(BY_ACT) + (q - BY_ACT[0] + 1))
                pe.wait_ge(added, m * BATCH + (s + 1))
                pe.matmul(psm[s % NB], of_dst[q % HOTS][:, s % GROUP, :], g[b][:, s, mlo:mhi],
                          start=True, stop=True).then_inc(summed, 1)

        def period(i, b):
            m = i * R + b
            m1, b1 = m + 1, (b + 1) % R
            if first:
                turn_scores(m1)
                sums(m, b, range(0, 2))
                turn_tips(m1)
                sums(m, b, range(2, 8))
                turn_context(m1)
                sums(m, b, range(8, 10))
                look_first(m + 2, (b + 2) % R, True)
                sums(m, b, range(10, 14))
                turn_probabilities(m1)
                sums(m, b, range(14, BATCH))
            else:
                w = load_windows(m1)
                for q in range(2, PAIRS):
                    look_second(m1, b1, q, w)
                    if q >= 3:
                        sums(m, b, range(2 * q - 6, 2 * q - 4))
                turn_scores(m1)
                sums(m, b, [10])
                turn_tips(m1)
                sums(m, b, range(11, 15))
                turn_context(m1)
                sums(m, b, [15])
                look_pairs(m + 2, (b + 2) % R)
                turn_probabilities(m1)

        if first:
            look_first(0, 0, False)
        else:
            w = load_windows(0)
            pe.wait_ge(masks_ready, 1)
            for q in range(PAIRS):
                look_second(0, 0, q, w)
        turn_scores(0)
        turn_tips(0)
        turn_context(0)
        if first:
            turn_probabilities(0)
            look_first(1, 1, True)
        else:
            look_pairs(1, 1)
            turn_probabilities(0)
        periods(pe, period, 0, BATCHES - 2)
        pe.wait_ge(prob_in_rows, BATCHES)
        sums(BATCHES - 1, (BATCHES - 1) % R, range(BATCH))


def mix_first(nc, k, a):
    with ExitStack() as ctx:
        def sb(name, shape, dt=F32):
            return ctx.enter_context(nc.sbuf_tensor(name, shape, dt))

        def sem(name):
            return ctx.enter_context(nc.semaphore(name))

        bias = sb("bias0", [P, D])
        inv = sb("inv0", [P, UNR, H0])
        xn = sb("xn1", [P, UNR, D])
        norm = Norm(ctx, nc, k, "ln1")
        ps_t = [ctx.enter_context(nc.psum_tensor(f"ps1_t{i}", [P, BANK], F32)) for i in range(2)]
        loaded, all_loaded = k.loads_in, k.expect_loads(1)
        normed = sem("normed1")
        turned = sem("turned1")
        xt_ready = sem("xt1_ready")
        block = ctx.enter_context(nc.Block())

        @block.sync
        def _(sp):
            sp.dma_start(bias[:, :], a["L0_gnn_bias"].partition_broadcast(P)).then_inc(loaded, 16)

        @block.vector
        def _(v):
            c = k.chain_on(v)
            v.wait_ge(loaded, all_loaded)
            with v.Fori(0, WROUNDS) as i:
                c.enter(i, Norm.LINKS + 6, WROUNDS)
                at = bass.ds(i * UNR, UNR)
                vals = k.acc0[:, at, 0:D].rearrange("p w (h f) -> p w h f", h=H0)
                c.link(v.tensor_scalar(inv[:, :, :], k.acc0[:, at, D:R0], 1e-10, None, ALU.max))
                c.inc(v.tensor_tensor(k.x[:, at, :], k.x[:, at, :],
                                      bias[:, :].unsqueeze(1).to_broadcast([P, UNR, D]), ALU.add))
                c.link(v.reciprocal(inv[:, :, :], inv[:, :, :]))
                c.link(v.tensor_tensor(vals, vals, inv[:, :, :].unsqueeze(3).to_broadcast([P, UNR, H0, F0]), ALU.mult))
                c.link(v.tensor_tensor(k.x[:, at, :], k.x[:, at, :], k.acc0[:, at, 0:D], ALU.add))
                norm.on_vector(v, c, i, lambda j: k.x[:, i * UNR + j, :])
                v.tensor_copy(k.rstd[:, at], norm.rstd[:, :])
                c.inc(v.tensor_copy(k.mean[:, at], norm.mv[:, :, 0]))
                v.wait_ge(turned, i * UNR)
                for j in range(UNR):
                    norm.apply(v, xn[:, j, :], k.x[:, i * UNR + j, :], j).then_inc(normed, 1)
                c.leave()
            v.wait_ge(xt_ready, WIN)
            v.tensor_reduce(k.total[:, :], k.xt[:, :, 0:N], AX_X, ALU.add)

        @block.scalar
        def _(act):
            with act.Fori(0, WROUNDS) as i:
                norm.on_scalar(act, i, k.eps)
                for j in range(UNR):
                    act.wait_ge(turned, i * UNR + (j + 1))
                    act.copy(k.xt[:, :, bass.ds((i * UNR + j) * P, P)],
                             ps_t[j % 2][:, 0:D].rearrange("p (c n) -> p c n", c=DC)).then_inc(xt_ready, 1)

        @block.tensor
        def _(pe):
            with pe.Fori(0, WROUNDS) as i:
                for j in range(UNR):
                    pe.wait_ge(normed, i * UNR + (j + 1))
                    pe.wait_ge(xt_ready, i * UNR + max(j - 1, 0))
                    for c in range(DC):
                        mm = pe.transpose(ps_t[j % 2][:, c * P:(c + 1) * P], xn[:, j, c * P:(c + 1) * P],
                                          k.ident[:, :])
                    mm.then_inc(turned, 1)


TOP = 2
E0, HID = 8, 512
FC = HID // P
CAPACITY = float(-(-N * 5 // (E0 * 4)))


def route_first(nc, k, a):
    with ExitStack() as ctx:
        def sb(name, shape, dt=F32):
            return ctx.enter_context(nc.sbuf_tensor(name, shape, dt))

        def sem(name):
            return ctx.enter_context(nc.semaphore(name))

        wr = sb("wr", [P, DC, E0])
        br = sb("br", [1, E0])
        lg = sb("lg", [1, E0])
        ex = sb("ex", [1, E0])
        top = sb("top", [1, 8])
        one = sb("one", [1, 8])
        idx_u = sb("idx_u", [1, 8], U32)
        idx = sb("idx", [1, 8], I32)
        tw = sb("tw", [1, TOP])
        tw_col = sb("tw_col", [TOP, P])
        tws = sb("tws", [P, TOP])
        b2 = sb("b2_0", [TOP, D])
        ps = ctx.enter_context(nc.psum_tensor("ps_route", [P, BANK], F32))
        ps_b = ctx.enter_context(nc.psum_tensor("ps_route_b", [P, BANK], F32))
        loaded, all_loaded = k.loads_in, k.expect_loads(2)
        exp_in = sem("route_exp_in")
        exp_out = sem("route_exp_out")
        pe_done = sem("route_pe")
        picked = sem("picked")
        w_in = sem("w0_in")
        block = ctx.enter_context(nc.Block())
        marks = {}

        @block.vector
        def _(v):
            c = k.chain_on(v)
            sent = [0]

            def softmax(x, n, out):
                c.link(v.tensor_reduce(one[:, 0:1], x, AX_X, ALU.max))
                v.tensor_scalar(ex[:, 0:n], x, one[:, 0:1], None, ALU.subtract).then_inc(exp_in, 1)
                sent[0] += 1
                v.wait_ge(exp_out, sent[0])
                c.link(v.tensor_reduce(one[:, 1:2], ex[:, 0:n], AX_X, ALU.add))
                c.link(v.reciprocal(one[:, 2:3], one[:, 1:2]))
                c.link(v.tensor_scalar(out, ex[:, 0:n], one[:, 2:3], None, ALU.mult))

            v.wait_ge(loaded, all_loaded)
            v.wait_ge(pe_done, 1)
            c.link(v.scalar_tensor_tensor(out=lg[:, :], in0=ps[0:1, 0:E0], scalar=1.0 / N, in1=br[:, :],
                                          op0=ALU.mult, op1=ALU.add))
            softmax(lg[:, :], E0, lg[:, :])
            c.link(v.tensor_scalar(ex[:, :], lg[:, :], float(N), None, ALU.mult))
            c.link(v.tensor_scalar(one[:, :], ex[:, :], CAPACITY, None, ALU.max))
            c.link(v.reciprocal(one[:, :], one[:, :]))
            c.link(v.tensor_scalar(one[:, :], one[:, :], CAPACITY, 1.0, ALU.mult, ALU.min))
            c.link(v.tensor_scalar(top[:, :], ex[:, :], CAPACITY, None, ALU.is_gt))
            c.link(v.scalar_tensor_tensor(out=one[:, :], in0=one[:, :], scalar=-1.0, in1=top[:, :],
                                          op0=ALU.add, op1=ALU.mult))
            c.link(v.scalar_tensor_tensor(out=lg[:, :], in0=one[:, :], scalar=1.0, in1=lg[:, :],
                                          op0=ALU.add, op1=ALU.mult))
            softmax(lg[:, :], E0, lg[:, :])
            c.link(v.max(top[:, :], lg[:, :]))
            c.link(v.max_index(idx_u[:, :], top[:, :], lg[:, :]))
            v.tensor_copy(idx[:, :], idx_u[:, :]).then_inc(picked, 1)
            softmax(top[:, 0:TOP], TOP, tw[:, :])
            marks["tw"] = c.count
            v.wait_ge(pe_done, 2)
            c.inc(v.tensor_copy(tws[:, :], ps[:, 16:16 + TOP]))
            c.link(v.tensor_copy(tw_col[:, :], ps[0:TOP, 32:32 + P]))
            marks["tw_col"] = c.count
            v.wait_ge(w_in, 16 * 4 * TOP)
            for e in range(TOP):
                v.tensor_scalar(k.w2[:, e, :, :], k.w2[:, e, :, :], tws[:, e:e + 1], None, ALU.mult)
            v.wait_ge(pe_done, 3)
            v.tensor_copy(k.b2row[:, :], ps_b[:, 0:D])

        @block.scalar
        def _(act):
            for t, n in enumerate((E0, E0, TOP)):
                act.wait_ge(exp_in, t + 1)
                act.activation(ex[:, 0:n], ex[:, 0:n], ACT.Exp).then_inc(exp_out, 1)

        @block.tensor
        def _(pe):
            pe.wait_ge(loaded, all_loaded)
            for dc in range(DC):
                mm = pe.matmul(ps[0:1, 0:E0], k.total[:, dc:dc + 1], wr[:, dc, :], start=(dc == 0), stop=(dc == DC - 1))
            mm.then_inc(pe_done, 1)
            pe.wait_ge(k.dve_steps, marks["tw"])
            pe.matmul(ps[:, 16:16 + TOP], k.ones[0:1, :], tw[:, :], start=True, stop=True)
            pe.matmul(ps[0:TOP, 32:32 + P], tw[:, :], k.ones[0:1, :], start=True, stop=True).then_inc(pe_done, 1)
            pe.wait_ge(k.dve_steps, marks["tw_col"])
            pe.wait_ge(w_in, 16 * 4 * TOP)
            pe.matmul(ps_b[:, 0:D], tw_col[:, :], b2[:, :], start=True, stop=True).then_inc(pe_done, 1)

        @block.sync
        def _(sp):
            sp.dma_start(wr[:, :, :], a["L0_ffn_Wr"].rearrange("(c p) e -> p c e", p=P)).then_inc(loaded, 16)
            sp.dma_start(br[:, :], a["L0_ffn_br"].unsqueeze(0)).then_inc(loaded, 16)
            sp.wait_ge(picked, 1)
            for e in range(TOP):
                x = sp.value_load(idx[0:1, e:e + 1], min_val=0, max_val=E0 - 1)
                one_of = bass.ds(x, 1)
                sp.dma_start(k.w1[:, e, :, :], a["L0_ffn_W1"][one_of, :, :].rearrange("o (c p) f -> p (o c) f", p=P)
                             ).then_inc(w_in, 16)
                sp.dma_start(k.w2[:, e, :, :], a["L0_ffn_W2"][one_of, :, :].rearrange("o (c p) f -> p (o c) f", p=P)
                             ).then_inc(w_in, 16)
                sp.dma_start(k.b1[:, e, :], a["L0_ffn_b1"][one_of, :].rearrange("o (c p) -> p (o c)", p=P),
                             allow_slow_non_contiguous=True).then_inc(w_in, 16)
                sp.dma_start(b2[e:e + 1, :], a["L0_ffn_b2"][one_of, :]).then_inc(w_in, 16)
            sp.wait_ge(w_in, 16 * 4 * TOP)


RN = UNR * P
QKV_LOADS = 9
HALF = RN // 2


def feed_first(nc, k, a):
    with ExitStack() as ctx:
        def sb(name, shape, dt=F32):
            return ctx.enter_context(nc.sbuf_tensor(name, shape, dt))

        def sem(name):
            return ctx.enter_context(nc.semaphore(name))

        EF = TOP * FC
        gamma = sb("gamma0", [P, D])
        beta = sb("beta0", [P, D])
        hid = sb("hid0", [P, EF, RN])
        zeros = sb("zeros", [P, D])
        z = sb("z0", [P, UNR, D])
        norm = Norm(ctx, nc, k, "ln2")
        ps_h = [ctx.enter_context(nc.psum_tensor(f"ps2_h{i}", [P, BANK], F32)) for i in range(4)]
        ps_y = [ctx.enter_context(nc.psum_tensor(f"ps2_y{i}", [P, BANK], F32)) for i in range(2)]
        loaded, all_loaded = k.loads_in, k.expect_loads(2)
        zeros_ready = sem("zeros_ready")
        zeroed = sem("sorted_zeroed")
        up = sem("up0")
        act_done = sem("gelu_done")
        down = sem("down0")
        y_used = sem("y0_used")
        block = ctx.enter_context(nc.Block())
        UP = EF * 2

        @block.sync
        def _(sp):
            sp.dma_start(gamma[:, :], a["L0_ffn_gamma"].partition_broadcast(P)).then_inc(loaded, 16)
            sp.dma_start(beta[:, :], a["L0_ffn_beta"].partition_broadcast(P)).then_inc(loaded, 16)
            for j, name in enumerate("kvq"):
                sp.dma_start(k.wqkv[:, :, j, :], a[f"L1_gnn_W{name}"].rearrange("(c p) f -> p c f", p=P)
                             ).then_inc(k.w_in, 16)
                sp.dma_start(k.bqkv[:, j, :], a[f"L1_gnn_b{name}"].partition_broadcast(P)).then_inc(k.w_in, 16)
            for c in range(DC):
                sp.dma_start(k.q01[:, c:c + 1], a["L1_gnn_query_emb"][c * P:(c + 1) * P]
                             .rearrange("(p o) -> p o", o=1)).then_inc(k.w_in, 16)
            sp.dma_start(k.relw[:, :], a["L1_gnn_rel_w"]).then_inc(k.w_in, 16)
            sp.wait_ge(zeros_ready, 1)
            sp.dma_start(k.sorted_rows[:, :].rearrange("(s p) d -> p s d", p=P),
                         zeros[:, :].unsqueeze(1).to_broadcast([P, SLOTS, D])).then_inc(zeroed, 16)
            sp.wait_ge(zeroed, 16)

        @block.gpsimd
        def _(pool):
            pool.memset(zeros[:, :], 0.0).then_inc(zeros_ready, 1)

        @block.tensor
        def _(pe):
            with pe.Fori(0, WROUNDS) as i:
                for t in range(UP):
                    ef, half = t // 2, t % 2
                    e, f = ef // FC, ef % FC
                    pe.wait_ge(act_done, i * UP + max(t - 3, 0))
                    for dc in range(DC):
                        mm = pe.matmul(ps_h[t % 4][:, 0:HALF], k.w1[:, e, dc, f * P:(f + 1) * P],
                                       k.xt[:, dc, bass.ds(i * RN + half * HALF, HALF)],
                                       start=(dc == 0), stop=(dc == DC - 1))
                    mm.then_inc(up, 1)
                pe.wait_ge(act_done, (i + 1) * UP)
                for j in range(UNR):
                    pe.wait_ge(y_used, i * UNR + max(j - 1, 0))
                    for ef in range(EF):
                        mm = pe.matmul(ps_y[j % 2][:, 0:D], hid[:, ef, j * P:(j + 1) * P],
                                       k.w2[:, ef // FC, ef % FC, :], start=(ef == 0), stop=(ef == EF - 1))
                    mm.then_inc(down, 1)

        @block.scalar
        def _(act):
            with act.Fori(0, WROUNDS) as i:
                for t in range(UP):
                    ef, half = t // 2, t % 2
                    act.wait_ge(up, i * UP + (t + 1))
                    act.wait_ge(down, i * UNR)
                    act.activation(hid[:, ef, half * HALF:(half + 1) * HALF], ps_h[t % 4][:, 0:HALF], ACT.Gelu,
                                   bias=k.b1[:, ef // FC, ef % FC:ef % FC + 1]).then_inc(act_done, 1)
                norm.on_scalar(act, i, k.eps)

        @block.vector
        def _(v):
            c = k.chain_on(v)
            v.wait_ge(loaded, all_loaded)
            with v.Fori(0, WROUNDS) as i:
                c.enter(i, UNR + 1 + 1 + Norm.LINKS + UNR + 3, WROUNDS)
                for j in range(UNR):
                    w = i * UNR + j
                    c.inc(v.tensor_scalar(z[:, j, :], k.x[:, w, :], k.mean[:, bass.ds(w, 1)],
                                          k.rstd[:, bass.ds(w, 1)], ALU.subtract, ALU.mult))
                c.wait()
                c.link(v.tensor_tensor(z[:, :, :], z[:, :, :], k.b2row[:, :].unsqueeze(1).to_broadcast([P, UNR, D]),
                                       ALU.add))
                for j in range(UNR):
                    v.wait_ge(down, i * UNR + (j + 1))
                    v.tensor_tensor(z[:, j, :], z[:, j, :], ps_y[j % 2][:, 0:D], ALU.add).then_inc(y_used, 1)
                v.wait_ge(y_used, (i + 1) * UNR)
                c.link(v.memset(norm.pad[:, :], 0.0))
                norm.on_vector(v, c, i, lambda j: z[:, j, :])
                for j in range(UNR):
                    c.inc(norm.apply(v, z[:, j, :], z[:, j, :], j))
                c.wait()
                c.link(v.tensor_tensor(z[:, :, :], z[:, :, :], gamma[:, :].unsqueeze(1).to_broadcast([P, UNR, D]),
                                       ALU.mult))
                c.link(v.tensor_tensor(z[:, :, :], z[:, :, :], beta[:, :].unsqueeze(1).to_broadcast([P, UNR, D]),
                                       ALU.add))
                at = bass.ds(i * UNR, UNR)
                c.link(v.tensor_tensor(k.x[:, at, :], k.x[:, at, :], z[:, :, :], ALU.add))
                c.leave()


def feed_forward_tensors(ctx, nc, k):
    def sb(name, shape, dt=F32):
        return ctx.enter_context(nc.sbuf_tensor(name, shape, dt))

    k.xt = sb("xt", [P, DC, NPAD])
    k.mean = sb("mean", [P, WIN])
    k.rstd = sb("rstd", [P, WIN])
    k.total = sb("total", [P, DC])
    k.w1 = sb("w1", [P, TOP, DC, HID])
    k.w2 = sb("w2", [P, TOP, FC, D])
    k.b1 = sb("b1", [P, TOP, FC])
    k.b2row = sb("b2row", [P, D])


def project_second(nc, k, a):
    with ExitStack() as ctx:
        def sb(name, shape, dt=F32):
            return ctx.enter_context(nc.sbuf_tensor(name, shape, dt))

        def sem(name):
            return ctx.enter_context(nc.semaphore(name))

        def bank(name):
            return ctx.enter_context(nc.psum_tensor(name, [P, BANK], F32))

        w, b, q01, relw = k.wqkv, k.bqkv, k.q01, k.relw
        rel_r = sb("rel_r", [F1, F1])
        xn = sb("xn2", [P, UNR, D])
        xt = sb("xt2", [P, UNR, DC, P])
        kv = sb("kv", [P, UNR, 2 * D])
        q = sb("qf", [P, UNR, D])
        norm = Norm(ctx, nc, k, "ln3")
        ps_t = [bank(f"ps3_t{i}") for i in range(2)]
        ps_kv = [bank(f"ps3_kv{i}") for i in range(2)]
        ps_q = [bank(f"ps3_q{i}") for i in range(2)]

        normed = sem("normed3")
        turned = sem("turned3")
        xt_ready = sem("xt3_ready")
        mm_done = sem("mm3_done")
        kv_ready = sem("kv_ready")
        q_ready = sem("q_ready")
        xn_kept = [sem(f"xn_kept{j}") for j in range(len(LOTS))]
        kv_kept = [sem(f"kv_kept{j}") for j in range(len(LOTS))]
        part = sem("q_part")
        rest = sem("q_rest")
        marks = {}
        block = ctx.enter_context(nc.Block())

        @block.sync
        def _(sp):
            with sp.Fori(0, WROUNDS) as i:
                for ready, dst, of, kept in ((normed, k.xin1_rows, xn, xn_kept), (kv_ready, k.kv_rows, kv, kv_kept)):
                    for n, (lo, hi) in enumerate(LOTS):
                        sp.wait_ge(ready, i * UNR + hi)
                        sp.dma_start(dst[bass.ds((i * UNR + lo) * P, (hi - lo) * P), :]
                                     .rearrange("(w p) r -> p w r", p=P), of[:, lo:hi, :]).then_inc(kept[n], 16)
            for n in range(len(LOTS)):
                sp.wait_ge(xn_kept[n], 16 * WROUNDS)
                sp.wait_ge(kv_kept[n], 16 * WROUNDS)

        @block.vector
        def _(v):
            c = k.chain_on(v)
            v.wait_ge(k.w_in, 16 * QKV_LOADS)
            c.inc(v.tensor_scalar(q01[:, :], q01[:, :], 0.1, None, ALU.mult))
            c.inc(v.tensor_scalar(b[:, 2, :], b[:, 2, :], 0.125, None, ALU.mult))
            c.link(v.tensor_scalar(relw[:, :], relw[:, :], 0.2, None, ALU.mult))
            marks["q01"] = c.count
            c.link(v.tensor_copy(k.rel3[:, 0, :], relw[:, :]))
            c.link(v.tensor_tensor(rel_r[:, :], relw[:, :], k.rel3[:, 0, :], ALU.subtract))
            c.link(v.tensor_copy(k.rel3[:, 1, :], rel_r[:, :]))
            c.link(v.tensor_tensor(rel_r[:, :], rel_r[:, :], k.rel3[:, 1, :], ALU.subtract))
            c.link(v.tensor_copy(k.rel3[:, 2, :], rel_r[:, :]))
            with v.Fori(0, WROUNDS) as i:
                c.enter(i, Norm.LINKS, WROUNDS)
                norm.on_vector(v, c, i, lambda j: k.x[:, i * UNR + j, :])
                for j in range(UNR):
                    v.wait_ge(turned, i * UNR)
                    v.wait_ge(xn_kept[lot_of(j)], i * 16)
                    norm.apply(v, xn[:, j, :], k.x[:, i * UNR + j, :], j).then_inc(normed, 1)
                for j in range(UNR):
                    v.wait_ge(mm_done, i * UNR + (j + 1))
                    v.wait_ge(kv_kept[lot_of(j)], i * 16)
                    v.tensor_tensor(kv[:, j, :].rearrange("p (a f) -> p a f", a=2),
                                    ps_kv[j % 2][:, :].rearrange("p (a f) -> p a f", a=2), b[:, 0:2, :], ALU.add
                                    ).then_inc(kv_ready, 1)
                    v.scalar_tensor_tensor(out=q[:, j, :], in0=ps_q[j % 2][:, 0:D], scalar=0.125,
                                           in1=b[:, 2, :], op0=ALU.mult, op1=ALU.add).then_inc(q_ready, 1)
                at = bass.ds(i * UNR, UNR)
                for t in range(2):
                    v.wait_ge(part, i * 3 + (t + 1))
                    v.tensor_tensor(q[:, :, :], q[:, :, :], k.q3[:, at, t, :], ALU.subtract).then_inc(rest, 1)
                v.wait_ge(part, i * 3 + 3)
                c.leave()

        @block.scalar
        def _(act):
            act.wait_ge(k.dve_steps, marks["q01"])
            with act.Fori(0, WROUNDS) as i:
                norm.on_scalar(act, i, k.eps)
                for j in range(UNR):
                    act.wait_ge(turned, i * UNR + (j + 1))
                    act.wait_ge(mm_done, i * UNR)
                    for c in range(DC):
                        ins = act.activation(xt[:, j, c, :], ps_t[j % 2][:, c * P:(c + 1) * P], ACT.Identity,
                                             bias=q01[:, c:c + 1])
                    ins.then_inc(xt_ready, 1)
                at = bass.ds(i * UNR, UNR)
                act.wait_ge(q_ready, (i + 1) * UNR)
                for t in range(3):
                    if t:
                        act.wait_ge(rest, i * 2 + t)
                    act.copy(k.q3[:, at, t, :], q[:, :, :]).then_inc(part, 1)

        @block.tensor
        def _(pe):
            pe.wait_ge(k.w_in, 16 * QKV_LOADS)

            def turn(i, j):
                pe.wait_ge(normed, i * UNR + (j + 1))
                pe.wait_ge(xt_ready, i * UNR + max(j - 1, 0))
                for c in range(DC):
                    mm = pe.transpose(ps_t[j % 2][:, c * P:(c + 1) * P], xn[:, j, c * P:(c + 1) * P], k.ident[:, :])
                mm.then_inc(turned, 1)

            def multiply(i, j):
                pe.wait_ge(xt_ready, i * UNR + (j + 1))
                pe.wait_ge(q_ready, i * UNR + max(j - 1, 0))
                for c in range(DC):
                    pe.matmul(ps_kv[j % 2][:, :], xt[:, j, c, :], w[:, c, 0:2, :].rearrange("p a f -> p (a f)"),
                              start=(c == 0), stop=(c == DC - 1))
                for c in range(DC):
                    mm = pe.matmul(ps_q[j % 2][:, 0:D], xt[:, j, c, :], w[:, c, 2, :],
                                   start=(c == 0), stop=(c == DC - 1))
                mm.then_inc(mm_done, 1)

            with pe.Fori(0, WROUNDS) as i:
                turn(i, 0)
                for j in range(1, UNR):
                    turn(i, j)
                    multiply(i, j - 1)
                multiply(i, UNR - 1)


E1, HID1 = 32, 64
SLOTS = WIN + E1 - 1
FR = 4
assert SLOTS % FR == 0


def mix_second(nc, k, a):
    with ExitStack() as ctx:
        def sb(name, shape, dt=F32):
            return ctx.enter_context(nc.sbuf_tensor(name, shape, dt))

        def sem(name):
            return ctx.enter_context(nc.semaphore(name))

        def bank(name):
            return ctx.enter_context(nc.psum_tensor(name, [P, BANK], F32))

        wo = sb("wo", [P, DC, D])
        bo = sb("bo", [P, D])
        gamma = sb("gamma1", [P, D])
        beta = sb("beta1", [P, D])
        rw = sb("rw", [E1, D])
        rwt = sb("rwt", [P, DC, E1])
        val = sb("val", [P, UNR, D])
        xin = sb("xin", [P, UNR, D])
        nz = sb("nz", [P, WIN, H1])
        inv = sb("inv1", [P, UNR, H1])
        mt = sb("mt", [P, UNR, DC, P])
        y = sb("y1", [P, UNR, D])
        xs = sb("xs", [P, UNR, DC, P])
        norm = Norm(ctx, nc, k, "ln4", 0, 2)
        norm2 = Norm(ctx, nc, k, "ln5", 1, 2)
        ps_t = [bank(f"ps4_t{i}") for i in range(2)]
        ps_y = [bank(f"ps4_y{i}") for i in range(2)]
        ps_l = [bank(f"ps4_l{i}") for i in range(2)]
        ps_o = [bank("ps4_o")]

        loaded, all_loaded = k.loads_in, k.expect_loads(6)
        val_in = sem("val_in")
        xin_in = sem("xin_in")
        xin_ready = sem("xin_ready")
        rwt_t = sem("rw_turned")
        rwt_ready = sem("rwt_ready")
        msg = sem("msg1")
        turned = sem("turned4")
        t_used = sem("t4_used")
        mm_done = sem("mm4_done")
        y_done = sem("y1_done")
        normed = sem("normed5")
        l_done = sem("logits_done")
        l_used = sem("logits_used")
        xn_kept = sem("xn5_kept")
        w2_padded = sem("w2_padded")
        block = ctx.enter_context(nc.Block())

        @block.sync
        def _(sp):
            sp.dma_start(rw[:, :], a["L1_ffn_router_w"]).then_inc(loaded, 16)
            sp.dma_start(wo[:, :, :], a["L1_gnn_Wo"].rearrange("(c p) f -> p c f", p=P)).then_inc(loaded, 16)
            for t, name in ((bo, "L1_gnn_bo"), (gamma, "L1_gnn_gamma"), (beta, "L1_gnn_beta"),
                            (k.rb, "L1_ffn_router_b")):
                sp.dma_start(t[:, :], a[name].partition_broadcast(P)).then_inc(loaded, 16)

            def load_val(rows):
                sp.dma_start(val[:, :, :], k.kv_rows[rows, D:2 * D].rearrange("(w p) d -> p w d", p=P)
                             ).then_inc(val_in, 16)

            def load_xin(rows):
                sp.dma_start(xin[:, :, :], k.xin1_rows[rows, :].rearrange("(w p) d -> p w d", p=P)
                             ).then_inc(xin_in, 16)

            load_val(slice(0, RN))
            load_xin(slice(0, RN))
            with sp.Fori(0, WROUNDS - 1) as i:
                rows = bass.ds((i + 1) * RN, RN)
                sp.wait_ge(turned, i * 2 * UNR + UNR)
                load_val(rows)
                sp.wait_ge(y_done, (i + 1) * UNR)
                load_xin(rows)
            sp.wait_ge(val_in, 16 * WROUNDS)
            sp.wait_ge(xin_in, 16 * WROUNDS)

        @block.vector
        def _(v):
            c = k.chain_on(v)
            v.wait_ge(loaded, all_loaded)
            v.wait_ge(rwt_t, 1)
            v.tensor_copy(rwt[:, :, :], ps_o[0][:, 0:DC * E1].rearrange("p (c e) -> p c e", c=DC)
                          ).then_inc(rwt_ready, 1)
            four = [P, UNR, H1, F1]
            for at in (slice(r * UNR, (r + 1) * UNR) for r in range(WROUNDS)):
                acc = k.acc1[:, at, H1:H1 + D].rearrange("p w (h f) -> p w h f", h=H1)
                c.link(v.tensor_scalar(nz[:, at, :], k.acc1[:, at, 0:H1], 0.0, None, ALU.is_equal))
                c.link(v.tensor_tensor(inv[:, :, :], nz[:, at, :], k.acc1[:, at, 0:H1], ALU.add))
                c.link(v.reciprocal(inv[:, :, :], inv[:, :, :]))
                c.link(v.tensor_tensor(acc, acc, inv[:, :, :].unsqueeze(3).to_broadcast(four), ALU.mult))
            with v.Fori(0, WROUNDS) as i:
                c.enter(i, 2 * Norm.LINKS + 5 + UNR, WROUNDS)
                at = bass.ds(i * UNR, UNR)
                vals = val[:, :, :].rearrange("p w (h f) -> p w h f", h=H1)
                v.wait_ge(val_in, (i + 1) * 16)
                c.link(v.tensor_tensor(vals, vals, nz[:, at, :].unsqueeze(3).to_broadcast(four), ALU.mult))
                c.link(v.tensor_tensor(val[:, :, :], val[:, :, :], k.acc1[:, at, H1:H1 + D], ALU.add))
                v.memset(norm.pad[:, :], 0.0).then_inc(msg, 1)
                v.wait_ge(xn_kept, i)
                v.wait_ge(xin_ready, i + 1)
                for j in range(UNR):
                    v.wait_ge(mm_done, i * UNR + (j + 1))
                    v.tensor_tensor(y[:, j, :], ps_y[j % 2][:, 0:D], xin[:, j, :], ALU.add).then_inc(y_done, 1)
                v.wait_ge(y_done, (i + 1) * UNR)
                norm.on_vector(v, c, i, lambda j: y[:, j, :])
                for j in range(UNR):
                    c.inc(norm.apply(v, y[:, j, :], y[:, j, :], j))
                c.wait()
                c.link(v.tensor_tensor(y[:, :, :], y[:, :, :], gamma[:, :].unsqueeze(1).to_broadcast([P, UNR, D]),
                                       ALU.mult))
                c.link(v.tensor_tensor(k.x[:, at, :], k.x[:, at, :], y[:, :, :], ALU.add))
                c.link(v.tensor_tensor(k.x[:, at, :], k.x[:, at, :],
                                       beta[:, :].unsqueeze(1).to_broadcast([P, UNR, D]), ALU.add))
                norm2.on_vector(v, c, i, lambda j: k.x[:, i * UNR + j, :])
                for j in range(UNR):
                    norm2.apply(v, y[:, j, :], k.x[:, i * UNR + j, :], j).then_inc(normed, 1)
                c.leave()

        @block.scalar
        def _(act):
            def take(i, t, dst):
                act.wait_ge(turned, i * 2 * UNR + (t + 1))
                act.copy(dst, ps_t[t % 2][:, 0:D].rearrange("p (c n) -> p c n", c=DC)).then_inc(t_used, 1)

            def take_logits(i, j):
                act.wait_ge(l_done, i * UNR + (j + 1))
                act.copy(k.lg[:, i * UNR + j, :], ps_l[j % 2][:, 0:E1]).then_inc(l_used, 1)

            with act.Fori(0, WROUNDS) as i:
                act.wait_ge(mm_done, i * UNR)
                for j in range(UNR):
                    take(i, j, mt[:, j, :, :])
                norm.on_scalar(act, i, k.eps)
                norm2.on_scalar(act, i, k.eps)
                act.wait_ge(l_done, i * UNR)
                for j in range(UNR):
                    take(i, UNR + j, xs[:, j, :, :])
                    if j:
                        take_logits(i, j - 1)
                take_logits(i, UNR - 1)
            for c in range(DC):
                act.dma_start(k.w1_1[:, c, :, :], a["L1_ffn_W1"][:, c * P:(c + 1) * P, :].rearrange("e p h -> p e h")
                             ).then_inc(k.w_in, 16)
            act.dma_start(k.b1_1[:, :, :].rearrange("p e h -> p (e h)"),
                         a["L1_ffn_b1"].rearrange("e h -> (e h)").partition_broadcast(P)).then_inc(k.w_in, 16)
            act.dma_start(k.w2_1[0:HID1, :, :], a["L1_ffn_W2"].rearrange("e h d -> h e d")).then_inc(k.w_in, 16)
            act.wait_ge(w2_padded, 1)
            act.dma_start(k.w2_1[HID1:HID1 + 1, :, :], a["L1_ffn_b2"].unsqueeze(0)).then_inc(k.w_in, 16)

        @block.gpsimd
        def _(pool):
            pool.memset(k.w2_1[HID1:P, :, :], 0.0).then_inc(w2_padded, 1)
            pool.wait_ge(w2_padded, 1)
            pool.wait_ge(loaded, all_loaded)
            with pool.Fori(0, WROUNDS) as i:
                pool.wait_ge(xin_in, (i + 1) * 16)
                pool.tensor_tensor(xin[:, :, :], xin[:, :, :], bo[:, :].unsqueeze(1).to_broadcast([P, UNR, D]),
                                   ALU.add).then_inc(xin_ready, 1)
                pool.wait_ge(normed, (i + 1) * UNR)
                pool.tensor_copy(k.xn5[:, bass.ds(i * UNR, UNR), :], y[:, :, :]).then_inc(xn_kept, 1)

        @block.tensor
        def _(pe):
            pe.wait_ge(loaded, all_loaded)
            for dc in range(DC):
                mm = pe.transpose(ps_o[0][:, dc * E1:(dc + 1) * E1], rw[:, dc * P:(dc + 1) * P], k.ident[0:E1, 0:E1])
            mm.then_inc(rwt_t, 1)
            pe.wait_ge(rwt_ready, 1)

            def turn(i, t, src):
                pe.wait_ge(t_used, i * 2 * UNR + max(t - 1, 0))
                for c in range(DC):
                    mm = pe.transpose(ps_t[t % 2][:, c * P:(c + 1) * P], src[:, c * P:(c + 1) * P], k.ident[:, :])
                mm.then_inc(turned, 1)

            def multiply(i, j):
                pe.wait_ge(t_used, i * 2 * UNR + (j + 1))
                pe.wait_ge(y_done, i * UNR + max(j - 1, 0))
                for c in range(DC):
                    mm = pe.matmul(ps_y[j % 2][:, 0:D], mt[:, j, c, :], wo[:, c, :], start=(c == 0), stop=(c == DC - 1))
                mm.then_inc(mm_done, 1)

            def logits(i, j):
                pe.wait_ge(t_used, i * 2 * UNR + (UNR + j + 1))
                pe.wait_ge(l_used, i * UNR + max(j - 1, 0))
                for c in range(DC):
                    mm = pe.matmul(ps_l[j % 2][:, 0:E1], xs[:, j, c, :], rwt[:, c, :], start=(c == 0), stop=(c == DC - 1))
                mm.then_inc(l_done, 1)

            with pe.Fori(0, WROUNDS) as i:
                pe.wait_ge(msg, i + 1)
                turn(i, 0, val[:, 0, :])
                for j in range(1, UNR):
                    turn(i, j, val[:, j, :])
                    multiply(i, j - 1)
                multiply(i, UNR - 1)
                for j in range(UNR):
                    pe.wait_ge(normed, i * UNR + (j + 1))
                    turn(i, UNR + j, y[:, j, :])
                    if j:
                        logits(i, j - 1)
                logits(i, UNR - 1)


def place(nc, k, a):
    with ExitStack() as ctx:
        def sb(name, shape, dt=F32):
            return ctx.enter_context(nc.sbuf_tensor("place_" + name, shape, dt))

        def sem(name):
            return ctx.enter_context(nc.semaphore(name))

        before = sb("before", [P, P])
        number = sb("number", [P, E1])
        cell = sb("cell", [P, WIN, E1])
        best = sb("best", [P, WIN])
        hot = sb("hot", [P, WIN, E1])
        count = sb("count", [P, E1, WIN])
        run = sb("run", [P, E1, WIN])
        fresh = sb("fresh", [P, E1, WIN])
        tiles_i = sb("tiles_i", [P, E1], I32)
        tiles = sb("tiles_f", [P, E1])
        until = sb("until", [P, E1])
        slot = sb("slot", [P, WIN])
        tile_no = sb("tile_no", [1, SLOTS])
        past = sb("past", [1, SLOTS, E1])
        who = sb("who", [1, SLOTS])
        ps_b = [ctx.enter_context(nc.psum_tensor(f"ps6_b{i}", [P, BANK], F32)) for i in range(2)]
        ps_c = [ctx.enter_context(nc.psum_tensor(f"ps6_c{i}", [P, BANK], F32)) for i in range(2)]
        HW = BANK // E1

        consts = sem("place_consts")
        counted = sem("counted")
        placed = sem("placed")
        scattered = sem("scattered")
        block = ctx.enter_context(nc.Block())
        marks = {}

        @block.gpsimd
        def _(pool):
            pool.memset(before[:, :], 0.0).then_inc(consts, 1)
            pool.wait_ge(consts, 1)
            pool.iota(tile_no[:, :], pattern=[[1, SLOTS]], base=0, channel_multiplier=0,
                      allow_small_or_imprecise_dtypes=True).then_inc(consts, 1)
            pool.wait_ge(consts, 2)
            pool.affine_select(out=before[:, :], in_=before[:, :], compare_op=ALU.is_ge, fill=1.0,
                               base=0, pattern=[[-1, P]], channel_multiplier=1).then_inc(consts, 1)
            pool.wait_ge(placed, 1)
            for w in range(WIN):
                pool.indirect_dma_start(out=k.sorted_rows[:, :],
                                        out_offset=bass.IndirectOffsetOnAxis(ap=k.slot_of[:, w:w + 1], axis=0),
                                        in_=k.xn5[:, w, :], in_offset=None).then_inc(scattered, 16)
            pool.wait_ge(scattered, 16 * WIN)

        @block.vector
        def _(v):
            c = k.chain_on(v)
            all_w = [P, WIN, E1]
            c.inc(v.tensor_scalar(number[:, :], k.iota_row[:, 0:E1], float(E1), None, ALU.subtract))
            c.inc(v.memset(fresh[:, :, 0:1], 0.0))
            c.inc(v.memset(fresh[:, :, 1:WIN], 1.0))
            numbers = number[:, :].unsqueeze(1).to_broadcast(all_w)
            c.link(v.tensor_tensor(k.lg[:, :, :], k.lg[:, :, :], k.rb[:, :].unsqueeze(1).to_broadcast(all_w), ALU.add))
            c.link(v.tensor_reduce(best[:, :], k.lg[:, :, :], AX_X, ALU.max))
            c.link(v.tensor_tensor(cell[:, :, :], k.lg[:, :, :], best[:, :].unsqueeze(2).to_broadcast(all_w),
                                   ALU.is_equal))
            c.link(v.tensor_tensor(cell[:, :, :], cell[:, :, :], numbers, ALU.mult))
            c.link(v.tensor_reduce(best[:, :], cell[:, :, :], AX_X, ALU.min))
            c.link(v.tensor_tensor(hot[:, :, :], best[:, :].unsqueeze(2).to_broadcast(all_w), numbers, ALU.is_equal))
            marks["hot"] = c.count
            v.wait_ge(counted, 2)
            for half in range(2):
                lo, hi = half * HW, min(WIN, (half + 1) * HW)
                c.inc(v.tensor_copy(count[:, :, lo:hi], ps_c[half][:, 0:(hi - lo) * E1]
                                    .rearrange("p (w e) -> p e w", e=E1)))
            c.wait()
            c.link(v.tensor_tensor_scan(run[:, :, :].rearrange("p e w -> p (e w)"),
                                        fresh[:, :, :].rearrange("p e w -> p (e w)"),
                                        count[:, :, :].rearrange("p e w -> p (e w)"), 0.0, ALU.mult, ALU.add))
            c.link(v.tensor_copy(tiles_i[:, :], run[:, :, WIN - 1]))
            c.link(v.tensor_single_scalar(tiles_i[:, :], tiles_i[:, :], P - 1, ALU.add))
            c.link(v.tensor_single_scalar(tiles_i[:, :], tiles_i[:, :], 7, ALU.arith_shift_right))
            c.link(v.tensor_copy(tiles[:, :], tiles_i[:, :]))
            c.link(v.tensor_tensor_scan(until[:, :], k.ones[:, 0:E1], tiles[:, :], 0.0, ALU.mult, ALU.add))
            c.link(v.tensor_tensor(run[:, :, :], run[:, :, :], count[:, :, :], ALU.subtract))
            c.link(v.tensor_tensor(tiles[:, :], until[:, :], tiles[:, :], ALU.subtract))
            c.link(v.tensor_scalar(tiles[:, :], tiles[:, :], float(P), None, ALU.mult))
            c.link(v.tensor_tensor(run[:, :, :], run[:, :, :], tiles[:, :].unsqueeze(2).to_broadcast([P, E1, WIN]),
                                   ALU.add))
            for half in range(2):
                lo, hi = half * HW, min(WIN, (half + 1) * HW)
                c.inc(v.tensor_tensor(cell[:, lo:hi, :], run[:, :, lo:hi].rearrange("p e w -> p w e"),
                                      ps_b[half][:, 0:(hi - lo) * E1].rearrange("p (w e) -> p w e", e=E1), ALU.add))
            c.wait()
            c.link(v.tensor_tensor(cell[:, :, :], cell[:, :, :], hot[:, :, :], ALU.mult))
            c.link(v.tensor_reduce(slot[:, :], cell[:, :, :], AX_X, ALU.add))
            v.tensor_copy(k.slot_of[:, :], slot[:, :]).then_inc(placed, 1)
            v.wait_ge(consts, 3)
            c.link(v.tensor_tensor(past[:, :, :], tile_no[:, :].unsqueeze(2).to_broadcast([1, SLOTS, E1]),
                                   until[0:1, :].unsqueeze(1).to_broadcast([1, SLOTS, E1]), ALU.is_ge))
            c.link(v.tensor_reduce(who[:, :], past[:, :, :], AX_X, ALU.add))
            c.link(v.tensor_scalar(who[:, :], who[:, :], float(E1 - 1), None, ALU.min))
            c.link(v.tensor_copy(k.expert_of[:, :], who[:, :]))

        @block.tensor
        def _(pe):
            pe.wait_ge(consts, 3)
            pe.wait_ge(k.dve_steps, marks["hot"])
            for lhs, banks in ((k.ones, ps_c), (before, ps_b)):
                for half in range(2):
                    lo, hi = half * HW, min(WIN, (half + 1) * HW)
                    mm = pe.matmul(banks[half][:, 0:(hi - lo) * E1], lhs[:, :],
                                   hot[:, lo:hi, :].rearrange("p w e -> p (w e)"), start=True, stop=True)
                mm.then_inc(counted, 1)


def feed_second(nc, k, a, out):
    with ExitStack() as ctx:
        def sb(name, shape, dt=F32):
            return ctx.enter_context(nc.sbuf_tensor(name, shape, dt))

        def sem(name):
            return ctx.enter_context(nc.semaphore(name))

        def bank(name):
            return ctx.enter_context(nc.psum_tensor(name, [P, BANK], F32))

        tiles, two = range(FR), range(2)
        FROUNDS = SLOTS // FR
        rows = [sb(f"rows5_{t}", [P, D]) for t in tiles]
        xt = [sb(f"xt5_{t}", [P, DC, P]) for t in tiles]
        hid = [sb(f"hid5_{t}", [P, P]) for t in tiles]
        hid_t = [sb(f"hid5_t{t}", [P, P]) for t in tiles]
        y = [sb(f"y5_{t}", [P, D]) for t in tiles]
        back = sb("back5", [P, WIN, D])
        ps_t = [bank(f"ps5_t{i}") for i in two]
        ps_u = [bank(f"ps5_u{i}") for i in two]
        ps_h = [bank(f"ps5_h{i}") for i in two]
        ps_y = [bank(f"ps5_y{i}") for i in two]

        rows_in = [sem(f"rows5_in{t}") for t in tiles]
        hid_set = sem("hid5_set")
        turned = sem("turned5")
        xt_ready = sem("xt5_ready")
        up = sem("up5")
        hid_ready = sem("hid5_ready")
        hid_turned = sem("hid5_turned")
        hid_t_ready = sem("hid5_t_ready")
        down = sem("down5")
        y_ready = sem("y5_ready")
        y_kept = [sem(f"y5_kept{t}") for t in tiles]
        LOT = 2 * UNR
        back_in = [sem(f"back_in{r}") for r in range(-(-WIN // LOT))]
        final = sem("x_final")
        kept = sem("out_kept")
        block = ctx.enter_context(nc.Block())

        def experts(eng, name):
            regs = [eng.alloc_register(f"{name}{t}") for t in tiles]

            def load(i):
                eng.load(regs, k.expert_of[0:1, bass.ds(i * FR, FR)])
                return [eng.snap(r, donate=True, min_val=0, max_val=E1 - 1) for r in regs]
            return load

        @block.gpsimd
        def _(pool):
            for t in tiles:
                for n, (lo, hi, x) in enumerate(((HID1, HID1 + 1, 1.0), (HID1 + 1, P, 0.0))):
                    if t or n:
                        pool.wait_ge(hid_set, 2 * t + n)
                    pool.memset(hid[t][:, lo:hi], x).then_inc(hid_set, 1)
            for t in tiles:
                pool.wait_ge(y_kept[t], 16 * FROUNDS)
            for w in range(WIN):
                pool.indirect_dma_start(out=back[:, w, :], out_offset=None, in_=k.y_rows[:, :],
                                        in_offset=bass.IndirectOffsetOnAxis(ap=k.slot_of[:, w:w + 1], axis=0)
                                        ).then_inc(back_in[w // LOT], 16)

        @block.sync
        def _(sp):
            def load(i, t):
                if not isinstance(i, int) or i:
                    sp.wait_ge(turned, (i - 1) * FR + (t + 1))
                sp.dma_start(rows[t][:, :], k.sorted_rows[bass.ds((i * FR + t) * P, P), :]).then_inc(rows_in[t], 16)

            def store(i, t):
                sp.wait_ge(y_ready, i * FR + (t + 1))
                sp.dma_start(k.y_rows[bass.ds((i * FR + t) * P, P), :], y[t][:, :]).then_inc(y_kept[t], 16)

            for i in range(2):
                for t in tiles:
                    load(i, t)
            with sp.Fori(0, FROUNDS - 2) as i:
                for t in tiles:
                    load(i + 2, t)
                for t in tiles:
                    store(i, t)
            for i in range(FROUNDS - 2, FROUNDS):
                for t in tiles:
                    store(i, t)
            for r in range(WROUNDS):
                sp.wait_ge(final, r + 1)
                lo, hi = r * UNR, min((r + 1) * UNR, WIN - 1)
                sp.dma_start(out[lo * P:hi * P, :].rearrange("(w p) d -> p w d", p=P), k.x[:, lo:hi, :]
                             ).then_inc(kept, 16)
            sp.dma_start(out[(WIN - 1) * P:N, :], k.x[0:LAST, WIN - 1, :]).then_inc(kept, 16)
            sp.wait_ge(kept, 16 * (WROUNDS + 1))

        @block.vector
        def _(v):
            load = experts(v, "dve_expert")
            v.wait_ge(hid_set, 2 * FR)
            v.wait_ge(k.w_in, 16 * (QKV_LOADS + DC + 3))
            with v.Fori(0, FROUNDS) as i:
                e = load(i)
                for t in tiles:
                    n = i * FR + t
                    v.wait_ge(up, n + 1)
                    v.tensor_tensor(hid[t][:, 0:HID1], ps_u[t % 2][:, 0:HID1], k.b1_1[:, e[t], :], ALU.add
                                    ).then_inc(hid_ready, 1)
                for t in tiles:
                    n = i * FR + t
                    v.wait_ge(down, n + 1)
                    v.wait_ge(y_kept[t], i * 16)
                    v.tensor_copy(y[t][:, :], ps_y[t % 2][:, 0:D]).then_inc(y_ready, 1)
            for r in range(WROUNDS):
                at = slice(r * UNR, (r + 1) * UNR)
                v.wait_ge(back_in[at.start // LOT], 16 * (min(WIN, (at.start // LOT + 1) * LOT) - at.start // LOT * LOT))
                v.scalar_tensor_tensor(out=k.x[:, at, :], in0=back[:, at, :], scalar=0.0, in1=k.x[:, at, :],
                                       op0=ALU.max, op1=ALU.add).then_inc(final, 1)

        @block.scalar
        def _(act):
            def take_rows(i, t):
                act.wait_ge(turned, i * FR + (t + 1))
                act.wait_ge(up, i * FR)
                act.copy(xt[t][:, :, :], ps_t[t % 2][:, 0:D].rearrange("p (c n) -> p c n", c=DC)
                         ).then_inc(xt_ready, 1)

            def take_hidden(i, t):
                act.wait_ge(hid_turned, i * FR + (t + 1))
                act.wait_ge(down, i * FR)
                act.activation(hid_t[t][:, :], ps_h[t % 2][:, 0:P], ACT.Relu).then_inc(hid_t_ready, 1)

            for t in tiles:
                take_rows(0, t)
            with act.Fori(0, FROUNDS - 1) as i:
                for t in tiles:
                    take_rows(i + 1, t)
                    take_hidden(i, t)
            for t in tiles:
                take_hidden(FROUNDS - 1, t)

        @block.tensor
        def _(pe):
            load = experts(pe, "pe_expert")
            pe.wait_ge(k.w_in, 16 * (QKV_LOADS + DC + 3))
            def turn(i, t):
                pe.wait_ge(rows_in[t], (i + 1) * 16)
                if t or not isinstance(i, int):
                    pe.wait_ge(xt_ready, i * FR + max(t - 1, 0))
                for c in range(DC):
                    mm = pe.transpose(ps_t[t % 2][:, c * P:(c + 1) * P], rows[t][:, c * P:(c + 1) * P],
                                      k.ident[:, :])
                mm.then_inc(turned, 1)

            def finish(i, e, last):
                for t in tiles:
                    pe.wait_ge(xt_ready, i * FR + (t + 1))
                    pe.wait_ge(hid_ready, i * FR + max(t - 1, 0))
                    for c in range(DC):
                        mm = pe.matmul(ps_u[t % 2][:, 0:HID1], xt[t][:, c, :], k.w1_1[:, c, e[t], :],
                                       start=(c == 0), stop=(c == DC - 1))
                    mm.then_inc(up, 1)
                for t in tiles:
                    if not last:
                        turn(i + 1, t)
                    pe.wait_ge(hid_ready, i * FR + (t + 1))
                    pe.wait_ge(hid_t_ready, i * FR + max(t - 1, 0))
                    pe.transpose(ps_h[t % 2][:, 0:P], hid[t][:, :], k.ident[:, :]).then_inc(hid_turned, 1)
                for t in tiles:
                    pe.wait_ge(hid_t_ready, i * FR + (t + 1))
                    pe.wait_ge(y_ready, i * FR + max(t - 1, 0))
                    pe.matmul(ps_y[t % 2][:, 0:D], hid_t[t][:, :], k.w2_1[:, e[t], :], start=True, stop=True
                              ).then_inc(down, 1)

            for t in tiles:
                turn(0, t)
            with pe.Fori(0, FROUNDS - 1) as i:
                finish(i, load(i), False)
            finish(FROUNDS - 1, load(FROUNDS - 1), True)


def build(nc, a, out):
    k = Kernel()
    with ExitStack() as ctx:
        def sb(on, name, shape, dt=F32):
            return on.enter_context(nc.sbuf_tensor(name, shape, dt))

        allocate(ctx, nc, k)
        k.w_in = ctx.enter_context(nc.semaphore("w_in"))
        k.acc1 = sb(ctx, "acc1", [P, WIN, H1 + D])
        flat = k.acc1[:, :, :].rearrange("p w r -> p (w r)")
        lo, mid, hi = DC * 3 * D, (DC + 1) * 3 * D, (DC + 1) * 3 * D + DC
        k.wqkv = flat[:, 0:lo].rearrange("p (c j f) -> p c j f", c=DC, j=3)
        k.bqkv = flat[:, lo:mid].rearrange("p (j f) -> p j f", j=3)
        k.q01 = flat[:, mid:hi]
        k.relw = flat[0:F1, hi:hi + F1]
        steps_of_edges(nc, k, a)
        with ExitStack() as stage:
            k.by_dst = sb(stage, "ad0", [P, WIN, 3, H0], BF16)
            project_first(nc, k, a)
            k.acc0 = sb(stage, "acc0", [P, WIN, R0])
            with ExitStack() as inner:
                edges(nc, k, FIRST, inner, k.acc0)
            feed_forward_tensors(stage, nc, k)
            mix_first(nc, k, a)
            route_first(nc, k, a)
            feed_first(nc, k, a)
        with ExitStack() as stage:
            with ExitStack() as inner:
                k.q3 = sb(inner, "q3", [P, WIN, 3, D], BF16)
                k.rel3 = sb(inner, "rel3", [F1, 3, F1], BF16)
                k.by_dst, k.by_typ = k.q3, k.rel3
                project_second(nc, k, a)
                edges(nc, k, SECOND, inner, k.acc1)
            k.xn5 = sb(stage, "xn5", [P, WIN, D])
            k.lg = sb(stage, "logits", [P, WIN, E1])
            k.slot_of = sb(stage, "slot_of", [P, WIN], I32)
            k.expert_of = sb(stage, "expert_of", [1, SLOTS], I32)
            k.w1_1 = sb(stage, "w1_1", [P, DC, E1, HID1])
            k.b1_1 = sb(stage, "b1_1", [P, E1, HID1])
            k.w2_1 = sb(stage, "w2_1", [P, E1, D])
            k.rb = sb(stage, "rb", [P, E1])
            mix_second(nc, k, a)
            place(nc, k, a)
            feed_second(nc, k, a, out)


_INS = ['x', 'src', 'dst', 'edge_type_64', 'L0_gnn_W', 'L0_gnn_a_src', 'L0_gnn_a_dst', 'L0_gnn_bias',
        'L0_ffn_Wr', 'L0_ffn_br', 'L0_ffn_W1', 'L0_ffn_b1', 'L0_ffn_W2', 'L0_ffn_b2', 'L0_ffn_gamma',
        'L0_ffn_beta', 'L1_gnn_query_emb', 'L1_gnn_Wq', 'L1_gnn_bq', 'L1_gnn_Wk', 'L1_gnn_bk', 'L1_gnn_Wv',
        'L1_gnn_bv', 'L1_gnn_rel_w', 'L1_gnn_Wo', 'L1_gnn_bo', 'L1_gnn_gamma', 'L1_gnn_beta',
        'L1_ffn_router_w', 'L1_ffn_router_b', 'L1_ffn_W1', 'L1_ffn_b1', 'L1_ffn_W2', 'L1_ffn_b2']


def kernel(**inputs):
    import numpy as _np
    import concourse.bacc as _bacc
    from concourse import mybir as _mybir
    from concourse.bass_utils import run_bass_kernel_spmd as _run

    nc = _bacc.Bacc("TRN2", target_bir_lowering=False, num_devices=1)
    arrays, args = {}, {}
    for name in _INS:
        a = _np.ascontiguousarray(inputs[name])
        arrays[f"in_{name}"] = a
        args[name] = nc.dram_tensor(f"in_{name}", a.shape, _mybir.dt.from_np(a.dtype), kind="ExternalInput").ap()
    out = nc.dram_tensor("out_0", (N, D), F32, kind="ExternalOutput").ap()
    build(nc, args, out)
    r = _run(nc, [arrays], core_ids=[0])
    return r.results[0]["out_0"]
```

```python
from contextlib import ExitStack

import numpy as np

import concourse.bass as bass
from concourse import mybir

F32 = mybir.dt.float32
BF16 = mybir.dt.bfloat16
I32 = mybir.dt.int32
U32 = mybir.dt.uint32
ALU = mybir.AluOpType
ACT = mybir.ActivationFunctionType
AX_X = mybir.AxisListType.X

P = 128
N = 3125
E = 50000
D = 256
DC = D // P
WIN = -(-N // P)
NPAD = WIN * P
LAST = N - (WIN - 1) * P
TILES = -(-E // P)
TROWS = TILES + 1
TC = 4
TP = TROWS // TC
BATCH = 16
STEPS = -(-(TILES + WIN - 1) // (2 * BATCH)) * 2 * BATCH
SC = 4
SP = STEPS // SC
NEG = -1e30
BANK = 512
UNR = 5
WROUNDS = WIN // UNR
EPS = 1e-5
assert TP * TC == TROWS and SP * SC == STEPS and TP <= P and SP <= P and UNR * WROUNDS == WIN

H0, F0 = 8, 32
R0 = D + H0
H1, F1 = 4, 64
R1 = 2 * D


X_LOADS = 2
QKV_LOADS = X_LOADS + 10


class Chain:

    def __init__(self, eng, sem, count=0):
        self.eng, self.sem, self.count, self.at = eng, sem, count, None

    def enter(self, i, per, trips, first=0):
        self.entered, self.per, self.trips = self.count, per, trips
        self.at = None if isinstance(i, int) else self.count + (i * per if not first else i * per - first * per)

    def leave(self):
        assert self.count - self.entered == self.per, (self.sem, self.count - self.entered, self.per)
        if self.at is not None:
            self.count, self.at = self.entered + self.per * self.trips, None

    def value(self):
        return self.count if self.at is None else self.at + (self.count - self.entered)

    def inc(self, ins):
        ins.then_inc(self.sem, 1)
        self.count += 1

    def wait(self):
        self.eng.wait_ge(self.sem, self.value())

    def link(self, ins):
        self.inc(ins)
        self.wait()


def rounds(eng, n, trip):
    trip(0)
    with eng.Fori(1, n) as i:
        trip(i)


def wait(eng, sem, value):
    if not isinstance(value, int) or value > 0:
        eng.wait_ge(sem, value)


class Kernel:

    chain = None
    loads = 0

    def expect_loads(self, n):
        self.loads += n
        return 16 * self.loads

    def chain_on(self, v):
        self.chain = Chain(v, self.dve_steps, self.chain.count if self.chain else 0)
        return self.chain


def allocate(ctx, nc, k):
    def dram(name, shape, dt):
        return nc.dram_tensor(name, shape, dt).ap()

    def sb(name, shape, dt=F32):
        return ctx.enter_context(nc.sbuf_tensor(name, shape, dt))

    k.dve_steps = ctx.enter_context(nc.semaphore("dve_steps"))
    k.ln_var = ctx.enter_context(nc.semaphore("ln_var"))
    k.ln_std = ctx.enter_context(nc.semaphore("ln_std"))
    k.ln_rounds = 0
    k.loads_in = ctx.enter_context(nc.semaphore("loads_in"))
    k.edge_rows = dram("edge_rows", [TROWS, 3 * P], I32)
    k.step_rel = dram("step_rel", [STEPS + BATCH, P], BF16)
    k.step_typ = dram("step_typ", [STEPS + BATCH, P], BF16)
    k.step_cut8 = dram("step_cut8", [STEPS, H0, P + 4], F32)
    k.step_cut4 = dram("step_cut4", [STEPS, H1, P + 4], F32)
    k.step_ends = dram("step_ends", [2, STEPS], F32)
    k.step_win = dram("step_win", [1, STEPS], I32)
    k.h_rows = dram("h_rows", [NPAD, R0], F32)
    k.kv_rows = dram("kv_rows", [NPAD, R1], F32)
    k.xin1_rows = dram("xin1_rows", [NPAD, D], F32)

    slots = WIN + 31
    k.sorted_rows = dram("sorted_rows", [slots * P, D], F32)
    k.y_rows = dram("y_rows", [slots * P, D], F32)

    k.ident = sb("ident", [P, P])
    k.iota_row = sb("iota_row", [P, P])
    k.iota_col = sb("iota_col", [P, 1])
    k.ones = sb("ones", [P, P])
    k.eps = sb("eps", [P, 1])
    k.x = sb("x", [P, WIN, D])
    k.rel_col = sb("rel_col", [P, STEPS])
    k.src_col = sb("src_col", [P, STEPS], I32)
    k.win_row = sb("win_row", [1, STEPS + BATCH], I32)
    k.joined = sb("joined", [8, 3, STEPS + BATCH])
    k.hsel8 = sb("hsel8", [P, H0])
    k.hselT8 = sb("hselT8", [H0, P])
    k.mask8 = sb("mask8", [P, BATCH])
    k.hsel4 = sb("hsel4", [P, H1])
    k.hselT4 = sb("hselT4", [H1, P // 2])
    k.mask4 = sb("mask4", [P // 2, BATCH])


def steps_of_edges(nc, k, a):
    with ExitStack() as ctx:
        def sb(name, shape, dt=F32):
            return ctx.enter_context(nc.sbuf_tensor(name, shape, dt))

        def sem(name):
            return ctx.enter_context(nc.semaphore(name))

        tiles = sb("tiles", [TP, TC, 3, P], I32)
        ends_i = sb("ends_i", [TP, 2, TC], I32)
        ends_w = sb("ends_w", [TP, 2, TC])
        count = sb("count", [TP, TC])
        last_of = sb("last_of", [TP, TC])
        tril = sb("tril", [TP, TP])
        base = sb("base", [TP, TC])
        tot = sb("tot", [TP, TC])
        tile_g = sb("tile_g", [TP, TC, 2])
        iota_s = sb("iota_s", [TP, STEPS])
        hit = sb("hit", [TP, TC, STEPS])
        hit2 = sb("hit2", [TP, STEPS])
        step_no = sb("step_no", [SP, SC])
        tile_i = sb("tile_i", [SP, SC], I32)
        win_f = sb("win_f", [SP, SC])
        win_i = sb("win_i", [SP, SC], I32)
        win_x = sb("win_x", [SP, SC])
        rows = sb("rows", [SP, SC, 3, P], I32)
        rows_f = sb("rows_f", [SP, SC, 3, P])
        rel = sb("rel", [SP, SC, P])
        rel_b = sb("rel_b", [SP, SC, P], BF16)
        typ_b = sb("typ_b", [SP, SC, P], BF16)
        cut = sb("cut", [SP, SC, P + 4])
        ends_f = sb("ends_f", [SP, 2, SC])
        ends_r = sb("ends_r", [8, 2, STEPS])
        single = sb("single", [8, STEPS])
        ps_a = ctx.enter_context(nc.psum_tensor("ps_a", [P, 512], F32))
        ps_b = ctx.enter_context(nc.psum_tensor("ps_b", [P, 512], F32))
        ps_c = ctx.enter_context(nc.psum_tensor("ps_c", [P, 512], F32))

        ready = sem("pool_consts")
        pads = sem("tile_pads")
        loaded, all_loaded = k.loads_in, k.expect_loads(9)
        kept = sem("edges_kept")
        pe_done = sem("prep_pe")
        tile_ready = sem("tile_ready")
        gathered = sem("rows_gathered")
        stored = sem("prep_stored")
        reread = sem("ends_reread")
        block = ctx.enter_context(nc.Block())
        marks = {}

        FULL = E // P
        CL = TC - 1
        assert (FULL == CL * TP + TP - 2) and TP - 2 == 96

        @block.gpsimd
        def _(pool):
            pool.memset(tiles[96:TP, CL, 0, :], 4000).then_inc(pads, 1)
            pool.memset(tiles[96:TP, CL, 1:3, :], 0).then_inc(pads, 1)
            pool.wait_ge(pads, 2)
            pool.memset(tiles[96:97, CL, 0, :], NPAD - 1).then_inc(pads, 1)
            pool.wait_ge(pads, 3)
            pool.memset(k.x[:, WIN - 1, :], 0.0).then_inc(pads, 1)
            pool.wait_ge(pads, 4)
            c = Chain(pool, ready)
            pool.memset(k.win_row[:, STEPS:STEPS + BATCH], 0)
            pool.memset(k.ident[:, :], 0.0).then_inc(ready, 1)
            pool.memset(tril[:, :], 0.0).then_inc(ready, 1)
            pool.memset(k.ones[:, :], 1.0).then_inc(ready, 1)
            pool.memset(k.hsel8[:, :], 0.0).then_inc(ready, 1)
            pool.memset(k.hselT8[:, :], 0.0).then_inc(ready, 1)
            pool.memset(k.mask8[:, :], 1.0).then_inc(ready, 1)
            pool.memset(k.hsel4[:, :], 0.0).then_inc(ready, 1)
            pool.memset(k.hselT4[:, :], 0.0).then_inc(ready, 1)
            pool.memset(k.mask4[:, :], 1.0).then_inc(ready, 1)
            pool.memset(k.eps[:, :], EPS).then_inc(ready, 1)
            c.count = 10
            c.wait()
            pool.affine_select(out=k.ident[:, :], in_=k.ident[:, :], compare_op=ALU.not_equal, fill=1.0,
                               base=0, pattern=[[-1, P]], channel_multiplier=1).then_inc(ready, 1)
            pool.affine_select(out=tril[:, :], in_=tril[:, :], compare_op=ALU.is_ge, fill=1.0,
                               base=0, pattern=[[-1, TP]], channel_multiplier=1).then_inc(ready, 1)
            pool.iota(k.iota_row[:, :], pattern=[[1, P]], base=0, channel_multiplier=0,
                      allow_small_or_imprecise_dtypes=True).then_inc(ready, 1)
            pool.iota(k.iota_col[:, :], pattern=[[1, 1]], base=0, channel_multiplier=1,
                      allow_small_or_imprecise_dtypes=True).then_inc(ready, 1)
            pool.iota(iota_s[:, :], pattern=[[1, STEPS]], base=0, channel_multiplier=0,
                      allow_small_or_imprecise_dtypes=True).then_inc(ready, 1)
            pool.iota(step_no[:, :], pattern=[[SP, SC]], base=0, channel_multiplier=1,
                      allow_small_or_imprecise_dtypes=True).then_inc(ready, 1)
            pool.iota(tile_g[:, :, 0], pattern=[[TP, TC]], base=0, channel_multiplier=1,
                      allow_small_or_imprecise_dtypes=True).then_inc(ready, 1)
            c.count = 17
            for hsel, hselT, mask, H in ((k.hsel8, k.hselT8, k.mask8, H0), (k.hsel4, k.hselT4, k.mask4, H1)):
                c.wait()
                v = hselT[:, :].rearrange("h (s g) -> h s g", g=H)
                c.link(pool.affine_select(out=v, in_=v, compare_op=ALU.not_equal, fill=1.0, base=0,
                                          pattern=[[0, BATCH], [-1, H]], channel_multiplier=1))
                c.link(pool.affine_select(out=mask[:, :], in_=mask[:, :], compare_op=ALU.is_ge, fill=0.0,
                                          base=0, pattern=[[-H, BATCH]], channel_multiplier=1))
                c.link(pool.affine_select(out=mask[:, :], in_=mask[:, :], compare_op=ALU.is_ge, fill=0.0,
                                          base=H - 1, pattern=[[H, BATCH]], channel_multiplier=-1))
            marks["consts"] = c.count
            pool.wait_ge(kept, 16)
            pool.wait_ge(tile_ready, 1)
            for c4 in range(SC):
                pool.indirect_dma_start(out=rows[:, c4, :, :].rearrange("p a e -> p (a e)"), out_offset=None,
                                        in_=k.edge_rows[:, :],
                                        in_offset=bass.IndirectOffsetOnAxis(ap=tile_i[:, c4:c4 + 1], axis=0)
                                        ).then_inc(gathered, 16)

        @block.vector
        def _(v):
            c = k.chain_on(v)
            v.wait_ge(loaded, all_loaded)
            v.wait_ge(ready, marks["consts"])
            c.inc(v.tensor_single_scalar(ends_i[:, 0, :], tiles[:, :, 0, 0], 7, ALU.arith_shift_right))
            c.link(v.tensor_single_scalar(ends_i[:, 1, :], tiles[:, :, 0, P - 1], 7, ALU.arith_shift_right))
            c.link(v.tensor_copy(ends_w[:, :, :], ends_i[:, :, :]))
            c.link(v.scalar_tensor_tensor(out=count[:, :], in0=ends_w[:, 1, :], scalar=1.0,
                                          in1=ends_w[:, 0, :], op0=ALU.add, op1=ALU.subtract))
            marks["count"] = c.count
            v.wait_ge(pe_done, 1)
            c.link(v.tensor_copy(tot[:, :], ps_a[0:TP, 8:8 + TC]))
            c.link(v.tensor_copy(base[:, :], ps_a[0:TP, 0:TC]))
            for j in range(1, TC):
                c.link(v.tensor_tensor(base[:, j:TC], base[:, j:TC],
                                       tot[:, j - 1:j].to_broadcast([TP, TC - j]), ALU.add))
            c.link(v.tensor_tensor(last_of[:, :], base[:, :], count[:, :], ALU.add))
            c.link(v.tensor_tensor(tile_g[:, :, 1], ends_w[:, 0, :], base[:, :], ALU.subtract))
            for j in range(TC):
                if j == TC - 1:
                    c.link(v.tensor_scalar(tot[:, j:j + 1], ends_w[:, 0, j:j + 1], float(WIN), None, ALU.is_gt))
                    c.link(v.scalar_tensor_tensor(out=last_of[:, j:j + 1], in0=tot[:, j:j + 1],
                                                  scalar=float(STEPS), in1=last_of[:, j:j + 1],
                                                  op0=ALU.mult, op1=ALU.add))
                c.link(v.tensor_scalar(hit2[:, :], iota_s[:, :], last_of[:, j:j + 1], None, ALU.is_ge))
                c.link(v.scalar_tensor_tensor(out=hit[:, j, :], in0=iota_s[:, :], scalar=base[:, j:j + 1],
                                              in1=hit2[:, :], op0=ALU.is_ge, op1=ALU.subtract))
            marks["hit"] = c.count
            v.wait_ge(pe_done, 2)
            pv = ps_b[0:SP, 0:2 * SC].rearrange("p (c j) -> p c j", j=2)
            v.tensor_copy(tile_i[:, :], pv[:, :, 0]).then_inc(tile_ready, 1)
            c.link(v.tensor_tensor(win_f[:, :], step_no[:, :], pv[:, :, 1], ALU.add))
            c.link(v.tensor_scalar(win_f[:, :], win_f[:, :], float(WIN - 1), None, ALU.min))
            c.link(v.tensor_copy(win_i[:, :], win_f[:, :]))
            c.link(v.tensor_scalar(win_x[:, :], win_f[:, :], float(P), None, ALU.mult))
            v.wait_ge(pe_done, 3)
            c.inc(v.tensor_copy(k.hsel8[:, :], ps_c[:, 0:H0]))
            c.inc(v.tensor_copy(k.hsel4[0:P // 2, :], ps_c[0:P // 2, 16:16 + H1]))
            v.wait_ge(gathered, 16 * SC)
            c.link(v.tensor_copy(rows_f[:, :, :, :], rows[:, :, :, :]))
            c.inc(v.tensor_copy(ends_f[:, 0, :], rows_f[:, :, 0, 0]))
            c.inc(v.tensor_copy(ends_f[:, 1, :], rows_f[:, :, 0, P - 1]))
            marks["ends"] = c.count
            for j in range(SC):
                c.inc(v.tensor_scalar(rel[:, j, :], rows_f[:, j, 0, :], win_x[:, j:j + 1], None, ALU.subtract))
            c.wait()
            marks["rows"] = c.count
            c.inc(v.tensor_copy(rel_b[:, :, :], rel[:, :, :]))
            c.inc(v.tensor_copy(typ_b[:, :, :], rows_f[:, :, 2, :]))
            c.link(v.memset(cut[:, :, :], 0.0))
            c.link(v.tensor_tensor(cut[:, :, 1:P], rows_f[:, :, 0, 1:P], rows_f[:, :, 0, 0:P - 1], ALU.not_equal))
            c.link(v.tensor_scalar(cut[:, :, 1:P], cut[:, :, 1:P], NEG, None, ALU.mult))
            marks["stores"] = c.count
            v.wait_ge(pe_done, 4)
            c.inc(v.tensor_copy(k.rel_col[:, :], ps_a[:, 0:STEPS]))
            c.inc(v.tensor_copy(k.src_col[:, :], ps_b[:, 0:STEPS]))
            v.wait_ge(reread, 32)
            c.link(v.memset(k.joined[:, :, :], 1.0))
            c.link(v.tensor_tensor(k.joined[:, 0, 1:STEPS], ends_r[:, 0, 1:STEPS], ends_r[:, 1, 0:STEPS - 1],
                                   ALU.not_equal))
            c.link(v.tensor_tensor(single[:, :], ends_r[:, 0, :], ends_r[:, 1, :], ALU.not_equal))
            c.inc(v.tensor_tensor(k.joined[:, 1, 0:STEPS], k.joined[:, 0, 0:STEPS], single[:, :], ALU.max))
            c.link(v.tensor_tensor(k.joined[:, 2, 0:STEPS - 1], k.joined[:, 0, 1:STEPS], single[:, 0:STEPS - 1],
                                   ALU.max))
            c.link(v.tensor_scalar(k.joined[:, :, :], k.joined[:, :, :], NEG, None, ALU.mult))

        @block.tensor
        def _(pe):
            pe.wait_ge(ready, marks["consts"])
            pe.wait_ge(k.dve_steps, marks["count"])
            pe.matmul(ps_a[0:TP, 0:TC], tril[:, :], count[:, :], start=True, stop=True)
            pe.matmul(ps_a[0:TP, 8:8 + TC], k.ones[0:TP, 0:TP], count[:, :], start=True, stop=True
                      ).then_inc(pe_done, 1)
            pe.wait_ge(k.dve_steps, marks["hit"])
            for sc in range(SC):
                for c in range(TC):
                    mm = pe.matmul(ps_b[0:SP, 2 * sc:2 * sc + 2], hit[:, c, sc * SP:(sc + 1) * SP],
                                   tile_g[:, c, :], start=(c == 0), stop=(c == TC - 1))
            mm.then_inc(pe_done, 1)
            pe.transpose(ps_c[:, 0:H0], k.hselT8[:, :], k.ident[0:H0, 0:H0])
            pe.transpose(ps_c[0:P // 2, 16:16 + H1], k.hselT4[:, :], k.ident[0:H1, 0:H1]).then_inc(pe_done, 1)
            pe.wait_ge(k.dve_steps, marks["rows"])
            for sc in range(SC):
                pe.transpose(ps_a[:, sc * SP:(sc + 1) * SP], rel[:, sc, :], k.ident[0:SP, 0:SP])
            for sc in range(SC):
                mm = pe.transpose(ps_b[:, sc * SP:(sc + 1) * SP], rows_f[:, sc, 1, :], k.ident[0:SP, 0:SP])
            mm.then_inc(pe_done, 1)

        @block.sync
        def _(sp):
            for j, name in enumerate(("dst", "src", "edge_type_64")):
                v = a[name]
                sp.dma_start(tiles[:, 0:CL, j, :],
                             v[0:CL * TP * P].rearrange("(c p e) -> p c e", c=CL, e=P)).then_inc(loaded, 16)
                sp.dma_start(tiles[0:96, CL, j, :],
                             v[CL * TP * P:FULL * P].rearrange("(p e) -> p e", e=P)).then_inc(loaded, 16)
            sp.wait_ge(pads, 3)
            for j, name in enumerate(("dst", "src", "edge_type_64")):
                sp.dma_start(tiles[96:97, CL, j, 0:E - FULL * P],
                             a[name][FULL * P:E].rearrange("(p e) -> p e", p=1)).then_inc(loaded, 16)
            sp.dma_start(k.x[:, 0:WIN - 1, :], a["x"][0:(WIN - 1) * P, :].rearrange("(w p) d -> p w d", p=P)
                         ).then_inc(k.w_in, 16)
            sp.wait_ge(pads, 4)
            sp.dma_start(k.x[0:LAST, WIN - 1, :], a["x"][(WIN - 1) * P:N, :]).then_inc(k.w_in, 16)
            sp.wait_ge(loaded, all_loaded)
            sp.dma_start(k.edge_rows[:, :].rearrange("(c p) (j e) -> p c j e", p=TP, e=P),
                         tiles[:, :, :, :]).then_inc(kept, 16)
            sp.wait_ge(k.dve_steps, marks["ends"])
            for j in range(2):
                for c4 in range(SC):
                    sp.dma_start(k.step_ends[j:j + 1, c4 * SP:(c4 + 1) * SP].rearrange("o p -> p o"),
                                 ends_f[:, j, c4:c4 + 1]).then_inc(stored, 16)
            for c4 in range(SC):
                sp.dma_start(k.step_win[0:1, c4 * SP:(c4 + 1) * SP].rearrange("o p -> p o"),
                             win_i[:, c4:c4 + 1]).then_inc(stored, 16)
            sp.wait_ge(stored, 12 * 16)
            sp.dma_start(ends_r[:, :, :].rearrange("p j s -> p (j s)"),
                         k.step_ends[:, :].rearrange("j s -> (j s)").partition_broadcast(8)
                         ).then_inc(reread, 16)
            sp.dma_start(k.win_row[:, 0:STEPS], k.step_win[:, :]).then_inc(reread, 16)
            sp.wait_ge(k.dve_steps, marks["stores"])
            for dst, of in ((k.step_rel, rel_b), (k.step_typ, typ_b)):
                sp.dma_start(dst[0:STEPS, :].rearrange("(c p) e -> p c e", p=SP), of[:, :, :]).then_inc(stored, 16)
                sp.dma_start(dst[STEPS:STEPS + BATCH, :], of[0:BATCH, 0, :]).then_inc(stored, 16)
            for H, dst in ((H0, k.step_cut8), (H1, k.step_cut4)):
                for c4 in range(SC):
                    sp.dma_start(dst[c4 * SP:(c4 + 1) * SP, :, :],
                                 cut[:, c4, :].unsqueeze(1).to_broadcast([SP, H, P + 4])).then_inc(stored, 16)
            sp.wait_ge(stored, 24 * 16)
            sp.wait_ge(reread, 32)


LOTS = ((0, 3), (3, UNR))


def lot_of(j):
    return [n for n, (lo, hi) in enumerate(LOTS) if lo <= j < hi][0]


class Norm:

    def __init__(self, ctx, nc, k, name, turn=0, turns=1):
        self.stats = ctx.enter_context(nc.sbuf_tensor(name + "_stats", [P, UNR, 6], F32))
        self.mv = ctx.enter_context(nc.sbuf_tensor(name + "_mv", [P, UNR, 2], F32))
        self.std = ctx.enter_context(nc.sbuf_tensor(name + "_std", [P, UNR], F32))
        self.rstd = ctx.enter_context(nc.sbuf_tensor(name + "_rstd", [P, UNR], F32))
        self.var_ready, self.std_ready = k.ln_var, k.ln_std
        self.before, self.turns = k.ln_rounds + turn + 1, turns
        if turn == turns - 1:
            k.ln_rounds += turns * WROUNDS
        self.pad = ctx.enter_context(nc.sbuf_tensor(name + "_pad", [P, 1], F32))

    LINKS = 2 * UNR + 2

    def on_vector(self, v, c, i, x_of):
        c.inc(v.memset(self.pad[:, :], 0.0))
        for j in range(UNR):
            c.inc(v.bn_stats(self.stats[:, j, :], x_of(j)))
        c.wait()
        c.inc(v.memset(self.pad[:, :], 0.0))
        for j in range(UNR):
            ins = v.bn_aggr(self.mv[:, j, :], self.stats[:, j, :])
            if j < UNR - 1:
                c.inc(ins)
        ins.then_inc(self.var_ready, 1)
        wait(v, self.std_ready, i * self.turns + self.before)
        c.link(v.reciprocal(self.rstd[:, :], self.std[:, :]))

    def on_scalar(self, act, i, eps):
        wait(act, self.var_ready, i * self.turns + self.before)
        act.activation(self.std[:, :], self.mv[:, :, 1], ACT.Sqrt, bias=eps[:, 0:1]).then_inc(self.std_ready, 1)

    def apply(self, v, out, x, j):
        return v.tensor_scalar(out, x, self.mv[:, j, 0:1], self.rstd[:, j:j + 1], ALU.subtract, ALU.mult)


def project_first(nc, k, a):
    with ExitStack() as ctx:
        def sb(name, shape, dt=F32):
            return ctx.enter_context(nc.sbuf_tensor(name, shape, dt))

        def ps(name, shape):
            return ctx.enter_context(nc.psum_tensor(name, shape, F32))

        def sem(name):
            return ctx.enter_context(nc.semaphore(name))

        RW = D + 2 * H0
        w = sb("w0", [P, DC, D])
        a_col = sb("a0_col", [P, 2, DC])
        amask = sb("amask", [P, DC, H0])
        ablk = sb("ablk", [P, DC, 2, H0])
        wx = sb("wx0", [P, DC, RW])
        ad = sb("ad0f", [P, WIN, H0])
        ad_r = sb("ad0r", [P, WIN, H0])
        xn = sb("xn0", [P, UNR, D])
        xt = sb("xt0", [P, UNR, DC, P])
        h = sb("h0", [P, UNR, RW])
        norm = Norm(ctx, nc, k, "ln0")
        ps_t = [ps(f"ps0_t{i}", [P, DC, P]) for i in range(2)]
        ps_h = [ps(f"ps0_h{i}", [P, RW]) for i in range(2)]
        ps_w = ps("ps0_w", [P, 2, D])
        ps_a = ps("ps0_a", [P, DC, 2 * H0])

        loaded, all_loaded = k.loads_in, k.expect_loads(5)
        masks = sem("amask_ready")
        abl = sem("ablk_ready")
        wt = sem("w0_transposed")
        wxr = sem("wx0_ready")
        normed = sem("normed0")
        turned = sem("turned0")
        xt_ready = sem("xt0_ready")
        mm_done = sem("mm0_done")
        h_ready = sem("h0_ready")
        h_kept = [sem(f"h0_kept{j}") for j in range(len(LOTS))]
        block = ctx.enter_context(nc.Block())

        @block.gpsimd
        def _(pool):
            pool.memset(amask[:, :, :], 1.0).then_inc(masks, 1)
            pool.wait_ge(masks, 1)
            pool.affine_select(out=amask[:, :, :], in_=amask[:, :, :], compare_op=ALU.is_ge, fill=0.0, base=0,
                               pattern=[[P, DC], [-F0, H0]], channel_multiplier=1).then_inc(masks, 1)
            pool.wait_ge(masks, 2)
            pool.affine_select(out=amask[:, :, :], in_=amask[:, :, :], compare_op=ALU.is_ge, fill=0.0, base=F0 - 1,
                               pattern=[[-P, DC], [F0, H0]], channel_multiplier=-1).then_inc(masks, 1)

        @block.sync
        def _(sp):
            sp.dma_start(w[:, :, :], a["L0_gnn_W"].rearrange("(c p) d -> p c d", p=P)).then_inc(loaded, 16)
            for j, name in enumerate(("L0_gnn_a_src", "L0_gnn_a_dst")):
                flat = a[name].rearrange("h f -> (h f)")
                for c in range(DC):
                    sp.dma_start(a_col[:, j, c:c + 1], flat[c * P:(c + 1) * P].rearrange("(p o) -> p o", o=1)
                                 ).then_inc(loaded, 16)

            def trip(i):
                for n, (lo, hi) in enumerate(LOTS):
                    wait(sp, h_ready, i * UNR + hi)
                    sp.dma_start(k.h_rows[bass.ds((i * UNR + lo) * P, (hi - lo) * P), :]
                                 .rearrange("(w p) r -> p w r", p=P), h[:, lo:hi, 0:R0]).then_inc(h_kept[n], 16)

            rounds(sp, WROUNDS, trip)
            for n in range(len(LOTS)):
                sp.wait_ge(h_kept[n], 16 * WROUNDS)

        @block.vector
        def _(v):
            c = k.chain_on(v)
            v.wait_ge(loaded, all_loaded)
            v.wait_ge(masks, 3)
            for j in range(2):
                for c2 in range(DC):
                    v.tensor_scalar(ablk[:, c2, j, :], amask[:, c2, :], a_col[:, j, c2:c2 + 1], None, ALU.mult
                                    ).then_inc(abl, 1)
            v.wait_ge(k.w_in, 16 * X_LOADS)

            def trip(i):
                c.enter(i, Norm.LINKS, WROUNDS - 1, first=1)
                norm.on_vector(v, c, i, lambda j: k.x[:, i * UNR + j, :])
                for j in range(UNR):
                    wait(v, turned, i * UNR)
                    norm.apply(v, xn[:, j, :], k.x[:, i * UNR + j, :], j).then_inc(normed, 1)
                c.leave()

            rounds(v, WROUNDS, trip)
            v.wait_ge(h_ready, WIN)
            hi, mid, lo = (k.by_dst[:, :, j, :] for j in range(3))
            c.link(v.tensor_copy(hi, ad[:, :, :]))
            c.link(v.tensor_tensor(ad_r[:, :, :], ad[:, :, :], hi, ALU.subtract))
            c.link(v.tensor_copy(mid, ad_r[:, :, :]))
            c.link(v.tensor_tensor(ad_r[:, :, :], ad_r[:, :, :], mid, ALU.subtract))
            c.link(v.tensor_copy(lo, ad_r[:, :, :]))

        @block.scalar
        def _(act):
            act.wait_ge(wt, 1)
            act.copy(wx[:, :, 0:D], ps_w[:, :, :]).then_inc(wxr, 1)
            act.wait_ge(wt, 2)
            act.copy(wx[:, :, D:RW], ps_a[:, :, :]).then_inc(wxr, 1)

            def turn(i, j):
                wait(act, turned, i * UNR + (j + 1))
                wait(act, mm_done, i * UNR)
                act.copy(xt[:, j, :, :], ps_t[j % 2][:, :, :]).then_inc(xt_ready, 1)

            def take(i, j):
                wait(act, mm_done, i * UNR + (j + 1))
                wait(act, h_kept[lot_of(j)], 16 * i)
                act.copy(h[:, j, :], ps_h[j % 2][:, :]).then_inc(h_copied, 1)
                wait(act, h_copied, i * UNR + (j + 1))
                act.copy(ad[:, i * UNR + j, :], h[:, j, R0:RW]).then_inc(h_ready, 1)

            h_copied = sem("h0_copied")

            def trip(i):
                norm.on_scalar(act, i, k.eps)
                turn(i, 0)
                for j in range(1, UNR):
                    turn(i, j)
                    take(i, j - 1)
                take(i, UNR - 1)

            rounds(act, WROUNDS, trip)

        @block.tensor
        def _(pe):
            pe.wait_ge(loaded, all_loaded)
            for c in range(DC):
                for dc in range(DC):
                    mm = pe.transpose(ps_w[:, dc, c * P:(c + 1) * P], w[:, c, dc * P:(dc + 1) * P], k.ident[:, :])
            mm.then_inc(wt, 1)
            pe.wait_ge(abl, 4)
            for dc in range(DC):
                for c in range(DC):
                    mm = pe.matmul(ps_a[:, dc, :], w[:, c, dc * P:(dc + 1) * P],
                                   ablk[:, c, :, :].rearrange("p j h -> p (j h)"),
                                   start=(c == 0), stop=(c == DC - 1))
            mm.then_inc(wt, 1)
            pe.wait_ge(wxr, 2)

            def turn(i, j):
                wait(pe, normed, i * UNR + (j + 1))
                if j >= 2:
                    wait(pe, xt_ready, i * UNR + (j - 1))
                else:
                    wait(pe, xt_ready, i * UNR)
                for c in range(DC):
                    mm = pe.transpose(ps_t[j % 2][:, c, :], xn[:, j, c * P:(c + 1) * P], k.ident[:, :])
                mm.then_inc(turned, 1)

            def multiply(i, j):
                wait(pe, xt_ready, i * UNR + (j + 1))
                wait(pe, h_ready, i * UNR + max(j - 1, 0))
                for c in range(DC):
                    mm = pe.matmul(ps_h[j % 2][:, :], xt[:, j, c, :], wx[:, c, :], start=(c == 0), stop=(c == DC - 1))
                mm.then_inc(mm_done, 1)

            def trip(i):
                turn(i, 0)
                for j in range(1, UNR):
                    turn(i, j)
                    multiply(i, j - 1)
                multiply(i, UNR - 1)

            rounds(pe, WROUNDS, trip)


class Layer:

    def __init__(self, H, F, R, ring, messages, sums, values):
        self.H, self.F, self.R = H, F, R
        self.ring = ring
        self.messages, self.sums, self.values = messages, sums, values
        self.value_column = self.R // (2 * D) * D
        self.PH = BATCH * H


FIRST = Layer(H0, F0, R0, 3, (0, R0), (D, R0), (0, D))
SECOND = Layer(H1, F1, R1, 2, (D - H1, R1), (0, H1), (H1, H1 + D))
GROUP = 4
GROUPS = BATCH // GROUP
BATCHES = STEPS // BATCH
QP = 2
PAIRS = BATCH // QP


def edges(nc, k, L, ctx, accs):
    H, F, PH = L.H, L.F, L.PH
    first = L is FIRST
    mlo, mhi = L.messages
    MW = mhi - mlo
    hsel, hselT, mask, cuts = ((k.hsel8, k.hselT8, k.mask8, k.step_cut8) if first
                               else (k.hsel4, k.hselT4, k.mask4, k.step_cut4))
    rows_of = k.h_rows if first else k.kv_rows
    n = "e0_" if first else "e1_"

    def sb(name, shape, dt=F32):
        return ctx.enter_context(nc.sbuf_tensor(n + name, shape, dt))

    def ps(name, shape):
        return ctx.enter_context(nc.psum_tensor(n + name, shape, F32))

    def sem(name):
        return ctx.enter_context(nc.semaphore(n + name))

    R = L.ring
    two = range(2)
    ring = range(R)
    PARTS = 1 if first else 2
    g = [sb(f"rows{b}", [P, BATCH, L.R]) for b in ring]
    src_i = [sb(f"src{b}", [P, BATCH], I32) for b in ring]
    rel = [sb(f"rel{b}", [P, BATCH * P], BF16) for b in ring]
    cut = [sb(f"cut{b}", [PH, P + 4]) for b in ring]
    to_dst = [sb(f"to_dst{b}", [P, BATCH * P], BF16) for b in ring]
    HOTS = 4 if first else 2
    of_dst = [sb(f"of_dst{b}", [P, GROUP, P]) for b in range(HOTS)]
    sc = sb("scores", [P, BATCH, H])
    sc2 = sb("scores2", [P, P // H, H])
    fwd = sb("fwd", [PH, P])
    bwd = sb("bwd", [PH, P])
    diff = sb("diff", [PH, P])
    prob = sb("prob", [P, P])
    tip = sb("tip", [P, 2, BATCH])
    run = [sb(f"run{b}", [H, BATCH + 1]) for b in ring]
    join_back = sb("join_back", [H, BATCH])
    back = sb("back", [H, BATCH + 1])
    ctxt = sb("ctxt", [H, 2, BATCH])
    new_max = sb("new_max", [H, 1])
    fall = sb("fall", [H, 1])
    factor = sb("factor", [H, 1])
    diag = sb("diag", [H, H])
    node0 = sb("node0", [H, P])
    ini2 = sb("ini2", [PH, 2, BATCH])
    ini = sb("ini", [PH, 2])
    fac = sb("fac", [P, H])
    tock = sb("tock", [P, 1])
    tick = sb("tick", [P, 1])
    NB = 6 if first else 3
    ZEROED = 3 if first else 6
    psm = [ps(f"sum{b}", [P, BANK])[:, 0:MW] for b in range(NB)]
    ps_t = ps("turned", [P, BANK])
    A = 2 * P
    ps_tip = ps_t[0:H, A:A + 2 * BATCH]
    ps_ctx = ps_t[0:PH, A + 2 * BATCH:A + 4 * BATCH]
    ps_fac = ps_t[:, A + 4 * BATCH:A + 4 * BATCH + H]
    if first:
        look = ps("look", [P, BANK])[:, 0:3 * PH].rearrange("p (s j h) -> p s j h", j=3, h=H)
    else:
        typ = [sb(f"typ{b}", [F1, BATCH * P], BF16) for b in ring]
        to_typ = sb("to_typ", [F1, BATCH * P], BF16)
        prod = [sb(f"prod{b}", [P, QP, H * F]) for b in two]
        ps_q = [ps(f"query{b}", [P, QP, D]) for b in two]
        ps_r = [ps(f"relation{b}", [P, BANK])[:, 0:QP * F].rearrange("p (s f) -> p s f", f=F) for b in two]

    zeroed = sem("zeroed")
    rel_in = [sem(f"rel_in{b}") for b in ring]
    cut_in = [sem(f"cut_in{b}") for b in ring]
    src_ready = sem("src_ready")
    rows_in = [[sem(f"rows_in{b}_{part}") for part in range(PARTS)] for b in ring]
    masks_ready = sem("masks_ready")
    looked = sem("looked")
    if not first:
        rel_copied = sem("rel_copied")
        rel_added = sem("rel_added")
        BY_POOL = (1, 3, 5, 7)
        rel_sb = sb("relations", [P, QP, F])
    look_used = sem("look_used")
    scored = sem("scored")
    sc_turned = sem("sc_turned")
    tips = sem("tips")
    tips_by_head = sem("tips_by_head")
    fall_ready = sem("fall_ready")
    factor_ready = sem("factor_ready")
    ctx_ready = sem("ctx_ready")
    ctx_back = sem("ctx_back")
    diff_ready = sem("diff_ready")
    prob_ready = sem("prob_ready")
    prob_turned = sem("prob_turned")
    prob_in_rows = sem("prob_in_rows")
    msg_ready = sem("msg_ready")
    hot_ready = sem("hot_ready")
    BY_ACT = range(2, GROUPS) if first else range(GROUPS)
    summed = sem("summed")
    added = sem("added")
    AHEAD = R * BATCH
    ROWS_IN = 16 * BATCH // PARTS
    KR = 16 if first else 32
    block = ctx.enter_context(nc.Block())

    plo = D if first else D - H

    def windows(eng, name):
        sets = []

        def load(m):
            regs = [eng.alloc_register(f"{n}{name}{len(sets)}_{s}") for s in range(BATCH)]
            sets.append(regs)
            eng.load(regs, k.win_row[0:1, bass.ds(m * BATCH, BATCH)])
            return [eng.snap(r, donate=True, min_val=0, max_val=WIN - 1) for r in regs]
        return load

    def after(i, b, d):
        return i + (b + d) // R, (b + d) % R

    def periods(eng, body, first_of, last, chain=None, per=0):
        assert first_of % R == 0
        trips = (last + 1 - first_of) // R
        with eng.Fori(0, trips) as i:
            if chain:
                chain.enter(i, per * R, trips)
            for b in ring:
                body(i + first_of // R if first_of else i, b)
            if chain:
                chain.leave()
        for m in range(first_of + trips * R, last + 1):
            body(m // R, m % R)

    @block.sync
    def _(sp):
        def load_rel(m, b):
            sp.dma_start(rel[b][:, :], k.step_rel[bass.ds(m * BATCH, BATCH), :].rearrange("s e -> (s e)")
                         .partition_broadcast(P)).then_inc(rel_in[b], 16)
            if not first:
                sp.dma_start(typ[b][:, :], k.step_typ[bass.ds(m * BATCH, BATCH), :].rearrange("s e -> (s e)")
                             .partition_broadcast(F1)).then_inc(rel_in[b], 16)

        def load_cut(m, b):
            sp.dma_start(cut[b][:, :], cuts[bass.ds(m * BATCH, BATCH), :, :].rearrange("s h e -> (s h) e")
                         ).then_inc(cut_in[b], 16)

        def refill(i, b):
            m = i * R + b
            sp.wait_ge(diff_ready, m - R + 1)
            load_rel(m, b)
            load_cut(m, b)

        for b in ring:
            load_rel(b, b)
            load_cut(b, b)
        periods(sp, refill, R, BATCHES - 1)
        sp.wait_ge(diff_ready, BATCHES - R + 1)
        load_rel(BATCHES, BATCHES % R)

    @block.gpsimd
    def _(pool):
        pool.memset(run[R - 1][:, :], NEG).then_inc(zeroed, 1)
        pool.memset(back[:, :], NEG).then_inc(zeroed, 1)
        pool.memset(tock[:, :], 0.0).then_inc(zeroed, 1)
        for t in () if first else (sc2, prob, tip):
            pool.memset(t[:], 0.0).then_inc(zeroed, 1)
        pool.wait_ge(zeroed, ZEROED)
        pool.memset(ctxt[:, :, :], NEG).then_inc(summed, AHEAD)
        pool.memset(ini[:, :], NEG).then_inc(look_used, 2)
        pool.memset(fac[:, :], 0.0).then_inc(added, NB)

        def gather(i, b, q):
            m = i * R + b
            steps = slice(q * GROUP, (q + 1) * GROUP)
            pool.tensor_copy(src_i[b][:, steps], k.src_col[:, bass.ds(m * BATCH + steps.start, GROUP)]
                             ).then_inc(src_ready, 1)
            pool.wait_ge(src_ready, (m * GROUPS + q) * 2 + 1)
            pool.tensor_tensor(tick[:, :], tock[:, :], tock[:, :], ALU.add).then_inc(src_ready, 1)
            for s in range(steps.start, steps.stop):
                pool.indirect_dma_start(out=g[b][:, s, :], out_offset=None, in_=rows_of[:, :],
                                        in_offset=bass.IndirectOffsetOnAxis(ap=src_i[b][:, s:s + 1], axis=0)
                                        ).then_inc(rows_in[b][q * PARTS // GROUPS], 16)

        def add_relations(i, b, chosen):
            keys = g[b][:, :, 0:D].rearrange("p s (h f) -> p s h f", h=H)
            for q in chosen:
                at = slice(q * QP, (q + 1) * QP)
                pool.wait_ge(rows_in[b][q * PARTS // PAIRS], (i + 1) * ROWS_IN)
                pool.wait_ge(rel_copied, (i * R + (b - 1)) * len(BY_POOL) + (BY_POOL.index(q) + 1))
                pool.tensor_tensor(keys[:, at, :, :], keys[:, at, :, :],
                                   rel_sb[:, :, :].unsqueeze(2).to_broadcast([P, QP, H, F]), ALU.add
                                   ).then_inc(rel_added, 1)

        def refill(i, b):
            if not first:
                add_relations(*after(i, b, 1), BY_POOL[:-1])
            for q in range(GROUPS):
                pool.wait_ge(summed, (i * R + b) * BATCH + ((q + 1) * GROUP + AHEAD))
                gather(i + 1, b, q)
                if q == 0 and not first:
                    add_relations(*after(i, b, 1), BY_POOL[-1:])

        for b in ring:
            for q in range(GROUPS):
                gather(0, b, q)
        periods(pool, refill, 0, BATCHES - R - 1)
        if not first:
            add_relations((BATCHES - 1) // R, (BATCHES - 1) % R, BY_POOL)

    @block.vector
    def _(v):
        c = k.chain_on(v)

        def masks(i, b):
            v.wait_ge(rel_in[b], (i + 1) * KR)
            if not first:
                v.tensor_scalar(to_typ[:, :], typ[b][:, :], k.iota_col[0:F1, 0:1], None, ALU.is_equal)
            v.tensor_scalar(to_dst[b][:, :], rel[b][:, :], k.iota_col[:, 0:1], None, ALU.is_equal
                            ).then_inc(masks_ready, 1)

        def scores_first(i, b):
            v.wait_ge(looked, i * R + (b + 1))
            v.wait_ge(rows_in[b][0], (i + 1) * ROWS_IN)
            c.link(v.tensor_reduce(sc[:, :, :], look.rearrange("p s j h -> p s h j"), AX_X, ALU.add))
            c.link(v.tensor_tensor(sc[:, :, :], sc[:, :, :], g[b][:, :, D:D + H], ALU.add))
            v.scalar_tensor_tensor(out=sc2[:, 0:BATCH, :], in0=sc[:, :, :], scalar=0.2, in1=sc[:, :, :],
                                   op0=ALU.mult, op1=ALU.max).then_inc(scored, 1)

        def scores_second(i, b, q, m=None, w=None, adds=()):
            pooled = m is not None and q in BY_POOL
            at = slice(q * QP, (q + 1) * QP)
            keys = g[b][:, at, 0:D].rearrange("p s (h f) -> p s h f", h=H)
            v.wait_ge(looked, (i * R + b) * PAIRS + (q + 1))
            v.wait_ge(rows_in[b][q * PARTS // PAIRS], (i + 1) * ROWS_IN)
            if pooled:
                add(m, adds[:1], w)
                v.wait_ge(rel_added, m * len(BY_POOL) + (BY_POOL.index(q) + 1))
            else:
                c.inc(v.tensor_tensor(keys, keys, ps_r[q % 2].unsqueeze(2).to_broadcast([P, QP, H, F]), ALU.add))
                add(m, adds[:1], w)
                c.wait()
            v.tensor_tensor(prod[q % 2][:, :, :], g[b][:, at, 0:D], ps_q[q % 2][:, :, :], ALU.mult
                            ).then_inc(look_used, 1)
            add(m, adds[1:], w)
            v.wait_ge(look_used, (i * R + b) * PAIRS + (q + 3))
            v.tensor_reduce(sc2[:, at, :], prod[q % 2][:, :, :].rearrange("p s (h f) -> p s h f", h=H), AX_X, ALU.add
                            ).then_inc(scored, 1)

        def scans(b, ini_f, ini_b):
            c.inc(v.tensor_tensor_scan(fwd[:, :], cut[b][:, 0:P], ps_t[0:PH, 0:P], ini_f, ALU.add, ALU.max))
            c.link(v.tensor_tensor_scan(bwd[:, ::-1], cut[b][:, P:0:-1], ps_t[0:PH, P - 1::-1], ini_b,
                                        ALU.add, ALU.max))

        def step_maxima(i, b):
            m = i * R + b
            v.wait_ge(sc_turned, m + 1)
            v.wait_ge(cut_in[b], (i + 1) * 16)
            c.inc(v.tensor_copy(join_back[:, :], k.joined[0:H, 2, bass.ds(m * BATCH, BATCH)]))
            scans(b, NEG, NEG)
            v.tensor_scalar(tip[0:PH, 0, :], mask[:, :], fwd[:, P - 1:P], None, ALU.mult)
            v.tensor_scalar(tip[0:PH, 1, :], mask[:, :], bwd[:, 0:1], None, ALU.mult).then_inc(tips, 1)

        def across_steps(i, b):
            m = i * R + b
            before = run[(b - 1) % R]
            v.wait_ge(tips_by_head, m + 1)
            c.inc(v.tensor_copy(run[b][:, 0:1], before[:, BATCH:BATCH + 1]))
            c.inc(v.tensor_tensor_scan(run[b][:, 1:BATCH + 1], k.joined[0:H, 1, bass.ds(m * BATCH, BATCH)],
                                       ps_tip[:, 0:BATCH], before[:, BATCH:BATCH + 1], ALU.add, ALU.max))
            c.link(v.tensor_tensor_scan(back[:, BATCH - 1::-1], join_back[:, BATCH - 1::-1],
                                        ps_tip[:, 2 * BATCH - 1:BATCH - 1:-1], NEG, ALU.add, ALU.max))
            c.inc(v.tensor_tensor(ctxt[:, 0, :], run[b][:, 0:BATCH], k.joined[0:H, 0, bass.ds(m * BATCH, BATCH)],
                                  ALU.add))
            c.link(v.tensor_tensor(ctxt[:, 1, :], back[:, 1:BATCH + 1],
                                   k.joined[0:H, 0, bass.ds(m * BATCH + 1, BATCH)], ALU.add))
            c.link(v.tensor_tensor(new_max[:, :], back[:, 0:1], ctxt[:, 0, 0:1], ALU.max))
            v.tensor_scalar(fall[:, :], ctxt[:, 0, 0:1], new_max[:, 0:1], -80.0, ALU.subtract, ALU.max
                            ).then_inc(fall_ready, 1)
            v.tensor_scalar(node0[:, :], k.iota_row[0:H, :], rel[b][0:H, 0:1], None, ALU.is_equal)

        def factors(i, b):
            v.wait_ge(factor_ready, i * R + (b + 1))
            v.scalar_tensor_tensor(out=diag[:, :], in0=k.ident[0:H, 0:H], scalar=factor[:, 0:1],
                                   in1=k.ident[0:H, 0:H], op0=ALU.mult, op1=ALU.subtract).then_inc(ctx_ready, 1)

        def differences(i, b, m=0, w=None, adds=()):
            v.wait_ge(ctx_back, i * R + (b + 1))
            c.inc(v.tensor_tensor(ini2[:, :, :], ps_ctx.rearrange("p (j s) -> p j s", j=2),
                                  mask[:, :].unsqueeze(1).to_broadcast([PH, 2, BATCH]), ALU.mult))
            add(m, adds[0:1], w)
            c.wait()
            c.inc(v.tensor_copy(fac[:, :], ps_fac))
            c.inc(v.tensor_reduce(ini[:, :], ini2[:, :, :], AX_X, ALU.add))
            add(m, adds[1:2], w)
            c.wait()
            scans(b, ini[:, 0:1], ini[:, 1:2])
            add(m, adds[2:3], w)
            c.link(v.tensor_tensor(fwd[:, :], fwd[:, :], bwd[:, :], ALU.max))
            v.tensor_tensor(diff[:, :], ps_t[0:PH, 0:P], fwd[:, :], ALU.subtract).then_inc(diff_ready, 1)

        def rescale(m, w):
            v.wait_ge(added, m * BATCH + NB)
            for acc in accs:
                sums = acc[:, w[0], L.sums[0]:L.sums[1]]
                vals = acc[:, w[0], L.values[0]:L.values[1]].rearrange("p (h f) -> p h f", h=H)
                c.inc(v.scalar_tensor_tensor(out=sums, in0=fac[:, :], scalar=1.0, in1=sums,
                                             op0=ALU.add, op1=ALU.mult))
                c.inc(v.scalar_tensor_tensor(out=vals, in0=fac[:, :].unsqueeze(2).to_broadcast([P, H, F]), scalar=1.0,
                                             in1=vals, op0=ALU.add, op1=ALU.mult))
            c.wait()

        def hot(i, b, q):
            ins = v.tensor_tensor(of_dst[q % HOTS][:, :, :], k.iota_row[:, :].unsqueeze(1).to_broadcast([P, GROUP, P]),
                                  k.rel_col[:, bass.ds((i * R + b) * BATCH + q * GROUP, GROUP)].unsqueeze(2)
                                  .to_broadcast([P, GROUP, P]), ALU.is_equal)
            if q in BY_ACT:
                ins.then_inc(hot_ready, 1)

        def values(i, b, q, half):
            if q == half == 0:
                v.wait_ge(prob_in_rows, i * R + (b + 1))
            lo = q * GROUP + half * GROUP // 2
            steps = slice(lo, lo + GROUP // 2)
            vals = g[b][:, steps, 0:D].rearrange("p s (h f) -> p s h f", h=H)
            pr = g[b][:, steps, plo:plo + H]
            ins = v.tensor_tensor(vals, vals, pr.unsqueeze(3).to_broadcast([P, GROUP // 2, H, F]), ALU.mult)
            if half:
                ins.then_inc(hot_ready, 1)

        def make(i, b, q):
            hot(i, b, q)
            if q not in BY_ACT:
                values(i, b, q, 0)
                values(i, b, q, 1)

        def add(m, steps, w):
            for s in steps:
                v.wait_ge(summed, m * BATCH + (s + 1 + AHEAD))
                v.wait_ge(added, m * BATCH + (s + NB + 1 - len(accs)))
                acc = accs[s % len(accs)]
                v.tensor_tensor(acc[:, w[s], :], acc[:, w[s], :], psm[s % NB], ALU.add).then_inc(added, 1)

        load_windows = windows(v, "dve_w")

        def period(i, b):
            m = i * R + b
            i1, b1 = after(i, b, 1)
            if first:
                scores_first(i1, b1)
                hot(i, b, 0)
                w = load_windows(m)
                rescale(m, w)
                values(i, b, 0, 0)
                values(i, b, 0, 1)
                step_maxima(i1, b1)
                make(i, b, 1)
                across_steps(i1, b1)
                add(m, [0], w)
                hot(i, b, 2)
                add(m, [1], w)
                factors(i1, b1)
                add(m, [2], w)
                hot(i, b, 3)
                add(m, [3], w)
                masks(*after(i, b, 2))
                add(m, range(4, 8), w)
                differences(i1, b1, m, w, [8, 9, 10])
                add(m, range(11, BATCH), w)
            else:
                hot(i, b, 0)
                hot(i, b, 1)
                w = load_windows(m)
                rescale(m, w)
                for q in range(PAIRS):
                    if q == 5:
                        hot(i, b, 2)
                    scores_second(i1, b1, q, m, w, range(2 * q - 6, 2 * q - 4) if q >= 3 else ())
                hot(i, b, 3)
                step_maxima(i1, b1)
                add(m, [10], w)
                across_steps(i1, b1)
                add(m, [11, 12], w)
                factors(i1, b1)
                masks(*after(i, b, 2))
                differences(i1, b1, m, w, [13, 14, 15])

        v.wait_ge(zeroed, ZEROED)
        v.wait_ge(summed, AHEAD)
        v.wait_ge(look_used, 2)
        masks(0, 0)
        for acc in accs:
            c.link(v.memset(acc[:, :, :], 0.0))
        if first:
            scores_first(0, 0)
        else:
            for q in range(PAIRS):
                scores_second(0, 0, q)
        step_maxima(0, 0)
        across_steps(0, 0)
        factors(0, 0)
        differences(0, 0)
        masks(*after(0, 0, 1))
        periods(v, period, 0, BATCHES - 2, c, 15 + 2 * len(accs) + (2 if first else PAIRS - len(BY_POOL)))
        m, i, b = BATCHES - 1, (BATCHES - 1) // R, (BATCHES - 1) % R
        w = load_windows(m)
        rescale(m, w)
        for q in range(GROUPS):
            make(i, b, q)
            if q or not first:
                lo = (q - first) * GROUP
                add(m, range(lo, lo + GROUP), w)
        if first:
            add(m, range(BATCH - GROUP, BATCH), w)

    @block.scalar
    def _(act):
        def values(i, b, q):
            for s in range(q * GROUP, (q + 1) * GROUP):
                for h in range(H):
                    lo = L.value_column + h * F
                    x = g[b][:, s, lo:lo + F]
                    ins = act.activation(x, x, ACT.Copy, scale=g[b][:, s, plo + h:plo + h + 1])
            ins.then_inc(msg_ready, 1)

        def fall_factor(m):
            act.wait_ge(fall_ready, m + 1)
            act.activation(factor[:, :], fall[:, :], ACT.Exp).then_inc(factor_ready, 1)

        def probabilities(m, b):
            act.wait_ge(diff_ready, m + 1)
            act.activation(prob[0:PH, :], diff[:, :], ACT.Exp).then_inc(prob_ready, 1)
            act.wait_ge(prob_turned, m + 1)
            act.copy(g[b][:, :, plo:plo + H],
                     ps_t[:, P:P + PH].rearrange("p (s h) -> p s h", h=H)).then_inc(prob_in_rows, 1)

        def period(i, b):
            m1, b1 = i * R + (b + 1), (b + 1) % R
            act.wait_ge(prob_in_rows, m1)
            if first:
                values(i, b, 2)
                fall_factor(m1)
                values(i, b, 3)
            else:
                for q in BY_ACT:
                    pair = BY_POOL[q]
                    act.wait_ge(looked, m1 * PAIRS + (pair + 1))
                    act.copy(rel_sb[:, :, :], ps_r[pair % 2]).then_inc(rel_copied, 1)
                    values(i, b, q)
                fall_factor(m1)
            probabilities(m1, b1)

        fall_factor(0)
        probabilities(0, 0)
        periods(act, period, 0, BATCHES - 2)
        act.wait_ge(prob_in_rows, BATCHES)
        for q in BY_ACT:
            values(0, (BATCHES - 1) % R, q)

    @block.tensor
    def _(pe):
        load_windows = windows(pe, "pe_w")

        def look_first(m, b, scores):
            w = load_windows(m)
            pe.wait_ge(masks_ready, m + 1)
            if scores:
                pe.wait_ge(scored, m)
            for s in range(BATCH):
                mm = pe.matmul(look[:, s, :, :].rearrange("p j h -> p (j h)"), to_dst[b][:, s * P:(s + 1) * P],
                               k.by_dst[:, w[s], :, :].rearrange("p j h -> p (j h)"), start=True, stop=True)
            mm.then_inc(looked, 1)

        def look_second(m, b, q, w):
            pe.wait_ge(look_used, m * PAIRS + (q + 1))
            for t in range(QP):
                s = q * QP + t
                for j in range(3):
                    pe.matmul(ps_q[q % 2][:, t, :], to_dst[b][:, s * P:(s + 1) * P],
                              k.by_dst[:, w[s], j, :], start=(j == 0), stop=(j == 2))
                for j in range(3):
                    mm = pe.matmul(ps_r[q % 2][:, t, :], to_typ[:, s * P:(s + 1) * P],
                                   k.by_typ[:, j, :], start=(j == 0), stop=(j == 2))
            mm.then_inc(looked, 1)

        def look_pairs(m, b):
            w = load_windows(m)
            pe.wait_ge(masks_ready, m + 1)
            for q in range(2):
                look_second(m, b, q, w)

        def turn_scores(m):
            pe.wait_ge(scored, m + 1 if first else (m + 1) * PAIRS)
            if not (isinstance(m, int) and m == 0):
                pe.wait_ge(prob_in_rows, m)
            pe.transpose(ps_t[:, 0:P], sc2[:, :, :].rearrange("p s h -> p (s h)"), k.ident[:, :]
                         ).then_inc(sc_turned, 1)

        def turn_tips(m):
            pe.wait_ge(tips, m + 1)
            pe.matmul(ps_tip, hsel[:, :], tip[:, :, :].rearrange("p j s -> p (j s)"), start=True, stop=True
                      ).then_inc(tips_by_head, 1)

        def turn_context(m):
            pe.wait_ge(ctx_ready, m + 1)
            pe.matmul(ps_ctx, hselT[:, :], ctxt[:, :, :].rearrange("h j s -> h (j s)"), start=True, stop=True)
            pe.matmul(ps_fac, node0[:, :], diag[:, :], start=True, stop=True).then_inc(ctx_back, 1)

        def turn_probabilities(m):
            pe.wait_ge(prob_ready, m + 1)
            pe.transpose(ps_t[:, P:2 * P], prob[:, :], k.ident[:, :]).then_inc(prob_turned, 1)

        def sums(m, b, steps):
            for s in steps:
                q = s // GROUP
                if s % GROUP == 0:
                    pe.wait_ge(hot_ready, m * GROUPS + (q + 1))
                    if q in BY_ACT:
                        pe.wait_ge(msg_ready, m * len(BY_ACT) + (q - BY_ACT[0] + 1))
                pe.wait_ge(added, m * BATCH + (s + 1))
                pe.matmul(psm[s % NB], of_dst[q % HOTS][:, s % GROUP, :], g[b][:, s, mlo:mhi],
                          start=True, stop=True).then_inc(summed, 1)

        def period(i, b):
            m = i * R + b
            m1, b1 = m + 1, (b + 1) % R
            if first:
                turn_scores(m1)
                sums(m, b, range(0, 2))
                turn_tips(m1)
                sums(m, b, range(2, 8))
                turn_context(m1)
                sums(m, b, range(8, 10))
                look_first(m + 2, (b + 2) % R, True)
                sums(m, b, range(10, 14))
                turn_probabilities(m1)
                sums(m, b, range(14, BATCH))
            else:
                w = load_windows(m1)
                for q in range(2, PAIRS):
                    look_second(m1, b1, q, w)
                    if q >= 3:
                        sums(m, b, range(2 * q - 6, 2 * q - 4))
                turn_scores(m1)
                sums(m, b, [10])
                turn_tips(m1)
                sums(m, b, range(11, 15))
                turn_context(m1)
                sums(m, b, [15])
                look_pairs(m + 2, (b + 2) % R)
                turn_probabilities(m1)

        if first:
            look_first(0, 0, False)
        else:
            w = load_windows(0)
            pe.wait_ge(masks_ready, 1)
            for q in range(PAIRS):
                look_second(0, 0, q, w)
        turn_scores(0)
        turn_tips(0)
        turn_context(0)
        if first:
            turn_probabilities(0)
            look_first(1, 1, True)
        else:
            look_pairs(1, 1)
            turn_probabilities(0)
        periods(pe, period, 0, BATCHES - 2)
        pe.wait_ge(prob_in_rows, BATCHES)
        sums(BATCHES - 1, (BATCHES - 1) % R, range(BATCH))


def mix_first(nc, k, a):
    with ExitStack() as ctx:
        def sb(name, shape, dt=F32):
            return ctx.enter_context(nc.sbuf_tensor(name, shape, dt))

        def sem(name):
            return ctx.enter_context(nc.semaphore(name))

        bias = sb("bias0", [P, D])
        inv = sb("inv0", [P, UNR, H0])
        xn = sb("xn1", [P, UNR, D])
        norm = Norm(ctx, nc, k, "ln1")
        ps_t = [ctx.enter_context(nc.psum_tensor(f"ps1_t{i}", [P, BANK], F32)) for i in range(2)]
        loaded, all_loaded = k.loads_in, k.expect_loads(1)
        normed = sem("normed1")
        merged = sem("acc0_merged")
        turned = sem("turned1")
        xt_ready = sem("xt1_ready")
        block = ctx.enter_context(nc.Block())

        @block.sync
        def _(sp):
            sp.dma_start(bias[:, :], a["L0_gnn_bias"].partition_broadcast(P)).then_inc(loaded, 16)

        @block.gpsimd
        def _(pool):
            for r in range(WROUNDS):
                at = slice(r * UNR, (r + 1) * UNR)
                if r:
                    pool.wait_ge(merged, r)
                pool.tensor_tensor(k.acc0[:, at, :], k.acc0[:, at, :], k.acc0_odd[:, at, :], ALU.add
                                   ).then_inc(merged, 1)

        @block.vector
        def _(v):
            c = k.chain_on(v)
            v.wait_ge(loaded, all_loaded)

            def trip(i):
                c.enter(i, Norm.LINKS + 6, WROUNDS - 1, first=1)
                at = bass.ds(i * UNR, UNR)
                vals = k.acc0[:, at, 0:D].rearrange("p w (h f) -> p w h f", h=H0)
                wait(v, merged, i + 1)
                c.link(v.tensor_scalar(inv[:, :, :], k.acc0[:, at, D:R0], 1e-10, None, ALU.max))
                c.inc(v.tensor_tensor(k.x[:, at, :], k.x[:, at, :],
                                      bias[:, :].unsqueeze(1).to_broadcast([P, UNR, D]), ALU.add))
                c.link(v.reciprocal(inv[:, :, :], inv[:, :, :]))
                c.link(v.tensor_tensor(vals, vals, inv[:, :, :].unsqueeze(3).to_broadcast([P, UNR, H0, F0]), ALU.mult))
                c.link(v.tensor_tensor(k.x[:, at, :], k.x[:, at, :], k.acc0[:, at, 0:D], ALU.add))
                norm.on_vector(v, c, i, lambda j: k.x[:, i * UNR + j, :])
                v.tensor_copy(k.rstd[:, at], norm.rstd[:, :])
                c.inc(v.tensor_copy(k.mean[:, at], norm.mv[:, :, 0]))
                wait(v, turned, i * UNR)
                for j in range(UNR):
                    norm.apply(v, xn[:, j, :], k.x[:, i * UNR + j, :], j).then_inc(normed, 1)
                c.leave()

            rounds(v, WROUNDS, trip)
            v.wait_ge(xt_ready, WIN)
            v.tensor_reduce(k.total[:, :], k.xt[:, :, 0:N], AX_X, ALU.add)

        @block.scalar
        def _(act):

            def trip(i):
                norm.on_scalar(act, i, k.eps)
                for j in range(UNR):
                    wait(act, turned, i * UNR + (j + 1))
                    act.copy(k.xt[:, :, bass.ds((i * UNR + j) * P, P)],
                             ps_t[j % 2][:, 0:D].rearrange("p (c n) -> p c n", c=DC)).then_inc(xt_ready, 1)

            rounds(act, WROUNDS, trip)

        @block.tensor
        def _(pe):

            def trip(i):
                for j in range(UNR):
                    wait(pe, normed, i * UNR + (j + 1))
                    wait(pe, xt_ready, i * UNR + max(j - 1, 0))
                    for c in range(DC):
                        mm = pe.transpose(ps_t[j % 2][:, c * P:(c + 1) * P], xn[:, j, c * P:(c + 1) * P],
                                          k.ident[:, :])
                    mm.then_inc(turned, 1)

            rounds(pe, WROUNDS, trip)


TOP = 2
E0, HID = 8, 512
FC = HID // P
CAPACITY = float(-(-N * 5 // (E0 * 4)))


def route_first(nc, k, a):
    with ExitStack() as ctx:
        def sb(name, shape, dt=F32):
            return ctx.enter_context(nc.sbuf_tensor(name, shape, dt))

        def sem(name):
            return ctx.enter_context(nc.semaphore(name))

        wr = sb("wr", [P, DC, E0])
        br = sb("br", [1, E0])
        lg = sb("lg", [1, E0])
        ex = sb("ex", [1, E0])
        top = sb("top", [1, 8])
        one = sb("one", [1, 8])
        idx_u = sb("idx_u", [1, 8], U32)
        idx = sb("idx", [1, 8], I32)
        tw = sb("tw", [1, TOP])
        tw_col = sb("tw_col", [TOP, P])
        tws = sb("tws", [P, TOP])
        b2 = sb("b2_0", [TOP, D])
        ps = ctx.enter_context(nc.psum_tensor("ps_route", [P, BANK], F32))
        ps_b = ctx.enter_context(nc.psum_tensor("ps_route_b", [P, BANK], F32))
        loaded, all_loaded = k.loads_in, k.expect_loads(2)
        exp_in = sem("route_exp_in")
        exp_out = sem("route_exp_out")
        pe_done = sem("route_pe")
        picked = sem("picked")
        w_in = sem("w0_in")
        block = ctx.enter_context(nc.Block())
        marks = {}

        @block.vector
        def _(v):
            c = k.chain_on(v)
            sent = [0]

            def softmax(x, n, out):
                c.link(v.tensor_reduce(one[:, 0:1], x, AX_X, ALU.max))
                v.tensor_scalar(ex[:, 0:n], x, one[:, 0:1], None, ALU.subtract).then_inc(exp_in, 1)
                sent[0] += 1
                v.wait_ge(exp_out, sent[0])
                c.link(v.tensor_reduce(one[:, 1:2], ex[:, 0:n], AX_X, ALU.add))
                c.link(v.reciprocal(one[:, 2:3], one[:, 1:2]))
                c.link(v.tensor_scalar(out, ex[:, 0:n], one[:, 2:3], None, ALU.mult))

            v.wait_ge(loaded, all_loaded)
            v.wait_ge(pe_done, 1)
            c.link(v.scalar_tensor_tensor(out=lg[:, :], in0=ps[0:1, 0:E0], scalar=1.0 / N, in1=br[:, :],
                                          op0=ALU.mult, op1=ALU.add))
            softmax(lg[:, :], E0, lg[:, :])
            c.link(v.tensor_scalar(ex[:, :], lg[:, :], float(N), None, ALU.mult))
            c.link(v.tensor_scalar(one[:, :], ex[:, :], CAPACITY, None, ALU.max))
            c.link(v.reciprocal(one[:, :], one[:, :]))
            c.link(v.tensor_scalar(one[:, :], one[:, :], CAPACITY, 1.0, ALU.mult, ALU.min))
            c.link(v.tensor_scalar(top[:, :], ex[:, :], CAPACITY, None, ALU.is_gt))
            c.link(v.scalar_tensor_tensor(out=one[:, :], in0=one[:, :], scalar=-1.0, in1=top[:, :],
                                          op0=ALU.add, op1=ALU.mult))
            c.link(v.scalar_tensor_tensor(out=lg[:, :], in0=one[:, :], scalar=1.0, in1=lg[:, :],
                                          op0=ALU.add, op1=ALU.mult))
            softmax(lg[:, :], E0, lg[:, :])
            c.link(v.max(top[:, :], lg[:, :]))
            c.link(v.max_index(idx_u[:, :], top[:, :], lg[:, :]))
            v.tensor_copy(idx[:, :], idx_u[:, :]).then_inc(picked, 1)
            softmax(top[:, 0:TOP], TOP, tw[:, :])
            marks["tw"] = c.count
            v.wait_ge(pe_done, 2)
            c.inc(v.tensor_copy(tws[:, :], ps[:, 16:16 + TOP]))
            c.link(v.tensor_copy(tw_col[:, :], ps[0:TOP, 32:32 + P]))
            marks["tw_col"] = c.count
            v.wait_ge(w_in, 16 * 4 * TOP)
            for e in range(TOP):
                v.tensor_scalar(k.w2[:, e, :, :], k.w2[:, e, :, :], tws[:, e:e + 1], None, ALU.mult)
            v.wait_ge(pe_done, 3)
            v.tensor_copy(k.b2row[:, :], ps_b[:, 0:D])

        @block.scalar
        def _(act):
            for t, n in enumerate((E0, E0, TOP)):
                act.wait_ge(exp_in, t + 1)
                act.activation(ex[:, 0:n], ex[:, 0:n], ACT.Exp).then_inc(exp_out, 1)

        @block.tensor
        def _(pe):
            pe.wait_ge(loaded, all_loaded)
            for dc in range(DC):
                mm = pe.matmul(ps[0:1, 0:E0], k.total[:, dc:dc + 1], wr[:, dc, :], start=(dc == 0), stop=(dc == DC - 1))
            mm.then_inc(pe_done, 1)
            pe.wait_ge(k.dve_steps, marks["tw"])
            pe.matmul(ps[:, 16:16 + TOP], k.ones[0:1, :], tw[:, :], start=True, stop=True)
            pe.matmul(ps[0:TOP, 32:32 + P], tw[:, :], k.ones[0:1, :], start=True, stop=True).then_inc(pe_done, 1)
            pe.wait_ge(k.dve_steps, marks["tw_col"])
            pe.wait_ge(w_in, 16 * 4 * TOP)
            pe.matmul(ps_b[:, 0:D], tw_col[:, :], b2[:, :], start=True, stop=True).then_inc(pe_done, 1)

        @block.sync
        def _(sp):
            sp.dma_start(wr[:, :, :], a["L0_ffn_Wr"].rearrange("(c p) e -> p c e", p=P)).then_inc(loaded, 16)
            sp.dma_start(br[:, :], a["L0_ffn_br"].unsqueeze(0)).then_inc(loaded, 16)
            sp.wait_ge(picked, 1)
            for e in range(TOP):
                x = sp.value_load(idx[0:1, e:e + 1], min_val=0, max_val=E0 - 1)
                one_of = bass.ds(x, 1)
                sp.dma_start(k.w1[:, e, :, :], a["L0_ffn_W1"][one_of, :, :].rearrange("o (c p) f -> p (o c) f", p=P)
                             ).then_inc(w_in, 16)
                sp.dma_start(k.w2[:, e, :, :], a["L0_ffn_W2"][one_of, :, :].rearrange("o (c p) f -> p (o c) f", p=P)
                             ).then_inc(w_in, 16)
                sp.dma_start(k.b1[:, e, :], a["L0_ffn_b1"][one_of, :].rearrange("o (c p) -> p (o c)", p=P),
                             allow_slow_non_contiguous=True).then_inc(w_in, 16)
                sp.dma_start(b2[e:e + 1, :], a["L0_ffn_b2"][one_of, :]).then_inc(w_in, 16)
            sp.wait_ge(w_in, 16 * 4 * TOP)


RN = UNR * P
HALF = RN // 2


def feed_first(nc, k, a):
    with ExitStack() as ctx:
        def sb(name, shape, dt=F32):
            return ctx.enter_context(nc.sbuf_tensor(name, shape, dt))

        def sem(name):
            return ctx.enter_context(nc.semaphore(name))

        EF = TOP * FC
        gamma = sb("gamma0", [P, D])
        beta = sb("beta0", [P, D])
        hid = sb("hid0", [P, EF, RN])
        zeros = sb("zeros", [P, D])
        z = sb("z0", [P, UNR, D])
        norm = Norm(ctx, nc, k, "ln2")
        ps_h = [ctx.enter_context(nc.psum_tensor(f"ps2_h{i}", [P, BANK], F32)) for i in range(4)]
        ps_y = [ctx.enter_context(nc.psum_tensor(f"ps2_y{i}", [P, BANK], F32)) for i in range(2)]
        loaded, all_loaded = k.loads_in, k.expect_loads(2)
        zeros_ready = sem("zeros_ready")
        up = sem("up0")
        act_done = sem("gelu_done")
        down = sem("down0")
        y_used = sem("y0_used")
        block = ctx.enter_context(nc.Block())
        UP = EF * 2

        @block.sync
        def _(sp):
            sp.dma_start(gamma[:, :], a["L0_ffn_gamma"].partition_broadcast(P)).then_inc(loaded, 16)
            sp.dma_start(beta[:, :], a["L0_ffn_beta"].partition_broadcast(P)).then_inc(loaded, 16)
            for j, name in enumerate("kvq"):
                sp.dma_start(k.wqkv[:, :, j, :], a[f"L1_gnn_W{name}"].rearrange("(c p) f -> p c f", p=P)
                             ).then_inc(k.w_in, 16)
                sp.dma_start(k.bqkv[:, j, :], a[f"L1_gnn_b{name}"].partition_broadcast(P)).then_inc(k.w_in, 16)
            for c in range(DC):
                sp.dma_start(k.q01[:, c:c + 1], a["L1_gnn_query_emb"][c * P:(c + 1) * P]
                             .rearrange("(p o) -> p o", o=1)).then_inc(k.w_in, 16)
            sp.dma_start(k.relw[:, :], a["L1_gnn_rel_w"]).then_inc(k.w_in, 16)
            sp.wait_ge(zeros_ready, 1)
            sp.dma_start(k.sorted_rows[:, :].rearrange("(s p) d -> p s d", p=P),
                         zeros[:, :].unsqueeze(1).to_broadcast([P, SLOTS, D])).then_inc(k.w_in, 16)
            sp.wait_ge(k.w_in, 16 * QKV_LOADS)

        @block.gpsimd
        def _(pool):
            pool.memset(zeros[:, :], 0.0).then_inc(zeros_ready, 1)

        @block.tensor
        def _(pe):

            def trip(i):
                for t in range(UP):
                    ef, half = t // 2, t % 2
                    e, f = ef // FC, ef % FC
                    wait(pe, act_done, i * UP + max(t - 3, 0))
                    for dc in range(DC):
                        mm = pe.matmul(ps_h[t % 4][:, 0:HALF], k.w1[:, e, dc, f * P:(f + 1) * P],
                                       k.xt[:, dc, bass.ds(i * RN + half * HALF, HALF)],
                                       start=(dc == 0), stop=(dc == DC - 1))
                    mm.then_inc(up, 1)
                wait(pe, act_done, (i + 1) * UP)
                for j in range(UNR):
                    wait(pe, y_used, i * UNR + max(j - 1, 0))
                    for ef in range(EF):
                        mm = pe.matmul(ps_y[j % 2][:, 0:D], hid[:, ef, j * P:(j + 1) * P],
                                       k.w2[:, ef // FC, ef % FC, :], start=(ef == 0), stop=(ef == EF - 1))
                    mm.then_inc(down, 1)

            rounds(pe, WROUNDS, trip)

        @block.scalar
        def _(act):

            def trip(i):
                for t in range(UP):
                    ef, half = t // 2, t % 2
                    wait(act, up, i * UP + (t + 1))
                    wait(act, down, i * UNR)
                    act.activation(hid[:, ef, half * HALF:(half + 1) * HALF], ps_h[t % 4][:, 0:HALF], ACT.Gelu,
                                   bias=k.b1[:, ef // FC, ef % FC:ef % FC + 1]).then_inc(act_done, 1)
                norm.on_scalar(act, i, k.eps)

            rounds(act, WROUNDS, trip)

        @block.vector
        def _(v):
            c = k.chain_on(v)
            v.wait_ge(loaded, all_loaded)

            def trip(i):
                c.enter(i, UNR + 1 + 1 + Norm.LINKS + UNR + 3, WROUNDS - 1, first=1)
                for j in range(UNR):
                    w = i * UNR + j
                    c.inc(v.tensor_scalar(z[:, j, :], k.x[:, w, :], k.mean[:, bass.ds(w, 1)],
                                          k.rstd[:, bass.ds(w, 1)], ALU.subtract, ALU.mult))
                c.wait()
                c.link(v.tensor_tensor(z[:, :, :], z[:, :, :], k.b2row[:, :].unsqueeze(1).to_broadcast([P, UNR, D]),
                                       ALU.add))
                for j in range(UNR):
                    wait(v, down, i * UNR + (j + 1))
                    v.tensor_tensor(z[:, j, :], z[:, j, :], ps_y[j % 2][:, 0:D], ALU.add).then_inc(y_used, 1)
                wait(v, y_used, (i + 1) * UNR)
                c.link(v.memset(norm.pad[:, :], 0.0))
                norm.on_vector(v, c, i, lambda j: z[:, j, :])
                for j in range(UNR):
                    c.inc(norm.apply(v, z[:, j, :], z[:, j, :], j))
                c.wait()
                c.link(v.tensor_tensor(z[:, :, :], z[:, :, :], gamma[:, :].unsqueeze(1).to_broadcast([P, UNR, D]),
                                       ALU.mult))
                c.link(v.tensor_tensor(z[:, :, :], z[:, :, :], beta[:, :].unsqueeze(1).to_broadcast([P, UNR, D]),
                                       ALU.add))
                at = bass.ds(i * UNR, UNR)
                c.link(v.tensor_tensor(k.x[:, at, :], k.x[:, at, :], z[:, :, :], ALU.add))
                c.leave()

            rounds(v, WROUNDS, trip)


def feed_forward_tensors(ctx, nc, k):
    def sb(name, shape, dt=F32):
        return ctx.enter_context(nc.sbuf_tensor(name, shape, dt))

    k.xt = sb("xt", [P, DC, NPAD])
    k.mean = sb("mean", [P, WIN])
    k.rstd = sb("rstd", [P, WIN])
    k.total = sb("total", [P, DC])
    k.w1 = sb("w1", [P, TOP, DC, HID])
    k.w2 = sb("w2", [P, TOP, FC, D])
    k.b1 = sb("b1", [P, TOP, FC])
    k.b2row = sb("b2row", [P, D])


def project_second(nc, k, a):
    with ExitStack() as ctx:
        def sb(name, shape, dt=F32):
            return ctx.enter_context(nc.sbuf_tensor(name, shape, dt))

        def sem(name):
            return ctx.enter_context(nc.semaphore(name))

        def bank(name):
            return ctx.enter_context(nc.psum_tensor(name, [P, BANK], F32))

        w, b, q01, relw = k.wqkv, k.bqkv, k.q01, k.relw
        rel_r = sb("rel_r", [F1, F1])
        xn = sb("xn2", [P, UNR, D])
        xt = sb("xt2", [P, UNR, DC, P])
        kv = sb("kv", [P, UNR, 2 * D])
        q = sb("qf", [P, UNR, D])
        norm = Norm(ctx, nc, k, "ln3")
        ps_t = [bank(f"ps3_t{i}") for i in range(2)]
        ps_kv = [bank(f"ps3_kv{i}") for i in range(2)]
        ps_q = [bank(f"ps3_q{i}") for i in range(2)]

        normed = sem("normed3")
        turned = sem("turned3")
        xt_ready = sem("xt3_ready")
        mm_done = sem("mm3_done")
        kv_ready = sem("kv_ready")
        q_ready = sem("q_ready")
        xn_kept = [sem(f"xn_kept{j}") for j in range(len(LOTS))]
        kv_kept = [sem(f"kv_kept{j}") for j in range(len(LOTS))]
        part = sem("q_part")
        rest = sem("q_rest")
        marks = {}
        block = ctx.enter_context(nc.Block())

        @block.sync
        def _(sp):

            def trip(i):
                for ready, dst, of, kept in ((normed, k.xin1_rows, xn, xn_kept), (kv_ready, k.kv_rows, kv, kv_kept)):
                    for n, (lo, hi) in enumerate(LOTS):
                        wait(sp, ready, i * UNR + hi)
                        sp.dma_start(dst[bass.ds((i * UNR + lo) * P, (hi - lo) * P), :]
                                     .rearrange("(w p) r -> p w r", p=P), of[:, lo:hi, :]).then_inc(kept[n], 16)

            rounds(sp, WROUNDS, trip)
            for n in range(len(LOTS)):
                sp.wait_ge(xn_kept[n], 16 * WROUNDS)
                sp.wait_ge(kv_kept[n], 16 * WROUNDS)

        @block.vector
        def _(v):
            c = k.chain_on(v)
            v.wait_ge(k.w_in, 16 * QKV_LOADS)
            c.inc(v.tensor_scalar(q01[:, :], q01[:, :], 0.1, None, ALU.mult))
            c.inc(v.tensor_scalar(b[:, 2, :], b[:, 2, :], 0.125, None, ALU.mult))
            c.link(v.tensor_scalar(relw[:, :], relw[:, :], 0.2, None, ALU.mult))
            marks["q01"] = c.count
            c.link(v.tensor_copy(k.rel3[:, 0, :], relw[:, :]))
            c.link(v.tensor_tensor(rel_r[:, :], relw[:, :], k.rel3[:, 0, :], ALU.subtract))
            c.link(v.tensor_copy(k.rel3[:, 1, :], rel_r[:, :]))
            c.link(v.tensor_tensor(rel_r[:, :], rel_r[:, :], k.rel3[:, 1, :], ALU.subtract))
            c.link(v.tensor_copy(k.rel3[:, 2, :], rel_r[:, :]))

            def normalise(i):
                norm.on_vector(v, c, i, lambda j: k.x[:, i * UNR + j, :])
                for j in range(UNR):
                    wait(v, turned, i * UNR)
                    wait(v, xn_kept[lot_of(j)], i * 16)
                    norm.apply(v, xn[:, j, :], k.x[:, i * UNR + j, :], j).then_inc(normed, 1)

            def trip(i, last=0):
                c.enter(i, 0 if last else Norm.LINKS, WROUNDS - 2, first=1)
                for j in range(UNR):
                    if j == UNR - 1 and not last:
                        normalise(i + 1)
                    wait(v, mm_done, i * UNR + (j + 1))
                    wait(v, kv_kept[lot_of(j)], i * 16)
                    v.tensor_tensor(kv[:, j, :].rearrange("p (a f) -> p a f", a=2),
                                    ps_kv[j % 2][:, :].rearrange("p (a f) -> p a f", a=2), b[:, 0:2, :], ALU.add
                                    ).then_inc(kv_ready, 1)
                    wait(v, part, (i - 1) * (3 * UNR) + 3 * (j + 1))
                    v.scalar_tensor_tensor(out=q[:, j, :], in0=ps_q[j % 2][:, 0:D], scalar=0.125,
                                           in1=b[:, 2, :], op0=ALU.mult, op1=ALU.add).then_inc(q_ready, 1)
                    for t in range(2):
                        wait(v, part, i * (3 * UNR) + (3 * j + t + 1))
                        v.tensor_tensor(q[:, j, :], q[:, j, :], k.q3[:, i * UNR + j, t, :], ALU.subtract
                                        ).then_inc(rest, 1)
                c.leave()

            normalise(0)
            rounds(v, WROUNDS - 1, trip)
            trip(WROUNDS - 1, last=1)

        @block.scalar
        def _(act):
            act.wait_ge(k.dve_steps, marks["q01"])

            def take(i, j):
                wait(act, turned, i * UNR + (j + 1))
                wait(act, mm_done, (i - 1) * UNR + (j + 1))
                for c in range(DC):
                    ins = act.activation(xt[:, j, c, :], ps_t[j % 2][:, c * P:(c + 1) * P], ACT.Identity,
                                         bias=q01[:, c:c + 1])
                ins.then_inc(xt_ready, 1)

            def take_part(i, j, t):
                if t:
                    wait(act, rest, i * (2 * UNR) + (2 * j + t))
                else:
                    wait(act, q_ready, i * UNR + (j + 1))
                act.copy(k.q3[:, i * UNR + j, t, :], q[:, j, :]).then_inc(part, 1)

            def trip(i, last=0):
                take(i, 0)
                take(i, 1)
                for j in range(UNR):
                    if j == UNR - 1 and not last:
                        norm.on_scalar(act, i + 1, k.eps)
                    take_part(i, j, 0)
                    if j + 2 < UNR:
                        take(i, j + 2)
                    take_part(i, j, 1)
                    take_part(i, j, 2)

            norm.on_scalar(act, 0, k.eps)
            rounds(act, WROUNDS - 1, trip)
            trip(WROUNDS - 1, last=1)

        @block.tensor
        def _(pe):
            pe.wait_ge(k.w_in, 16 * QKV_LOADS)

            def turn(i, j):
                wait(pe, normed, i * UNR + (j + 1))
                wait(pe, xt_ready, i * UNR + max(j - 1, 0))
                for c in range(DC):
                    mm = pe.transpose(ps_t[j % 2][:, c * P:(c + 1) * P], xn[:, j, c * P:(c + 1) * P], k.ident[:, :])
                mm.then_inc(turned, 1)

            def multiply(i, j):
                wait(pe, xt_ready, i * UNR + (j + 1))
                wait(pe, q_ready, i * UNR + max(j - 1, 0))
                for c in range(DC):
                    pe.matmul(ps_kv[j % 2][:, :], xt[:, j, c, :], w[:, c, 0:2, :].rearrange("p a f -> p (a f)"),
                              start=(c == 0), stop=(c == DC - 1))
                for c in range(DC):
                    mm = pe.matmul(ps_q[j % 2][:, 0:D], xt[:, j, c, :], w[:, c, 2, :],
                                   start=(c == 0), stop=(c == DC - 1))
                mm.then_inc(mm_done, 1)

            def trip(i):
                turn(i, 0)
                for j in range(1, UNR):
                    turn(i, j)
                    multiply(i, j - 1)
                multiply(i, UNR - 1)

            rounds(pe, WROUNDS, trip)


E1, HID1 = 32, 64
SLOTS = WIN + E1 - 1
FR = 4
assert SLOTS % FR == 0


def mix_second(nc, k, a):
    with ExitStack() as ctx:
        def sb(name, shape, dt=F32):
            return ctx.enter_context(nc.sbuf_tensor(name, shape, dt))

        def sem(name):
            return ctx.enter_context(nc.semaphore(name))

        def bank(name):
            return ctx.enter_context(nc.psum_tensor(name, [P, BANK], F32))

        wo = sb("wo", [P, DC, D])
        bo = sb("bo", [P, D])
        gamma = sb("gamma1", [P, D])
        beta = sb("beta1", [P, D])
        rw = sb("rw", [E1, D])
        rwt = sb("rwt", [P, DC, E1])
        val = sb("val", [P, UNR, D])
        xin = sb("xin", [P, UNR, D])
        nz = sb("nz", [P, WIN, H1])
        inv = sb("inv1", [P, UNR, H1])
        mt = sb("mt", [P, UNR, DC, P])
        z = sb("z1", [P, UNR, D])
        y = sb("y1", [P, UNR, D])
        xs = sb("xs", [P, UNR, DC, P])
        norm = Norm(ctx, nc, k, "ln4", 0, 2)
        norm2 = Norm(ctx, nc, k, "ln5", 1, 2)
        ps_m = [bank(f"ps4_m{i}") for i in range(2)]
        ps_n = [bank(f"ps4_n{i}") for i in range(2)]
        ps_y = [bank(f"ps4_y{i}") for i in range(2)]
        ps_l = [bank(f"ps4_l{i}") for i in range(2)]
        ps_y = [ps_y[j // 2 % 2][:, j % 2 * D:(j % 2 + 1) * D] for j in range(UNR)]

        loaded, all_loaded = k.loads_in, k.expect_loads(6)
        val_in = sem("val_in")
        xin_in = sem("xin_in")
        xin_ready = sem("xin_ready")
        rwt_t = sem("rw_turned")
        rwt_ready = sem("rwt_ready")
        msg = sem("msg1")
        m_turned = sem("messages_turned")
        m_used = sem("messages_used")
        n_turned = sem("norm_turned")
        n_used = sem("norm_used")
        mm_done = sem("mm4_done")
        y_done = sem("y1_done")
        normed = sem("normed5")
        l_done = sem("logits_done")
        l_used = sem("logits_used")
        xn_kept = sem("xn5_kept")
        w2_padded = sem("w2_padded")
        block = ctx.enter_context(nc.Block())

        @block.sync
        def _(sp):
            sp.dma_start(rw[:, :], a["L1_ffn_router_w"]).then_inc(loaded, 16)
            sp.dma_start(wo[:, :, :], a["L1_gnn_Wo"].rearrange("(c p) f -> p c f", p=P)).then_inc(loaded, 16)
            for t, name in ((bo, "L1_gnn_bo"), (gamma, "L1_gnn_gamma"), (beta, "L1_gnn_beta"),
                            (k.rb, "L1_ffn_router_b")):
                sp.dma_start(t[:, :], a[name].partition_broadcast(P)).then_inc(loaded, 16)

            def load_val(rows):
                sp.dma_start(val[:, :, :], k.kv_rows[rows, D:2 * D].rearrange("(w p) d -> p w d", p=P)
                             ).then_inc(val_in, 16)

            def load_xin(rows):
                sp.dma_start(xin[:, :, :], k.xin1_rows[rows, :].rearrange("(w p) d -> p w d", p=P)
                             ).then_inc(xin_in, 16)

            load_val(slice(0, RN))
            load_xin(slice(0, RN))

            def trip(i):
                rows = bass.ds((i + 1) * RN, RN)
                wait(sp, m_turned, (i + 1) * UNR)
                load_val(rows)
                wait(sp, y_done, (i + 1) * UNR)
                load_xin(rows)

            rounds(sp, WROUNDS - 1, trip)
            sp.wait_ge(val_in, 16 * WROUNDS)
            sp.wait_ge(xin_in, 16 * WROUNDS)

        @block.vector
        def _(v):
            c = k.chain_on(v)
            v.wait_ge(loaded, all_loaded)
            v.wait_ge(rwt_t, 1)
            v.tensor_copy(rwt[:, :, :], ps_l[0][:, 0:DC * E1].rearrange("p (c e) -> p c e", c=DC)
                          ).then_inc(rwt_ready, 1)
            four = [P, UNR, H1, F1]

            def attend(r):
                at = slice(r * UNR, (r + 1) * UNR)
                acc = k.acc1[:, at, H1:H1 + D].rearrange("p w (h f) -> p w h f", h=H1)
                c.link(v.tensor_scalar(nz[:, at, :], k.acc1[:, at, 0:H1], 0.0, None, ALU.is_equal))
                c.link(v.tensor_tensor(inv[:, :, :], nz[:, at, :], k.acc1[:, at, 0:H1], ALU.add))
                c.link(v.reciprocal(inv[:, :, :], inv[:, :, :]))
                c.link(v.tensor_tensor(acc, acc, inv[:, :, :].unsqueeze(3).to_broadcast(four), ALU.mult))

            def message(i):
                at = bass.ds(i * UNR, UNR)
                vals = val[:, :, :].rearrange("p w (h f) -> p w h f", h=H1)
                wait(v, val_in, (i + 1) * 16)
                c.link(v.tensor_tensor(vals, vals, nz[:, at, :].unsqueeze(3).to_broadcast(four), ALU.mult))
                c.inc(v.tensor_tensor(val[:, :, :], val[:, :, :], k.acc1[:, at, H1:H1 + D], ALU.add))
                c.wait()
                v.memset(norm.pad[:, :], 0.0).then_inc(msg, 1)

            attend(0)
            message(0)
            for r in range(1, WROUNDS):
                attend(r)

            def trip(i, last=False):
                c.enter(i, 2 * Norm.LINKS + 3 + UNR + (0 if last else 2), WROUNDS - 2, first=1)
                at = bass.ds(i * UNR, UNR)
                wait(v, xin_ready, i + 1)
                for j in range(UNR):
                    wait(v, mm_done, i * UNR + (j // 2 * 2 + 2 if j < UNR - 1 else UNR))
                    v.tensor_tensor(z[:, j, :], ps_y[j], xin[:, j, :], ALU.add).then_inc(y_done, 1)
                wait(v, y_done, (i + 1) * UNR)
                norm.on_vector(v, c, i, lambda j: z[:, j, :])
                if not last:
                    message(i + 1)
                for j in range(UNR):
                    c.inc(norm.apply(v, z[:, j, :], z[:, j, :], j))
                c.wait()
                c.link(v.tensor_tensor(z[:, :, :], z[:, :, :], gamma[:, :].unsqueeze(1).to_broadcast([P, UNR, D]),
                                       ALU.mult))
                c.link(v.tensor_tensor(k.x[:, at, :], k.x[:, at, :], z[:, :, :], ALU.add))
                c.link(v.tensor_tensor(k.x[:, at, :], k.x[:, at, :],
                                       beta[:, :].unsqueeze(1).to_broadcast([P, UNR, D]), ALU.add))
                norm2.on_vector(v, c, i, lambda j: k.x[:, i * UNR + j, :])
                wait(v, xn_kept, i)
                for j in range(UNR):
                    wait(v, n_turned, i * UNR)
                    norm2.apply(v, y[:, j, :], k.x[:, i * UNR + j, :], j).then_inc(normed, 1)
                c.leave()

            rounds(v, WROUNDS - 1, trip)
            trip(WROUNDS - 1, last=True)

        @block.scalar
        def _(act):
            def take_messages(i):
                for j in range(UNR):
                    wait(act, m_turned, i * UNR + (j + 1))
                    wait(act, mm_done, (i - 1) * UNR + (j + 1))
                    act.copy(mt[:, j, :, :], ps_m[j % 2][:, 0:D].rearrange("p (c n) -> p c n", c=DC)
                             ).then_inc(m_used, 1)

            def take_logits(i, j):
                wait(act, l_done, i * UNR + (j + 1))
                act.copy(k.lg[:, i * UNR + j, :], ps_l[j % 2][:, 0:E1]).then_inc(l_used, 1)

            def trip(i, last=False):
                norm.on_scalar(act, i, k.eps)
                if not last:
                    take_messages(i + 1)
                norm2.on_scalar(act, i, k.eps)
                for j in range(UNR):
                    wait(act, n_turned, i * UNR + (j + 1))
                    wait(act, l_done, i * UNR)
                    act.copy(xs[:, j, :, :], ps_n[j % 2][:, 0:D].rearrange("p (c n) -> p c n", c=DC)
                             ).then_inc(n_used, 1)
                    if j:
                        take_logits(i, j - 1)
                take_logits(i, UNR - 1)

            take_messages(0)
            rounds(act, WROUNDS - 1, trip)
            trip(WROUNDS - 1, last=True)
            for c in range(DC):
                act.dma_start(k.w1_1[:, c, :, :], a["L1_ffn_W1"][:, c * P:(c + 1) * P, :].rearrange("e p h -> p e h")
                             ).then_inc(k.w_in, 16)
            act.dma_start(k.b1_1[:, :, :].rearrange("p e h -> p (e h)"),
                         a["L1_ffn_b1"].rearrange("e h -> (e h)").partition_broadcast(P)).then_inc(k.w_in, 16)
            act.dma_start(k.w2_1[0:HID1, :, :], a["L1_ffn_W2"].rearrange("e h d -> h e d")).then_inc(k.w_in, 16)
            act.wait_ge(w2_padded, 1)
            act.dma_start(k.w2_1[HID1:HID1 + 1, :, :], a["L1_ffn_b2"].unsqueeze(0)).then_inc(k.w_in, 16)

        @block.gpsimd
        def _(pool):
            pool.memset(k.w2_1[HID1:P, :, :], 0.0).then_inc(w2_padded, 1)
            pool.wait_ge(w2_padded, 1)
            pool.wait_ge(loaded, all_loaded)

            def add_bo(i):
                wait(pool, xin_in, (i + 1) * 16)
                pool.tensor_tensor(xin[:, :, :], xin[:, :, :], bo[:, :].unsqueeze(1).to_broadcast([P, UNR, D]),
                                   ALU.add).then_inc(xin_ready, 1)

            def trip(i, last=False):
                if not last:
                    add_bo(i + 1)
                wait(pool, normed, (i + 1) * UNR)
                pool.tensor_copy(k.xn5[:, bass.ds(i * UNR, UNR), :], y[:, :, :]).then_inc(xn_kept, 1)

            add_bo(0)
            rounds(pool, WROUNDS - 1, trip)
            trip(WROUNDS - 1, last=True)

        @block.tensor
        def _(pe):
            pe.wait_ge(loaded, all_loaded)
            for dc in range(DC):
                mm = pe.transpose(ps_l[0][:, dc * E1:(dc + 1) * E1], rw[:, dc * P:(dc + 1) * P], k.ident[0:E1, 0:E1])
            mm.then_inc(rwt_t, 1)
            pe.wait_ge(rwt_ready, 1)

            def turn(bank, src):
                for c in range(DC):
                    mm = pe.transpose(bank[:, c * P:(c + 1) * P], src[:, c * P:(c + 1) * P], k.ident[:, :])
                return mm

            def turn_message(i, j):
                wait(pe, m_used, i * UNR + (j - 1))
                turn(ps_m[j % 2], val[:, j, :]).then_inc(m_turned, 1)

            def multiply(i, j):
                wait(pe, m_used, i * UNR + (j + 1))
                wait(pe, y_done, i * UNR + (2 if j == UNR - 1 else 0))
                for c in range(DC):
                    mm = pe.matmul(ps_y[j], mt[:, j, c, :], wo[:, c, :], start=(c == 0), stop=(c == DC - 1))
                mm.then_inc(mm_done, 1)

            def logits(i, j):
                wait(pe, n_used, i * UNR + (j + 1))
                wait(pe, l_used, i * UNR + (j - 1))
                for c in range(DC):
                    mm = pe.matmul(ps_l[j % 2][:, 0:E1], xs[:, j, c, :], rwt[:, c, :], start=(c == 0), stop=(c == DC - 1))
                mm.then_inc(l_done, 1)

            def multiply_messages(i):
                wait(pe, msg, i + 1)
                turn_message(i, 0)
                for j in range(1, UNR):
                    turn_message(i, j)
                    multiply(i, j - 1)

            def trip(i, last=False):
                multiply(i, UNR - 1)
                if not last:
                    multiply_messages(i + 1)
                for j in range(UNR):
                    wait(pe, normed, i * UNR + (j + 1))
                    wait(pe, n_used, i * UNR + (j - 1))
                    turn(ps_n[j % 2], y[:, j, :]).then_inc(n_turned, 1)
                    if j:
                        logits(i, j - 1)
                logits(i, UNR - 1)

            multiply_messages(0)
            rounds(pe, WROUNDS - 1, trip)
            trip(WROUNDS - 1, last=True)


def place(nc, k, a):
    with ExitStack() as ctx:
        def sb(name, shape, dt=F32):
            return ctx.enter_context(nc.sbuf_tensor("place_" + name, shape, dt))

        def sem(name):
            return ctx.enter_context(nc.semaphore(name))

        before = sb("before", [P, P])
        number = sb("number", [P, E1])
        cell = sb("cell", [P, WIN, E1])
        best = sb("best", [P, WIN])
        hot = sb("hot", [P, WIN, E1])
        count = sb("count", [P, E1, WIN])
        run = sb("run", [P, E1, WIN])
        fresh = sb("fresh", [P, E1, WIN])
        tiles_i = sb("tiles_i", [P, E1], I32)
        tiles = sb("tiles_f", [P, E1])
        until = sb("until", [P, E1])
        slot = sb("slot", [P, WIN])
        tile_no = sb("tile_no", [1, SLOTS])
        past = sb("past", [1, SLOTS, E1])
        who = sb("who", [1, SLOTS])
        ps_b = [ctx.enter_context(nc.psum_tensor(f"ps6_b{i}", [P, BANK], F32)) for i in range(2)]
        ps_c = [ctx.enter_context(nc.psum_tensor(f"ps6_c{i}", [P, BANK], F32)) for i in range(2)]
        HW = BANK // E1

        consts = sem("place_consts")
        counted = sem("counted")
        placed = sem("placed")
        scattered = sem("scattered")
        block = ctx.enter_context(nc.Block())
        marks = {}

        @block.gpsimd
        def _(pool):
            pool.memset(before[:, :], 0.0).then_inc(consts, 1)
            pool.wait_ge(consts, 1)
            pool.iota(tile_no[:, :], pattern=[[1, SLOTS]], base=0, channel_multiplier=0,
                      allow_small_or_imprecise_dtypes=True).then_inc(consts, 1)
            pool.wait_ge(consts, 2)
            pool.affine_select(out=before[:, :], in_=before[:, :], compare_op=ALU.is_ge, fill=1.0,
                               base=0, pattern=[[-1, P]], channel_multiplier=1).then_inc(consts, 1)
            pool.wait_ge(placed, 1)
            for w in range(WIN):
                pool.indirect_dma_start(out=k.sorted_rows[:, :],
                                        out_offset=bass.IndirectOffsetOnAxis(ap=k.slot_of[:, w:w + 1], axis=0),
                                        in_=k.xn5[:, w, :], in_offset=None).then_inc(scattered, 16)
            pool.wait_ge(scattered, 16 * WIN)

        @block.vector
        def _(v):
            c = k.chain_on(v)
            all_w = [P, WIN, E1]
            c.inc(v.tensor_scalar(number[:, :], k.iota_row[:, 0:E1], float(E1), None, ALU.subtract))
            c.inc(v.memset(fresh[:, :, 0:1], 0.0))
            c.inc(v.memset(fresh[:, :, 1:WIN], 1.0))
            numbers = number[:, :].unsqueeze(1).to_broadcast(all_w)
            c.link(v.tensor_tensor(k.lg[:, :, :], k.lg[:, :, :], k.rb[:, :].unsqueeze(1).to_broadcast(all_w), ALU.add))
            c.link(v.tensor_reduce(best[:, :], k.lg[:, :, :], AX_X, ALU.max))
            c.link(v.tensor_tensor(cell[:, :, :], k.lg[:, :, :], best[:, :].unsqueeze(2).to_broadcast(all_w),
                                   ALU.is_equal))
            c.link(v.tensor_tensor(cell[:, :, :], cell[:, :, :], numbers, ALU.mult))
            c.link(v.tensor_reduce(best[:, :], cell[:, :, :], AX_X, ALU.min))
            c.link(v.tensor_tensor(hot[:, :, :], best[:, :].unsqueeze(2).to_broadcast(all_w), numbers, ALU.is_equal))
            marks["hot"] = c.count
            v.wait_ge(counted, 2)
            for half in range(2):
                lo, hi = half * HW, min(WIN, (half + 1) * HW)
                c.inc(v.tensor_copy(count[:, :, lo:hi], ps_c[half][:, 0:(hi - lo) * E1]
                                    .rearrange("p (w e) -> p e w", e=E1)))
            c.wait()
            c.link(v.tensor_tensor_scan(run[:, :, :].rearrange("p e w -> p (e w)"),
                                        fresh[:, :, :].rearrange("p e w -> p (e w)"),
                                        count[:, :, :].rearrange("p e w -> p (e w)"), 0.0, ALU.mult, ALU.add))
            c.link(v.tensor_copy(tiles_i[:, :], run[:, :, WIN - 1]))
            c.link(v.tensor_single_scalar(tiles_i[:, :], tiles_i[:, :], P - 1, ALU.add))
            c.link(v.tensor_single_scalar(tiles_i[:, :], tiles_i[:, :], 7, ALU.arith_shift_right))
            c.link(v.tensor_copy(tiles[:, :], tiles_i[:, :]))
            c.link(v.tensor_tensor_scan(until[:, :], k.ones[:, 0:E1], tiles[:, :], 0.0, ALU.mult, ALU.add))
            c.link(v.tensor_tensor(run[:, :, :], run[:, :, :], count[:, :, :], ALU.subtract))
            c.link(v.tensor_tensor(tiles[:, :], until[:, :], tiles[:, :], ALU.subtract))
            c.link(v.tensor_scalar(tiles[:, :], tiles[:, :], float(P), None, ALU.mult))
            c.link(v.tensor_tensor(run[:, :, :], run[:, :, :], tiles[:, :].unsqueeze(2).to_broadcast([P, E1, WIN]),
                                   ALU.add))
            for half in range(2):
                lo, hi = half * HW, min(WIN, (half + 1) * HW)
                c.inc(v.tensor_tensor(cell[:, lo:hi, :], run[:, :, lo:hi].rearrange("p e w -> p w e"),
                                      ps_b[half][:, 0:(hi - lo) * E1].rearrange("p (w e) -> p w e", e=E1), ALU.add))
            c.wait()
            c.link(v.tensor_tensor(cell[:, :, :], cell[:, :, :], hot[:, :, :], ALU.mult))
            c.link(v.tensor_reduce(slot[:, :], cell[:, :, :], AX_X, ALU.add))
            v.tensor_copy(k.slot_of[:, :], slot[:, :]).then_inc(placed, 1)
            v.wait_ge(consts, 3)
            c.link(v.tensor_tensor(past[:, :, :], tile_no[:, :].unsqueeze(2).to_broadcast([1, SLOTS, E1]),
                                   until[0:1, :].unsqueeze(1).to_broadcast([1, SLOTS, E1]), ALU.is_ge))
            c.link(v.tensor_reduce(who[:, :], past[:, :, :], AX_X, ALU.add))
            c.link(v.tensor_scalar(who[:, :], who[:, :], float(E1 - 1), None, ALU.min))
            c.link(v.tensor_copy(k.expert_of[:, :], who[:, :]))

        @block.tensor
        def _(pe):
            pe.wait_ge(consts, 3)
            pe.wait_ge(k.dve_steps, marks["hot"])
            for lhs, banks in ((k.ones, ps_c), (before, ps_b)):
                for half in range(2):
                    lo, hi = half * HW, min(WIN, (half + 1) * HW)
                    mm = pe.matmul(banks[half][:, 0:(hi - lo) * E1], lhs[:, :],
                                   hot[:, lo:hi, :].rearrange("p w e -> p (w e)"), start=True, stop=True)
                mm.then_inc(counted, 1)


def feed_second(nc, k, a, out):
    with ExitStack() as ctx:
        def sb(name, shape, dt=F32):
            return ctx.enter_context(nc.sbuf_tensor(name, shape, dt))

        def sem(name):
            return ctx.enter_context(nc.semaphore(name))

        def bank(name):
            return ctx.enter_context(nc.psum_tensor(name, [P, BANK], F32))

        tiles, two = range(FR), range(2)
        FROUNDS = SLOTS // FR
        rows = [sb(f"rows5_{t}", [P, D]) for t in tiles]
        xt = [sb(f"xt5_{t}", [P, DC, P]) for t in tiles]
        hid = [sb(f"hid5_{t}", [P, P]) for t in tiles]
        hid_t = [sb(f"hid5_t{t}", [P, P]) for t in tiles]
        y = [sb(f"y5_{t}", [P, D]) for t in tiles]
        back = sb("back5", [P, WIN, D])
        ps_t = [bank(f"ps5_t{i}") for i in two]
        ps_u = [bank(f"ps5_u{i}") for i in two]
        ps_h = [bank(f"ps5_h{i}") for i in two]
        ps_y = [bank(f"ps5_y{i}") for i in two]

        rows_in = [sem(f"rows5_in{t}") for t in tiles]
        hid_set = sem("hid5_set")
        turned = sem("turned5")
        xt_ready = sem("xt5_ready")
        up = sem("up5")
        hid_ready = sem("hid5_ready")
        hid_turned = sem("hid5_turned")
        hid_t_ready = sem("hid5_t_ready")
        down = sem("down5")
        y_ready = sem("y5_ready")
        y_kept = [sem(f"y5_kept{t}") for t in tiles]
        LOT = 2 * UNR
        back_in = [sem(f"back_in{r}") for r in range(-(-WIN // LOT))]
        final = sem("x_final")
        kept, all_kept = k.loads_in, k.expect_loads(WROUNDS + 1)
        block = ctx.enter_context(nc.Block())

        def experts(eng, name):
            sets = []

            def load(i):
                regs = [eng.alloc_register(f"{name}{len(sets)}_{t}") for t in tiles]
                sets.append(regs)
                eng.load(regs, k.expert_of[0:1, bass.ds(i * FR, FR)])
                return [eng.snap(r, donate=True, min_val=0, max_val=E1 - 1) for r in regs]
            return load

        @block.gpsimd
        def _(pool):
            for t in tiles:
                for n, (lo, hi, x) in enumerate(((HID1, HID1 + 1, 1.0), (HID1 + 1, P, 0.0))):
                    if t or n:
                        pool.wait_ge(hid_set, 2 * t + n)
                    pool.memset(hid[t][:, lo:hi], x).then_inc(hid_set, 1)
            for t in tiles:
                pool.wait_ge(y_kept[t], 16 * FROUNDS)
            for w in range(WIN):
                pool.indirect_dma_start(out=back[:, w, :], out_offset=None, in_=k.y_rows[:, :],
                                        in_offset=bass.IndirectOffsetOnAxis(ap=k.slot_of[:, w:w + 1], axis=0)
                                        ).then_inc(back_in[w // LOT], 16)

        @block.sync
        def _(sp):
            def load(i, t):
                wait(sp, turned, (i - 1) * FR + (t + 1))
                sp.dma_start(rows[t][:, :], k.sorted_rows[bass.ds((i * FR + t) * P, P), :]).then_inc(rows_in[t], 16)

            def store(i, t):
                wait(sp, y_ready, i * FR + (t + 1))
                sp.dma_start(k.y_rows[bass.ds((i * FR + t) * P, P), :], y[t][:, :]).then_inc(y_kept[t], 16)

            for i in range(2):
                for t in tiles:
                    load(i, t)

            def trip(i):
                for t in tiles:
                    load(i + 2, t)
                for t in tiles:
                    store(i, t)

            rounds(sp, FROUNDS - 2, trip)
            for i in range(FROUNDS - 2, FROUNDS):
                for t in tiles:
                    store(i, t)
            for r in range(WROUNDS):
                sp.wait_ge(final, r + 1)
                lo, hi = r * UNR, min((r + 1) * UNR, WIN - 1)
                sp.dma_start(out[lo * P:hi * P, :].rearrange("(w p) d -> p w d", p=P), k.x[:, lo:hi, :]
                             ).then_inc(kept, 16)
            sp.dma_start(out[(WIN - 1) * P:N, :], k.x[0:LAST, WIN - 1, :]).then_inc(kept, 16)
            sp.wait_ge(kept, all_kept)

        @block.vector
        def _(v):
            load = experts(v, "dve_expert")
            v.wait_ge(hid_set, 2 * FR)
            v.wait_ge(k.w_in, 16 * (QKV_LOADS + DC + 3))

            def trip(i):
                e = load(i)
                for t in tiles:
                    n = i * FR + t
                    v.wait_ge(up, n + 1)
                    v.tensor_tensor(hid[t][:, 0:HID1], ps_u[t % 2][:, 0:HID1], k.b1_1[:, e[t], :], ALU.add
                                    ).then_inc(hid_ready, 1)
                for t in tiles:
                    n = i * FR + t
                    v.wait_ge(down, n + 1)
                    wait(v, y_kept[t], i * 16)
                    v.tensor_copy(y[t][:, :], ps_y[t % 2][:, 0:D]).then_inc(y_ready, 1)

            rounds(v, FROUNDS, trip)
            for r in range(WROUNDS):
                at = slice(r * UNR, (r + 1) * UNR)
                v.wait_ge(back_in[at.start // LOT], 16 * (min(WIN, (at.start // LOT + 1) * LOT) - at.start // LOT * LOT))
                v.scalar_tensor_tensor(out=k.x[:, at, :], in0=back[:, at, :], scalar=0.0, in1=k.x[:, at, :],
                                       op0=ALU.max, op1=ALU.add).then_inc(final, 1)

        @block.scalar
        def _(act):
            def take_rows(i, t):
                wait(act, turned, i * FR + (t + 1))
                wait(act, up, i * FR)
                act.copy(xt[t][:, :, :], ps_t[t % 2][:, 0:D].rearrange("p (c n) -> p c n", c=DC)
                         ).then_inc(xt_ready, 1)

            def take_hidden(i, t):
                wait(act, hid_turned, i * FR + (t + 1))
                wait(act, down, i * FR)
                act.activation(hid_t[t][:, :], ps_h[t % 2][:, 0:P], ACT.Relu).then_inc(hid_t_ready, 1)

            for t in tiles:
                take_rows(0, t)

            def trip(i):
                for t in tiles:
                    take_rows(i + 1, t)
                    take_hidden(i, t)

            rounds(act, FROUNDS - 1, trip)
            for t in tiles:
                take_hidden(FROUNDS - 1, t)

        @block.tensor
        def _(pe):
            load = experts(pe, "pe_expert")
            pe.wait_ge(k.w_in, 16 * (QKV_LOADS + DC + 3))
            def turn(i, t):
                wait(pe, rows_in[t], (i + 1) * 16)
                wait(pe, xt_ready, i * FR + max(t - 1, 0))
                for c in range(DC):
                    mm = pe.transpose(ps_t[t % 2][:, c * P:(c + 1) * P], rows[t][:, c * P:(c + 1) * P],
                                      k.ident[:, :])
                mm.then_inc(turned, 1)

            def finish(i, e, last):
                for t in tiles:
                    wait(pe, xt_ready, i * FR + (t + 1))
                    wait(pe, hid_ready, i * FR + max(t - 1, 0))
                    for c in range(DC):
                        mm = pe.matmul(ps_u[t % 2][:, 0:HID1], xt[t][:, c, :], k.w1_1[:, c, e[t], :],
                                       start=(c == 0), stop=(c == DC - 1))
                    mm.then_inc(up, 1)
                for t in tiles:
                    if not last:
                        turn(i + 1, t)
                    wait(pe, hid_ready, i * FR + (t + 1))
                    wait(pe, hid_t_ready, i * FR + max(t - 1, 0))
                    pe.transpose(ps_h[t % 2][:, 0:P], hid[t][:, :], k.ident[:, :]).then_inc(hid_turned, 1)
                for t in tiles:
                    wait(pe, hid_t_ready, i * FR + (t + 1))
                    wait(pe, y_ready, i * FR + max(t - 1, 0))
                    pe.matmul(ps_y[t % 2][:, 0:D], hid_t[t][:, :], k.w2_1[:, e[t], :], start=True, stop=True
                              ).then_inc(down, 1)

            for t in tiles:
                turn(0, t)

            def trip(i):
                finish(i, load(i), False)

            rounds(pe, FROUNDS - 1, trip)
            finish(FROUNDS - 1, load(FROUNDS - 1), True)


def build(nc, a, out):
    k = Kernel()
    with ExitStack() as ctx:
        def sb(on, name, shape, dt=F32):
            return on.enter_context(nc.sbuf_tensor(name, shape, dt))

        allocate(ctx, nc, k)
        k.w_in = ctx.enter_context(nc.semaphore("w_in"))
        k.acc1 = sb(ctx, "acc1", [P, WIN, H1 + D])
        flat = k.acc1[:, :, :].rearrange("p w r -> p (w r)")
        lo, mid, hi = DC * 3 * D, (DC + 1) * 3 * D, (DC + 1) * 3 * D + DC
        k.wqkv = flat[:, 0:lo].rearrange("p (c j f) -> p c j f", c=DC, j=3)
        k.bqkv = flat[:, lo:mid].rearrange("p (j f) -> p j f", j=3)
        k.q01 = flat[:, mid:hi]
        k.relw = flat[0:F1, hi:hi + F1]
        steps_of_edges(nc, k, a)
        with ExitStack() as stage:
            k.by_dst = sb(stage, "ad0", [P, WIN, 3, H0], BF16)
            project_first(nc, k, a)
            k.acc0 = sb(stage, "acc0", [P, WIN, R0])
            k.acc0_odd = sb(stage, "acc0_odd", [P, WIN, R0])
            with ExitStack() as inner:
                edges(nc, k, FIRST, inner, [k.acc0, k.acc0_odd])
            feed_forward_tensors(stage, nc, k)
            mix_first(nc, k, a)
            route_first(nc, k, a)
            feed_first(nc, k, a)
        with ExitStack() as stage:
            with ExitStack() as inner:
                k.q3 = sb(inner, "q3", [P, WIN, 3, D], BF16)
                k.rel3 = sb(inner, "rel3", [F1, 3, F1], BF16)
                k.by_dst, k.by_typ = k.q3, k.rel3
                project_second(nc, k, a)
                edges(nc, k, SECOND, inner, [k.acc1])
            k.xn5 = sb(stage, "xn5", [P, WIN, D])
            k.lg = sb(stage, "logits", [P, WIN, E1])
            k.slot_of = sb(stage, "slot_of", [P, WIN], I32)
            k.expert_of = sb(stage, "expert_of", [1, SLOTS], I32)
            k.w1_1 = sb(stage, "w1_1", [P, DC, E1, HID1])
            k.b1_1 = sb(stage, "b1_1", [P, E1, HID1])
            k.w2_1 = sb(stage, "w2_1", [P, E1, D])
            k.rb = sb(stage, "rb", [P, E1])
            mix_second(nc, k, a)
            place(nc, k, a)
            feed_second(nc, k, a, out)


_INS = ['x', 'src', 'dst', 'edge_type_64', 'L0_gnn_W', 'L0_gnn_a_src', 'L0_gnn_a_dst', 'L0_gnn_bias',
        'L0_ffn_Wr', 'L0_ffn_br', 'L0_ffn_W1', 'L0_ffn_b1', 'L0_ffn_W2', 'L0_ffn_b2', 'L0_ffn_gamma',
        'L0_ffn_beta', 'L1_gnn_query_emb', 'L1_gnn_Wq', 'L1_gnn_bq', 'L1_gnn_Wk', 'L1_gnn_bk', 'L1_gnn_Wv',
        'L1_gnn_bv', 'L1_gnn_rel_w', 'L1_gnn_Wo', 'L1_gnn_bo', 'L1_gnn_gamma', 'L1_gnn_beta',
        'L1_ffn_router_w', 'L1_ffn_router_b', 'L1_ffn_W1', 'L1_ffn_b1', 'L1_ffn_W2', 'L1_ffn_b2']


def kernel(**inputs):
    import numpy as _np
    import concourse.bacc as _bacc
    from concourse import mybir as _mybir
    from concourse.bass_utils import run_bass_kernel_spmd as _run

    nc = _bacc.Bacc("TRN2", target_bir_lowering=False, num_devices=1)
    arrays, args = {}, {}
    for name in _INS:
        a = _np.ascontiguousarray(inputs[name])
        arrays[f"in_{name}"] = a
        args[name] = nc.dram_tensor(f"in_{name}", a.shape, _mybir.dt.from_np(a.dtype), kind="ExternalInput").ap()
    out = nc.dram_tensor("out_0", (N, D), F32, kind="ExternalOutput").ap()
    build(nc, args, out)
    r = _run(nc, [arrays], core_ids=[0])
    return r.results[0]["out_0"]
```
